# Optimizing a Trainium2 kernel written in Bass

```python
import numpy as np
import jax
import jax.numpy as jnp

def _softmax(x, axis=-1):
    return jax.nn.softmax(x, axis=axis)

def _gelu(x):
    return jax.nn.gelu(x, approximate=True)

def _silu(x):
    return jax.nn.silu(x)

def _sigmoid(x):
    return jax.nn.sigmoid(x)

def _layernorm(x, axis=-1, eps=1e-05):
    m = jnp.mean(x, axis=axis, keepdims=True)
    v = jnp.var(x, axis=axis, keepdims=True)
    return (x - m) / jnp.sqrt(v + eps)

def _scatter_add(tgt, idx, src, axis=0):
    return tgt.at[idx].add(src)

def _segment_sum(src, seg, n):
    return jax.ops.segment_sum(src, seg, n)
kernel_name = 'mk_xattn_seq_d2_seqx_r8_8b004c'

def setup_inputs(seed: int=0):
    np.random.seed(seed)
    _w = jnp.asarray

    def _rec_inputs():
        import jax
        import jax.numpy as jnp
        _rk = jax.random.key(seed)
        x = -0.000296 + 1 * jax.random.normal(jax.random.fold_in(_rk, 1), (4, 256, 160), jnp.float32)
        _lenS = 256 - jax.random.randint(jax.random.fold_in(_rk, 7), (4,), 0, max(1, 256 // 4) + 1, jnp.int32)
        _lenS2 = 1601 - jax.random.randint(jax.random.fold_in(_rk, 8), (4,), 0, max(1, 1601 // 4) + 1, jnp.int32)
        _ctx_2048P = jax.random.normal(jax.random.fold_in(_rk, 11), (4, 16, 256), jnp.float32)
        _ctx_2048c = jax.random.dirichlet(jax.random.fold_in(_rk, 511), 0.3 * jnp.ones((16,), jnp.float32), (4, 1601))
        _ctx_2048t = jnp.einsum('bsk,bkd->bsd', _ctx_2048c, _ctx_2048P)
        _ctx_2048t = _ctx_2048t * jax.lax.rsqrt(jnp.mean(jnp.square(_ctx_2048t)) + 1e-12) * 0.953939
        ctx_2048 = 0.00118529 + 0.99962 * (_ctx_2048t + 0.3 * jax.random.normal(jax.random.fold_in(_rk, 611), (4, 1601, 256), jnp.float32))
        fside_Bx4x4_0 = jax.random.uniform(jax.random.fold_in(_rk, 12), (4, 4, 4), jnp.float32, 0.0, 0.981965)
        fside_S_0 = jax.random.uniform(jax.random.fold_in(_rk, 13), (256,), jnp.float32, 0.0, 0.999706)
        return (x, ctx_2048, fside_Bx4x4_0, fside_S_0)
    x, ctx_2048, fside_Bx4x4_0, fside_S_0 = _rec_inputs()

    def _L0_xattn_setup():
        import jax, jax.numpy as jnp
        import numpy as np
        HEADS = 20
        NUM_IP_TOKENS = 4
        NUM_DUMMY_TOKENS = 4
        IP_SCALE = 1.0
        ASPECT_RATIO = 1.0
        NEG = -10000.0

        def _grid_hw(seq_len, aspect_ratio):
            width = int((seq_len / aspect_ratio) ** 0.5)
            height = seq_len // width
            while width * height != seq_len:
                if width * height < seq_len:
                    width += 1
                else:
                    width -= 1
                height = seq_len // width
            return (height, width)

        def _sdpa(q, k, v, mask=None):
            dh = q.shape[-1]
            scores = jnp.einsum('bhqd,bhkd->bhqk', q, k) / jnp.sqrt(jnp.asarray(dh, q.dtype))
            if mask is not None:
                scores = scores + mask
            probs = jax.nn.softmax(scores, axis=-1)
            return jnp.einsum('bhqk,bhkd->bhqd', probs, v)

        def _split_heads(x, heads):
            b, l, d = x.shape
            return x.reshape(b, l, heads, d // heads).transpose(0, 2, 1, 3)

        def _merge_heads(x):
            b, h, l, dh = x.shape
            return x.transpose(0, 2, 1, 3).reshape(b, l, h * dh)

        def _ip_mask(bbox, batch_size, seq_len, dtype):
            M = bbox.shape[1]
            height, width = _grid_hw(seq_len, ASPECT_RATIO)
            x = jnp.linspace(0.0, 1.0, width, dtype=dtype)
            y = jnp.linspace(0.0, 1.0, height, dtype=dtype)
            yg, xg = jnp.meshgrid(y, x, indexing='ij')
            xg = xg.reshape(-1)
            yg = yg.reshape(-1)
            x1, y1, x2, y2 = (bbox[..., 0:1], bbox[..., 1:2], bbox[..., 2:3], bbox[..., 3:4])
            inside = (xg >= x1) & (xg <= x2) & (yg >= y1) & (yg <= y2)
            ip_mask = jnp.where(inside, 0.0, NEG).astype(dtype)
            ip_mask = jnp.transpose(ip_mask, (0, 2, 1))[:, None]
            ip_mask = jnp.repeat(ip_mask, NUM_IP_TOKENS // M, axis=-1)
            dummy = jnp.where(jnp.any(inside, axis=1), NEG, 0.0).astype(dtype)
            dummy = jnp.repeat(dummy[:, None, :, None], NUM_DUMMY_TOKENS, axis=-1)
            return jnp.concatenate([dummy, ip_mask], axis=-1)
        key = jax.random.key(seed)
        ks = jax.random.split(key, 12)
        B, S, D, C = (4, 512, 160, 256)
        text_len, M = (77, 4)
        hidden_states = jax.random.normal(ks[0], (B, S, D), jnp.float32)
        encoder_hidden_states = jax.random.normal(ks[1], (B, text_len + NUM_IP_TOKENS + NUM_DUMMY_TOKENS, C), jnp.float32)
        p1 = jax.random.uniform(ks[2], (B, M, 2), jnp.float32)
        p2 = jax.random.uniform(ks[3], (B, M, 2), jnp.float32)
        bbox = jnp.concatenate([jnp.minimum(p1, p2), jnp.maximum(p1, p2)], axis=-1)
        s = 0.02
        w_q = jax.random.normal(ks[4], (D, D), jnp.float32) * s
        w_k = jax.random.normal(ks[5], (C, D), jnp.float32) * s
        w_v = jax.random.normal(ks[6], (C, D), jnp.float32) * s
        w_k_ip = jax.random.normal(ks[7], (C, D), jnp.float32) * s
        w_v_ip = jax.random.normal(ks[8], (C, D), jnp.float32) * s
        w_out = jax.random.normal(ks[9], (D, D), jnp.float32) * s
        b_out = jnp.zeros((D,), jnp.float32)
        return {'hidden_states': hidden_states, 'encoder_hidden_states': encoder_hidden_states, 'bbox': bbox, 'w_q': w_q, 'w_k': w_k, 'w_v': w_v, 'w_k_ip': w_k_ip, 'w_v_ip': w_v_ip, 'w_out': w_out, 'b_out': b_out}
    _L0_xattn_all = _L0_xattn_setup()
    _L0_xattn_in = {k: v for k, v in _L0_xattn_all.items() if k in ('w_q', 'w_k', 'w_v', 'w_k_ip', 'w_v_ip', 'w_out', 'b_out')}
    del _L0_xattn_all

    def _L1_xattn_setup():
        import jax, jax.numpy as jnp
        import numpy as np
        HEADS = 20
        NUM_TOKENS = 4
        IP_SCALE = 1.0
        SEM_SCALE = 0.5
        RESCALE = 1.0
        EPS = 1e-12

        def _l2norm(x, axis=-1):
            n = jnp.sqrt(jnp.sum(x * x, axis=axis, keepdims=True))
            return x / jnp.maximum(n, EPS)
        key = jax.random.key(seed)
        ks = jax.random.split(key, 10)
        B, S, C = (2, 128, 160)
        T, E = (81, 256)
        inp = {'hidden_states': jax.random.normal(ks[0], (B, S, C), jnp.float32), 'encoder_hidden_states': jax.random.normal(ks[1], (B, T, E), jnp.float32), 'spatial_mask': jax.random.uniform(ks[2], (S,), jnp.float32), 'W_q': jax.random.normal(ks[3], (C, C), jnp.float32) * C ** (-0.5), 'W_k': jax.random.normal(ks[4], (E, C), jnp.float32) * E ** (-0.5), 'W_v': jax.random.normal(ks[5], (E, C), jnp.float32) * E ** (-0.5), 'W_k_ip': jax.random.normal(ks[6], (E, C), jnp.float32) * E ** (-0.5), 'W_v_ip': jax.random.normal(ks[7], (E, C), jnp.float32) * E ** (-0.5), 'W_out': jax.random.normal(ks[8], (C, C), jnp.float32) * C ** (-0.5), 'b_out': jnp.zeros((C,), jnp.float32)}
        return inp
    _L1_xattn_all = _L1_xattn_setup()
    _L1_xattn_in = {k: v for k, v in _L1_xattn_all.items() if k in ('W_q', 'W_k', 'W_v', 'W_k_ip', 'W_v_ip', 'W_out', 'b_out')}
    del _L1_xattn_all
    return {'x': x, 'ctx_2048': ctx_2048, 'fside_Bx4x4_0': fside_Bx4x4_0, 'fside_S_0': fside_S_0, 'L0_xattn_w_q': _L0_xattn_in['w_q'], 'L0_xattn_w_k': _L0_xattn_in['w_k'], 'L0_xattn_w_v': _L0_xattn_in['w_v'], 'L0_xattn_w_k_ip': _L0_xattn_in['w_k_ip'], 'L0_xattn_w_v_ip': _L0_xattn_in['w_v_ip'], 'L0_xattn_w_out': _L0_xattn_in['w_out'], 'L0_xattn_b_out': _L0_xattn_in['b_out'], 'L1_xattn_W_q': _L1_xattn_in['W_q'], 'L1_xattn_W_k': _L1_xattn_in['W_k'], 'L1_xattn_W_v': _L1_xattn_in['W_v'], 'L1_xattn_W_k_ip': _L1_xattn_in['W_k_ip'], 'L1_xattn_W_v_ip': _L1_xattn_in['W_v_ip'], 'L1_xattn_W_out': _L1_xattn_in['W_out'], 'L1_xattn_b_out': _L1_xattn_in['b_out']}

def reference(x, ctx_2048, fside_Bx4x4_0, fside_S_0, L0_xattn_w_q, L0_xattn_w_k, L0_xattn_w_v, L0_xattn_w_k_ip, L0_xattn_w_v_ip, L0_xattn_w_out, L0_xattn_b_out, L1_xattn_W_q, L1_xattn_W_k, L1_xattn_W_v, L1_xattn_W_k_ip, L1_xattn_W_v_ip, L1_xattn_W_out, L1_xattn_b_out):
    import jax
    import jax.numpy as jnp

    def _L0_xattn_ref(hidden_states, encoder_hidden_states, bbox, w_q, w_k, w_v, w_k_ip, w_v_ip, w_out, b_out):
        import jax, jax.numpy as jnp
        import numpy as np
        HEADS = 20
        NUM_IP_TOKENS = 4
        NUM_DUMMY_TOKENS = 4
        IP_SCALE = 1.0
        ASPECT_RATIO = 1.0
        NEG = -10000.0

        def _grid_hw(seq_len, aspect_ratio):
            width = int((seq_len / aspect_ratio) ** 0.5)
            height = seq_len // width
            while width * height != seq_len:
                if width * height < seq_len:
                    width += 1
                else:
                    width -= 1
                height = seq_len // width
            return (height, width)

        def _sdpa(q, k, v, mask=None):
            dh = q.shape[-1]
            scores = jnp.einsum('bhqd,bhkd->bhqk', q, k) / jnp.sqrt(jnp.asarray(dh, q.dtype))
            if mask is not None:
                scores = scores + mask
            probs = jax.nn.softmax(scores, axis=-1)
            return jnp.einsum('bhqk,bhkd->bhqd', probs, v)

        def _split_heads(x, heads):
            b, l, d = x.shape
            return x.reshape(b, l, heads, d // heads).transpose(0, 2, 1, 3)

        def _merge_heads(x):
            b, h, l, dh = x.shape
            return x.transpose(0, 2, 1, 3).reshape(b, l, h * dh)

        def _ip_mask(bbox, batch_size, seq_len, dtype):
            M = bbox.shape[1]
            height, width = _grid_hw(seq_len, ASPECT_RATIO)
            x = jnp.linspace(0.0, 1.0, width, dtype=dtype)
            y = jnp.linspace(0.0, 1.0, height, dtype=dtype)
            yg, xg = jnp.meshgrid(y, x, indexing='ij')
            xg = xg.reshape(-1)
            yg = yg.reshape(-1)
            x1, y1, x2, y2 = (bbox[..., 0:1], bbox[..., 1:2], bbox[..., 2:3], bbox[..., 3:4])
            inside = (xg >= x1) & (xg <= x2) & (yg >= y1) & (yg <= y2)
            ip_mask = jnp.where(inside, 0.0, NEG).astype(dtype)
            ip_mask = jnp.transpose(ip_mask, (0, 2, 1))[:, None]
            ip_mask = jnp.repeat(ip_mask, NUM_IP_TOKENS // M, axis=-1)
            dummy = jnp.where(jnp.any(inside, axis=1), NEG, 0.0).astype(dtype)
            dummy = jnp.repeat(dummy[:, None, :, None], NUM_DUMMY_TOKENS, axis=-1)
            return jnp.concatenate([dummy, ip_mask], axis=-1)
        B, S, D = hidden_states.shape
        residual = hidden_states
        end_pos = encoder_hidden_states.shape[1] - (NUM_IP_TOKENS + NUM_DUMMY_TOKENS)
        text = encoder_hidden_states[:, :end_pos]
        ip_h = encoder_hidden_states[:, end_pos:]
        q = _split_heads(hidden_states @ w_q, HEADS)
        k = _split_heads(text @ w_k, HEADS)
        v = _split_heads(text @ w_v, HEADS)
        out_text = _sdpa(q, k, v)
        out_text = _merge_heads(out_text)
        mask_ip = _ip_mask(bbox, B, S, hidden_states.dtype)
        k_ip = _split_heads(ip_h @ w_k_ip, HEADS)
        v_ip = _split_heads(ip_h @ w_v_ip, HEADS)
        out_ip = _merge_heads(_sdpa(q, k_ip, v_ip, mask=mask_ip))
        out = out_text + IP_SCALE * out_ip
        out = out @ w_out + b_out
        out = out + residual
        return out

    def _L1_xattn_ref(hidden_states, encoder_hidden_states, spatial_mask, W_q, W_k, W_v, W_k_ip, W_v_ip, W_out, b_out):
        import jax, jax.numpy as jnp
        import numpy as np
        HEADS = 20
        NUM_TOKENS = 4
        IP_SCALE = 1.0
        SEM_SCALE = 0.5
        RESCALE = 1.0
        EPS = 1e-12

        def _l2norm(x, axis=-1):
            n = jnp.sqrt(jnp.sum(x * x, axis=axis, keepdims=True))
            return x / jnp.maximum(n, EPS)
        B, S, C = hidden_states.shape
        H = HEADS
        Dh = C // H
        attn_scale = Dh ** (-0.5)
        residual = hidden_states
        text_ehs = encoder_hidden_states[:, :-NUM_TOKENS]
        ip_ehs = encoder_hidden_states[:, -NUM_TOKENS:]

        def heads(x):
            return x.reshape(B, -1, H, Dh).transpose(0, 2, 1, 3)
        q = heads(hidden_states @ W_q)
        k_t = heads(text_ehs @ W_k)
        v_t = heads(text_ehs @ W_v)
        scores_t = jnp.einsum('bhsd,bhtd->bhst', q, k_t) * attn_scale
        probs_t = jax.nn.softmax(scores_t, axis=-1)
        text_out = jnp.einsum('bhst,bhtd->bhsd', probs_t, v_t)
        text_out = text_out.transpose(0, 2, 1, 3).reshape(B, S, C)
        k_ip = heads(ip_ehs @ W_k_ip)
        v_ip = heads(ip_ehs @ W_v_ip)
        attn_scores = jnp.einsum('bhsd,bhnd->bhsn', q, k_ip) * attn_scale
        qsem = jnp.einsum('bhst,bte->bhse', probs_t, text_ehs)
        qsem = _l2norm(qsem)
        ip_n = _l2norm(ip_ehs)
        sem = jnp.einsum('bhse,bne->bhsn', qsem, ip_n)
        sem = jax.lax.stop_gradient(sem)
        fused = attn_scores + SEM_SCALE * sem
        probs_ip = jax.nn.softmax(fused, axis=-1)
        probs_ip = probs_ip * spatial_mask[None, None, :, None]
        ip_out = jnp.einsum('bhsn,bhnd->bhsd', probs_ip, v_ip)
        ip_out = ip_out.transpose(0, 2, 1, 3).reshape(B, S, C)
        out = text_out + IP_SCALE * ip_out
        out = out @ W_out + b_out
        out = out + residual
        return out / RESCALE
    x = _L0_xattn_ref(x, ctx_2048, fside_Bx4x4_0, L0_xattn_w_q, L0_xattn_w_k, L0_xattn_w_v, L0_xattn_w_k_ip, L0_xattn_w_v_ip, L0_xattn_w_out, L0_xattn_b_out)
    x = _L1_xattn_ref(x, ctx_2048, fside_S_0, L1_xattn_W_q, L1_xattn_W_k, L1_xattn_W_v, L1_xattn_W_k_ip, L1_xattn_W_v_ip, L1_xattn_W_out, L1_xattn_b_out)
    return x

_drawn_inputs = setup_inputs


def setup_inputs(seed=0):
    import zlib

    import numpy as np

    out = dict(_drawn_inputs(seed))
    spreads = {'L0_xattn_b_out': (0.0, 0.1), 'L1_xattn_b_out': (0.0, 0.1)}
    factors = {'fside_Bx4x4_0': 3.108, 'L0_xattn_w_q': 8.0, 'L0_xattn_w_k': 8.0, 'L0_xattn_w_k_ip': 8.0}
    for name, (base, spread) in spreads.items():
        noise = np.random.default_rng([zlib.crc32(name.encode()), seed]).standard_normal(out[name].shape)
        drawn = base * np.exp(spread * noise) if base else spread * noise
        out[name] = jnp.asarray(drawn.astype(out[name].dtype))
    for name, factor in factors.items():
        out[name] = (out[name] * factor).astype(out[name].dtype)
    return out
```

```python
from contextlib import ExitStack

import numpy as np
import concourse.bass as bass
from concourse import mybir

F32 = mybir.dt.float32
BF16 = mybir.dt.bfloat16
F16 = mybir.dt.float16
U32 = mybir.dt.uint32
ALU = mybir.AluOpType
ACT = mybir.ActivationFunctionType
AX = mybir.AxisListType

P = 128
B, S, D, C = 4, 256, 160, 256
H, DH = 20, 8
TOK = 1601
IP = (8, 4)
TXT = (TOK - IP[0], TOK - IP[1])
NT = (TOK + P - 1) // P
NPAD = NT * P
NK = 1600
PAIRS = H // 2
G = B * PAIRS
NH = S // P
U = B * NH
VW = 13
RING = 4
KROWS = 96
Q_PART = (0, 0, 0, 1, 1, 2)
K_RUNS = ((0, 3), (3, 2), (5, 1))
SCALE = float(DH) ** -0.5
EPS = 1e-12
NEG = -10000.0
SEM_SCALE = 0.5
SHIFT = (0.0, 14 * float(np.log(2.0)) / SCALE)
KSEG = ((0, 0, 128, 0, 0), (1, 0, 32, 0, 16), (1, 32, 96, 1, 0), (2, 0, 64, 1, 12))


def build(nc, x, ctx_in, bbox, spatial, w, consts, out):
    top = ExitStack()
    with top:
        def sbuf(name, shape, dt, stack=top):
            return stack.enter_context(nc.sbuf_tensor(name, shape, dt))

        KS = [nc.dram_tensor(f"k_parts_{l}", [H, B, 3, DH, NK], BF16).ap() for l in range(2)]
        QS = [nc.dram_tensor(f"q_parts_{l}", [H, 6, DH, B, S], BF16).ap() for l in range(2)]
        VS = [nc.dram_tensor(f"v_cols_{l}", [PAIRS, B, P, NT * 2 * VW], F32).ap() for l in range(2)]

        ps_x = top.enter_context(nc.psum_tensor("ps_x", [P, 2, 512], F32))
        ps_y = top.enter_context(nc.psum_tensor("ps_y", [P, 2, 512], F32))
        ps_t = top.enter_context(nc.psum_tensor("ps_t", [P, 2, 512], F32))
        ps_v = top.enter_context(nc.psum_tensor("ps_v", [P, 512], F32))
        ps_n = top.enter_context(nc.psum_tensor("ps_n", [P, 512], F32))
        banks = [ps_x[:, 0], ps_x[:, 1], ps_y[:, 0], ps_y[:, 1], ps_t[:, 0], ps_t[:, 1], ps_v[:, :], ps_n[:, :]]

        K = dict(
            ident=sbuf("ident", [P, P], F32), identb=sbuf("identb", [P, P], BF16), fold=sbuf("fold", [P, 2 * VW], F32),
            xq=sbuf("xq", [P, U, D], F32),
            qT0=sbuf("qT0", [P, U * P], F32), qT1=sbuf("qT1", [D - P, U * P], F32),
            ipT=sbuf("ipT", [P, 2, B, IP[0]], F32),
            eh=sbuf("eh", [P, B, NT, C], F16), el=sbuf("el", [P, B, NT, C], F16),
            einv=sbuf("einv", [P, B], F32),
            res=sbuf("res", [P, G, NH, 2 * VW], F32),
            n2=sbuf("n2", [P, G, 4], F32),
            kb=sbuf("kb", [P, RING, NPAD], BF16),
            qb=sbuf("qb", [P, RING, 2 * S], BF16),
        )
        prepare(nc, K, banks, ctx_in, x, w, consts, KS, VS)
        queries(nc, K, 0, banks, w["wq"][0], QS[0])
        attend(nc, K, 0, KS[0], QS[0], VS[0], ps_x, ps_y, ps_t, ps_v, ps_n)
        close(nc, K, 0, banks, w, consts, bbox, spatial, None)
        queries(nc, K, 1, banks, w["wq"][1], QS[1])
        attend(nc, K, 1, KS[1], QS[1], VS[1], ps_x, ps_y, ps_t, ps_v, ps_n)
        close(nc, K, 1, banks, w, consts, bbox, spatial, out)


CHUNK_AT = ({0: (1, 2), 2: (1, 3), 4: (1, 4), 5: (1, 5), 6: (1, 6), 8: (1, 7), 10: (2, 0), 12: (2, 1)},
            {0: (1, 1), 2: (1, 2), 3: (1, 3), 5: (1, 4), 6: (1, 5), 8: (1, 6), 9: (1, 7), 11: (2, 0)})


def prepare(nc, K, banks, ctx_in, x, w, consts, KS, VS):
    with ExitStack() as st:
        def sbuf(name, shape, dt):
            return st.enter_context(nc.sbuf_tensor(name, shape, dt))

        def sem(name):
            return st.enter_context(nc.semaphore(name))

        LAST = TOK - P * (NT - 1)
        TR, KI, KC = (NT + 1) // 2, 12, 400
        e32 = sbuf("e32", [P, NT, C], F32)
        ctxT = sbuf("ctxT", [P, 2, NPAD], F32)
        kp = sbuf("kp", [P, 3, 3, NK], BF16)
        rem = sbuf("rem", [P, 2, KC], F32)
        vaug = sbuf("vaug", [P, 2 * PAIRS, NT, 2, VW], F32)
        wk = sbuf("wk", [P, 2, 2 * D], F32)
        wv = sbuf("wv", [P, 2, 2 * D + IP[1]], F32)
        amax = sbuf("amax", [P, 2], F32)
        ebits = sbuf("ebits", [P, 4], U32)
        const_in, weights_in, init = sem("const_in"), sem("weights_in"), sem("init")
        pool_init = sem("pool_init")
        ctx_loaded = sem("ctx_loaded")
        filled = [sem(f"filled_{n}") for n in range(8)]
        freed = [sem(f"freed_{n}") for n in range(8)]
        ip_done, k0_done, k1_done, k2_done = sem("ip_done"), sem("k0_done"), sem("k1_done"), sem("k2_done")
        v_sent, k_sent = sem("v_sent"), sem("k_sent")
        amax_done, amax_all, bits = sem("amax_done"), sem("amax_all"), sem("bits")
        eh_done, el_done = sem("eh_done"), sem("el_done")

        def fills(b, n):
            return 4 * b + n // 8 + 1

        with nc.Block() as block:
            @block.sync
            def _(sp):
                sp.dma_start(K["ident"][:], consts["ident"]).then_inc(const_in, 16)
                sp.dma_start(K["fold"][:], consts["fold"]).then_inc(const_in, 16)
                sp.wait_ge(init, 1)

                def load(b):
                    src = ctx_in[b] if isinstance(b, int) else ctx_in[bass.ds(b, 1)].rearrange("a t c -> (a t) c")
                    sp.dma_start(e32[:, 0:NT - 1, :], src[0:P * (NT - 1)].rearrange("(t p) c -> p t c", p=P)).then_inc(ctx_loaded, 16)
                    sp.dma_start(e32[0:LAST, NT - 1, :], src[P * (NT - 1):TOK]).then_inc(ctx_loaded, 16)

                def send(b):
                    for m, r0, rows, l, h0 in KSEG:
                        sp.wait_ge(k2_done, KI * b + 4 * (m + 1))
                        sp.wait_ge(init, 1)
                        for part in range(3):
                            dst = KS[l][h0:h0 + rows // DH, bass.ds(b, 1), part]
                            sp.dma_start(dst, kp[r0:r0 + rows, m, part, :]).then_inc(k_sent, 16)
                    sp.wait_ge(freed[7], fills(b, 31))
                    sp.wait_ge(init, 1)
                    for l in range(2):
                        dst = VS[l][:, bass.ds(b, 1)].rearrange("g b p n -> p b g n")
                        sp.dma_start(dst, vaug[:, l * PAIRS:(l + 1) * PAIRS].rearrange("p g t i n -> p g (t i n)")).then_inc(v_sent, 16)

                load(0)
                for l in range(2):
                    sp.dma_start(wk[:, :, l * D:(l + 1) * D], w["wk"][l].rearrange("(c p) n -> p c n", p=P)).then_inc(weights_in, 16)
                    sp.dma_start(wv[:, :, l * D:(l + 1) * D], w["wv"][l].rearrange("(c p) n -> p c n", p=P)).then_inc(weights_in, 16)
                sp.dma_start(K["xq"][:], x.rearrange("b (h p) c -> p (b h) c", p=P)).then_inc(const_in, 16)

                def turn(b):
                    sp.wait_ge(el_done, 2 * b)
                    sp.wait_ge(freed[TR - 1], fills(b - 1, TR - 1))
                    sp.wait_ge(init, 1)
                    load(b)
                    send(b - 1)

                turn(1)
                with sp.Fori(2, B, 1) as b:
                    turn(b)
                send(B - 1)
                sp.wait_ge(const_in, 48)
                sp.wait_ge(k_sent, 16 * 3 * len(KSEG) * B)
                sp.wait_ge(v_sent, 16 * 2 * B)

            @block.tensor
            def _(pe):
                pe.wait_ge(const_in, 48)
                pe.wait_ge(weights_in, 64)

                def batch(b, first):
                    def bank(n):
                        if n >= 8 or not first:
                            pe.wait_ge(freed[n % 8], fills(b, n) - 1)
                        return banks[n % 8]

                    pe.wait_ge(ctx_loaded, 32 * (b + 1))
                    for n in range(TR):
                        ps = bank(n)
                        for t in range(2 * n, min(2 * n + 2, NT)):
                            for c in range(2):
                                at = ((t % 2) * 2 + c) * P
                                last = pe.transpose(ps[:, at:at + P], e32[:, t, c * P:(c + 1) * P], K["ident"][:])
                        last.then_inc(filled[n % 8], 1)
                    for n in range(TR):
                        pe.wait_ge(freed[n], fills(b, n))
                    for n in range(KI):
                        m, kc = n // 4, n % 4
                        rows = min(P, 2 * D - m * P)
                        ps = bank(TR + n)
                        for c in range(2):
                            last = pe.matmul(ps[0:rows, 0:KC], wk[:, c, m * P:m * P + rows],
                                             ctxT[:, c, kc * KC:(kc + 1) * KC], start=(c == 0), stop=(c == 1))
                        last.then_inc(filled[(TR + n) % 8], 1)
                    pe.wait_ge(ip_done, 2 * (b + 1))
                    for t in range(NT):
                        n = TR + KI + t
                        ps = bank(n)
                        for c in range(2):
                            last = pe.matmul(ps[:, 0:2 * D + IP[1]], ctxT[:, c, t * P:(t + 1) * P], wv[:, c, :],
                                             start=(c == 0), stop=(c == 1))
                        last.then_inc(filled[n % 8], 1)

                batch(0, True)
                with pe.Fori(1, B, 1) as b:
                    batch(b, False)

            def copy_transposed(eng, copy, b, n):
                nt = 2 if n < TR - 1 else 1
                eng.wait_ge(filled[n], fills(b, n))
                src = banks[n][:, 0:nt * 2 * P].rearrange("p (t c q) -> p c t q", t=nt, c=2)
                dst = ctxT[:, :, 2 * n * P:(2 * n + nt) * P].rearrange("p c (t q) -> p c t q", t=nt)
                copy(dst, src).then_inc(freed[n], 1)

            @block.scalar
            def _(act):
                def batch(b, first):
                    for n in (1, 3, 5):
                        copy_transposed(act, nc.scalar.copy, b, n)
                    if not first:
                        act.wait_ge(k_sent, 16 * 3 * len(KSEG) * b)
                    for n in range(KI):
                        m, kc = n // 4, n % 4
                        rows = min(P, 2 * D - m * P)
                        act.wait_ge(filled[(TR + n) % 8], fills(b, TR + n))
                        nc.scalar.copy(kp[0:rows, m, 0, kc * KC:(kc + 1) * KC], banks[(TR + n) % 8][0:rows, 0:KC]).then_inc(k0_done, 1)
                        if n == 3:
                            act.wait_ge(bits, 4 * (b + 1))
                            scale = ebits[:, 2:3].bitcast(F32)
                            act.wait_ge(init, 3)
                            for t0, t1, rows in ((0, NT - 1, P), (NT - 1, NT, TXT[1] - P * (NT - 1))):
                                dst = K["eh"][0:rows, b, t0:t1, :] if isinstance(b, int) else K["eh"][0:rows, bass.ds(b, 1), t0:t1, :].rearrange("p b t c -> p (b t) c")
                                nc.scalar.activation(dst, e32[0:rows, t0:t1, :], ACT.Copy, scale=scale[0:rows]).then_inc(eh_done, 1)
                    act.wait_ge(pool_init, 4)
                    if not first:
                        act.wait_ge(v_sent, 16 * 2 * b)
                    for t in range(NT):
                        n = TR + KI + t
                        act.wait_ge(filled[n % 8], fills(b, n))
                        for l in range(2):
                            rows = min(P, TXT[l] - t * P)
                            nc.scalar.copy(vaug[0:rows, l * PAIRS:(l + 1) * PAIRS, t, :, 0:DH],
                                           banks[n % 8][0:rows, l * D:(l + 1) * D].rearrange("p (g i d) -> p g i d", g=PAIRS, i=2))
                        rows = min(P, TXT[1] - t * P)
                        dots = banks[n % 8][0:rows, 2 * D:2 * D + IP[1]].unsqueeze(1).unsqueeze(1)
                        nc.scalar.copy(vaug[0:rows, PAIRS:2 * PAIRS, t, :, DH + 1:VW],
                                       dots.to_broadcast([rows, PAIRS, 2, IP[1]])).then_inc(freed[n % 8], 1)

                batch(0, True)
                with act.Fori(1, B, 1) as b:
                    batch(b, False)

            @block.gpsimd
            def _(pool):
                nc.gpsimd.memset(vaug[:], 0.0).then_inc(pool_init, 1)
                pool.wait_ge(pool_init, 1)
                for l in range(2):
                    rows = TXT[l] - P * (NT - 1)
                    ones = vaug[:, l * PAIRS:(l + 1) * PAIRS, :, :, DH]
                    nc.gpsimd.memset(ones[:, :, 0:NT - 1], 1.0)
                    last = nc.gpsimd.memset(ones[0:rows, :, NT - 1], 1.0)
                last.then_inc(pool_init, 3)
                def batch(b):
                    pool.wait_ge(amax_done, b + 1)
                    nc.gpsimd.partition_all_reduce(amax[:, 1:2], amax[:, 0:1], P, bass.bass_isa.ReduceOp.max).then_inc(amax_all, 1)

                batch(0)
                pool.wait_ge(amax_all, 1)
                nc.gpsimd.memset(K["qb"][:], 0.0)
                nc.gpsimd.memset(K["kb"][:, :, TXT[0]:NPAD], 0.0).then_inc(pool_init, 1)
                pool.wait_ge(pool_init, 5)
                nc.gpsimd.memset(K["kb"][KROWS:KROWS + 2, :, 0:TXT[0]], 1.0).then_inc(pool_init, 1)
                pool.wait_ge(pool_init, 6)
                for b in range(1, B):
                    batch(b)

            @block.vector
            def _(dve):
                nc.vector.memset(e32[64:P, NT - 1, :], 0.0).then_inc(init, 1)
                nc.vector.memset(K["eh"][:, :, NT - 1, :], 0.0).then_inc(init, 1)
                nc.vector.memset(K["el"][:, :, NT - 1, :], 0.0).then_inc(init, 1)
                dve.wait_ge(init, 3)
                dve.wait_ge(const_in, 48)
                nc.vector.tensor_copy(K["identb"][:], K["ident"][:]).then_inc(init, 1)
                dve.wait_ge(init, 4)

                def batch(b, first):
                    for n in (0, 2, 4, 6):
                        copy_transposed(dve, nc.vector.tensor_copy, b, n)
                    dve.wait_ge(freed[6], fills(b, 6))
                    ipd = K["ipT"][:, :, b, :] if isinstance(b, int) else K["ipT"][:, :, bass.ds(b, 1), :].rearrange("p c b n -> p c (b n)")
                    nc.vector.tensor_copy(ipd, ctxT[:, :, TOK - IP[0]:TOK]).then_inc(ip_done, 1)
                    if not first:
                        dve.wait_ge(filled[7], fills(b, 31) - 4)
                    nc.vector.tensor_copy(wv[:, :, 2 * D:2 * D + IP[1]], ctxT[:, :, TOK - IP[1]:TOK]).then_inc(ip_done, 1)
                    nc.vector.tensor_reduce(amax[:, 0:1], e32[:], AX.XY, ALU.max, apply_absolute_value=True).then_inc(amax_done, 1)
                    for n in range(KI):
                        m, kc = n // 4, n % 4
                        rows = min(P, 2 * D - m * P)
                        k0 = kp[0:rows, m, 0, kc * KC:(kc + 1) * KC]
                        k1 = kp[0:rows, m, 1, kc * KC:(kc + 1) * KC]
                        k2 = kp[0:rows, m, 2, kc * KC:(kc + 1) * KC]
                        r = rem[0:rows, n % 2, :]
                        dve.wait_ge(k0_done, KI * b + n + 1)
                        nc.vector.tensor_tensor(r, banks[(TR + n) % 8][0:rows, 0:KC], k0, ALU.subtract).then_inc(freed[(TR + n) % 8], 1)
                        dve.wait_ge(freed[(TR + n) % 8], fills(b, TR + n))
                        nc.vector.tensor_copy(k1, r).then_inc(k1_done, 1)
                        dve.wait_ge(k1_done, KI * b + n + 1)
                        nc.vector.tensor_tensor(k2, r, k1, ALU.subtract).then_inc(k2_done, 1)
                        if n == 1:
                            dve.wait_ge(amax_all, b + 1)
                            if not first:
                                dve.wait_ge(el_done, 2 * b)
                            e = ebits[:, 0:1]
                            nc.vector.tensor_scalar(e, amax[:, 1:2].bitcast(U32), 23, None, ALU.logical_shift_right).then_inc(bits, 1)
                            dve.wait_ge(bits, 4 * b + 1)
                            nc.vector.tensor_scalar(e, e, 15, None, ALU.max).then_inc(bits, 1)
                            dve.wait_ge(bits, 4 * b + 2)
                            nc.vector.tensor_scalar(ebits[:, 1:2], e, -1, 268, ALU.mult, ALU.add)
                            nc.vector.tensor_scalar(ebits[:, 3:4], e, -14, None, ALU.add).then_inc(bits, 1)
                            dve.wait_ge(bits, 4 * b + 3)
                            einv = K["einv"][:, b:b + 1] if isinstance(b, int) else K["einv"][:, bass.ds(b, 1)]
                            nc.vector.tensor_scalar(einv.bitcast(U32), ebits[:, 3:4], 23, None, ALU.logical_shift_left)
                            nc.vector.tensor_scalar(ebits[:, 2:3], ebits[:, 1:2], 23, None, ALU.logical_shift_left).then_inc(bits, 1)
                            dve.wait_ge(bits, 4 * b + 4)
                        if n in (5, 6):
                            t0, t1, rows = ((0, NT - 1, P), (NT - 1, NT, TXT[1] - P * (NT - 1)))[n - 5]
                            at = (lambda a: a[0:rows, b, t0:t1, :]) if isinstance(b, int) else (lambda a: a[0:rows, bass.ds(b, 1), t0:t1, :].rearrange("p b t c -> p (b t) c"))
                            dve.wait_ge(eh_done, 2 * b + n - 4)
                            nc.vector.scalar_tensor_tensor(out=at(K["el"]), in0=e32[0:rows, t0:t1, :], scalar=ebits[0:rows, 2:3].bitcast(F32),
                                                           in1=at(K["eh"]), op0=ALU.mult, op1=ALU.subtract).then_inc(el_done, 1)

                batch(0, True)
                with dve.Fori(1, B, 1) as b:
                    batch(b, False)


def queries(nc, K, layer, banks, wq, QS):
    with ExitStack() as st:
        def sbuf(name, shape, dt):
            return st.enter_context(nc.sbuf_tensor(f"{name}_{layer}", shape, dt))

        def sem(name):
            return st.enter_context(nc.semaphore(f"{name}_{layer}"))

        R1 = D - P
        xT0, xT1 = sbuf("xT0", [P, U * P], F32), sbuf("xT1", [R1, U * P], F32)
        w0, w1 = sbuf("wq0", [P, D], F32), sbuf("wq1", [R1, D], F32)
        parts = (sbuf("qp0", [P, 3, U * P], BF16), sbuf("qp1", [R1, 3, U * P], BF16))
        r = (sbuf("qr0", [P, U * P], F32), sbuf("qr1", [R1, U * P], F32))
        w_in, turned, xT_done, made, q_done = sem("w_in"), sem("turned"), sem("xT_done"), sem("made"), sem("q_done")
        cut = (sem("cut_0"), sem("cut_1"))
        sent = sem("sent")
        with nc.Block() as block:
            @block.sync
            def _(sp):
                sp.dma_start(w0[:], wq[0:P]).then_inc(w_in, 16)
                sp.dma_start(w1[:], wq[P:D]).then_inc(w_in, 16)
                for m in range(2):
                    sp.wait_ge(cut[m], 4)
                for m in range(2):
                    h0, nh = ((0, P // DH), (P // DH, R1 // DH))[m]
                    for j, part in enumerate(Q_PART):
                        dst = QS[h0:h0 + nh, j].rearrange("h d b q -> h d (b q)")
                        sp.dma_start(dst, parts[m][:, part, :]).then_inc(sent, 16)
                sp.wait_ge(sent, 16 * 12)

            @block.tensor
            def _(pe):
                for u in range(U):
                    pe.transpose(banks[u // 4][:, (u % 4) * P:(u % 4 + 1) * P], K["xq"][:, u, 0:P], K["ident"][:])
                    last = pe.transpose(banks[2 + u // 4][0:R1, (u % 4) * P:(u % 4 + 1) * P], K["xq"][:, u, P:D], K["ident"][:])
                last.then_inc(turned, 1)
                pe.wait_ge(w_in, 32)
                pe.wait_ge(xT_done, 4)
                for n in range(2):
                    for m, (c0, c1) in enumerate(((0, P), (P, D))):
                        ps = banks[4 + 2 * m + n][0:c1 - c0, :]
                        pe.matmul(ps, w0[:, c0:c1], xT0[:, n * 512:(n + 1) * 512], start=True, stop=False)
                        pe.matmul(ps, w1[:, c0:c1], xT1[:, n * 512:(n + 1) * 512], start=False, stop=True).then_inc(made, 1)

            @block.scalar
            def _(act):
                act.wait_ge(turned, 1)
                for n in range(2):
                    nc.scalar.copy(xT0[:, n * 512:(n + 1) * 512], banks[n]).then_inc(xT_done, 1)
                act.wait_ge(made, 4)
                for n in range(2):
                    nc.scalar.copy(K["qT0"][:, n * 512:(n + 1) * 512], banks[4 + n]).then_inc(q_done, 1)
                for n in range(2):
                    nc.scalar.copy(K["qT1"][:, n * 512:(n + 1) * 512], banks[6 + n][0:R1, :]).then_inc(q_done, 1)

            def cut_parts(eng, m, q):
                steps = cut[m]
                eng.tensor_copy(parts[m][:, 0], q).then_inc(steps, 1)
                eng.wait_ge(steps, 1)
                eng.tensor_tensor(r[m][:], q, parts[m][:, 0], ALU.subtract).then_inc(steps, 1)
                eng.wait_ge(steps, 2)
                eng.tensor_copy(parts[m][:, 1], r[m][:]).then_inc(steps, 1)
                eng.wait_ge(steps, 3)
                eng.tensor_tensor(parts[m][:, 2], r[m][:], parts[m][:, 1], ALU.subtract).then_inc(steps, 1)

            @block.vector
            def _(dve):
                dve.wait_ge(turned, 1)
                for n in range(2):
                    nc.vector.tensor_copy(xT1[:, n * 512:(n + 1) * 512], banks[2 + n][0:R1, :]).then_inc(xT_done, 1)
                dve.wait_ge(q_done, 2)
                cut_parts(nc.vector, 0, K["qT0"][:])
                dve.wait_ge(q_done, 4)
                cut_parts(nc.vector, 1, K["qT1"][:])


def attend(nc, K, layer, KS, QS, VS, ps_x, ps_y, ps_t, ps_v, ps_n):
    with ExitStack() as st:
        def sbuf(name, shape, dt):
            return st.enter_context(nc.sbuf_tensor(f"{name}_{layer}", shape, dt))

        def sem(name):
            return st.enter_context(nc.semaphore(f"{name}_{layer}"))

        NV = TXT[layer]
        CUT = ((NV + 1) // 2, NV // 2)
        kb, qb = K["kb"], K["qb"]
        vb = sbuf("vb", [P, 2, NT, 2, VW], F32)
        pe32 = sbuf("pe32", [P, 2, NT, 2 * S], F32)
        if layer:
            ph = sbuf("ph", [P, 2, NT, 2 * S], F16)
            pl = sbuf("pl", [P, 2, NT, 2 * S], F16)
            junk = sbuf("junk", [P, 2, S], F32)
        acc = sbuf("acc", [P, 2, S], F32)
        mx = sbuf("mx", [P, 2, 8], F32)
        mm = sbuf("mm", [P, 2, 4], F32)
        mn = sbuf("mn", [P, 2, 4], F32)
        shift = sbuf("shift", [P, 4], F32)
        mp = sbuf("mp", [P, 2, 4, 2], BF16)
        ready = sem("ready")
        kq_loaded = [sem(f"kq_loaded_{n}") for n in range(RING)]
        v_loaded = [sem(f"v_loaded_{n}") for n in range(2)]
        chunk_made, chunk_max = sem("chunk_made"), sem("chunk_max")
        m1, m2, m3, m_parts = sem("m1"), sem("m2"), sem("m3"), sem("m_parts")
        m_turned, m_rows = sem("m_turned"), sem("m_rows")
        st_made, exp_done = sem("st_made"), sem("exp_done")
        acc_made, acc_out, turned, turned_out = sem("acc_made"), sem("acc_out"), sem("turned"), sem("turned_out")
        if layer:
            half_done, low_done, norm_made, norm_out = sem("half_done"), sem("low_done"), sem("norm_made"), sem("norm_out")
        HALVES = (NT + 1) // 2

        def TILE_POS(t):
            return t if t < 3 else t + 1 if t < NT - 1 else NT + 1

        def TURN(o, pos):
            return (o + pos) % 2

        def at_least(eng, semaphore, value):
            if not isinstance(value, int) or value > 0:
                eng.wait_ge(semaphore, value)

        def uses(k, o, n):
            return (4 // n) * k + o // n + 1

        def steps(eng, step):
            for s in range(-2, 2):
                step(0, s)
            with eng.Fori(0, (G - 4) // 4, 1) as k:
                for o in range(2, 6):
                    step(k, o)
            for s in range(G - 2, G + 2):
                step(0, s)

        def has(k, o, d):
            return not isinstance(k, int) or 0 <= o + d < G

        with nc.Block() as block:
            @block.sync
            def _(sp):
                sp.wait_ge(ready, 2)

                def load(k, o):
                    s, n = 4 * k + o, o % RING
                    if not isinstance(s, int) or s >= RING:
                        sp.wait_ge(st_made, NT * (s - RING + 1))
                        sp.wait_ge(ready, 2)
                    for i in range(2):
                        for j, parts in K_RUNS:
                            src = KS[bass.ds(2 * (k + o // B) + i, 1), o % B, 0:parts, :, 0:NV].rearrange("h j d k -> (h j d) k")
                            r0 = 48 * i + DH * j
                            sp.dma_start(kb[r0:r0 + DH * parts, n, 0:NV], src).then_inc(kq_loaded[n], 16)
                        src = QS[bass.ds(2 * (k + o // B) + i, 1), :, :, o % B, :].rearrange("h j d q -> (h j d) q")
                        sp.dma_start(qb[48 * i:48 * i + 48, n, i * S:(i + 1) * S], src).then_inc(kq_loaded[n], 16)

                def load_v(k, o):
                    s = 4 * k + o
                    if not isinstance(s, int) or s >= 2:
                        sp.wait_ge(acc_made, s - 1)
                        sp.wait_ge(ready, 2)
                    src = VS[bass.ds(k + o // B, 1), o % B].rearrange("g p n -> (g p) n")
                    sp.dma_start(vb[:, o % 2].rearrange("p t i n -> p (t i n)"), src).then_inc(v_loaded[o % 2], 16)

                for s in range(RING):
                    load(0, s)
                    if s:
                        load_v(0, s - 1)
                with sp.Fori(1, G // 4, 1) as k:
                    for o in range(4):
                        load(k, o)
                        load_v(k, o - 1)
                load_v(0, G - 1)

            @block.tensor
            def _(pe):
                pe.wait_ge(ready, 2)

                def scores(k, o, c):
                    if not has(k, o, 1):
                        return
                    s, n = 4 * k + o + 1, (o + 1) % RING
                    hh, e = c // 2, c % 2
                    if c == 0:
                        pe.wait_ge(kq_loaded[n], 128 * uses(k, o + 1, RING))
                    at_least(pe, chunk_max, 8 * s + c - 1)
                    ps = (ps_x, ps_y)[c % 2]
                    k0, k1 = (0, CUT[0]) if e == 0 else (CUT[0], NV)
                    for a in range(k0, k1, 512):
                        z = min(a + 512, k1)
                        last = pe.matmul(ps[:, (a - k0) // 512, 0:z - a], qb[0:KROWS, n, hh * P:(hh + 1) * P],
                                         kb[0:KROWS, n, a:z], start=True, stop=True)
                    last.then_inc(chunk_made, 1)

                def turn_max(k, o):
                    if not has(k, o, 1):
                        return
                    s = 4 * k + o
                    pe.wait_ge(m_parts, s + 2)
                    if has(k, o, 0):
                        pe.wait_ge(exp_done, NT * s + NT - 2)
                    for hh in range(4):
                        last = pe.matmul(ps_t[KROWS:KROWS + 2, TURN(o, NT), hh * P:(hh + 1) * P], mp[:, (o + 1) % 2, hh, :], K["identb"][:],
                                         start=True, stop=True)
                    last.then_inc(m_turned, 1)

                def turn_result(k, o):
                    if not has(k, o, -2):
                        return
                    s = 4 * k + o
                    pe.wait_ge(acc_out, s - 1)
                    at_least(pe, exp_done, NT * s + 2 if has(k, o, 0) else NT * G)
                    for h in range(NH):
                        last = pe.matmul(ps_t[:, TURN(o, 3), 32 * h:32 * h + 2 * VW], acc[:, o % 2, h * P:(h + 1) * P], K["fold"][:],
                                         start=True, stop=True)
                    last.then_inc(turned, 1)

                def exponents(k, o, t):
                    if not has(k, o, 0):
                        return
                    s, n = 4 * k + o, o % RING
                    if t == 0:
                        pe.wait_ge(m_rows, s + 1)
                    if t == 4 and has(k, o, -2):
                        pe.wait_ge(turned_out, s - 1)
                    elif t:
                        at_least(pe, exp_done, NT * s + t - (0 if t in (3, NT - 1) else 1))
                    pe.matmul(ps_t[:, TURN(o, TILE_POS(t)), :], kb[0:KROWS + 2, n, t * P:(t + 1) * P], qb[0:KROWS + 2, n, :],
                              start=True, stop=True).then_inc(st_made, 1)

                def products(k, o, tiles):
                    if not has(k, o, -1):
                        return
                    s, n = 4 * k + o, (o - 1) % 2
                    if tiles[0] == 0:
                        at_least(pe, acc_out, s - 1)
                        pe.wait_ge(v_loaded[n], 16 * uses(k, o - 1, 2))
                    pe.wait_ge(exp_done, NT * (s - 1) + tiles[-1] + 1)
                    for i in range(2):
                        for t in tiles:
                            r0 = 32 * (2 * i + t % 2)
                            last = pe.matmul(ps_v[r0:r0 + VW, 0:S], vb[:, n, t, i, :], pe32[:, n, t, i * S:(i + 1) * S],
                                             start=(t < 2), stop=(t >= NT - 2))
                    if tiles[-1] == NT - 1:
                        last.then_inc(acc_made, 1)

                def norm_unit(k, o, q):
                    s, n = 4 * k + o, (o - 1) % 2
                    hh, t = q // NT, q % NT
                    if t == 0:
                        at_least(pe, norm_out, 4 * (s - 1) + hh)
                    if hh == 0:
                        pe.wait_ge(low_done, HALVES * (s - 1) + t // 2 + 1)
                    b = (o - 1) % B
                    hi, lo = ph[:, n, t, hh * P:(hh + 1) * P], pl[:, n, t, hh * P:(hh + 1) * P]
                    eh, el = K["eh"][:, b, t, :], K["el"][:, b, t, :]
                    pe.matmul(ps_n[:, 0:C], hi, eh, start=(t == 0), stop=False)
                    pe.matmul(ps_n[:, 0:C], hi, el, start=False, stop=False)
                    last = pe.matmul(ps_n[:, 0:C], lo, eh, start=False, stop=(t == NT - 1))
                    if t == NT - 1:
                        last.then_inc(norm_made, 1)

                def step(k, o):
                    for t in range(NT):
                        units = range(4 * t, 4 * t + 4) if layer and has(k, o, -1) else ()
                        before = [q for q in units if q // NT != (4 * t + 3) // NT]
                        for q in before:
                            norm_unit(k, o, q)
                        if t == NT - 1:
                            turn_max(k, o)
                        exponents(k, o, t)
                        if t == 2:
                            turn_result(k, o)
                        if t in CHUNK_AT[layer]:
                            d, c = CHUNK_AT[layer][t]
                            scores(k, o + d - 1, c)
                        if t % 2 == 1:
                            products(k, o, (t - 1, t))
                        elif t == NT - 1:
                            products(k, o, (t,))
                        for q in units:
                            if q not in before:
                                norm_unit(k, o, q)

                steps(pe, step)

            @block.scalar
            def _(act):
                def step(k, o):
                    s = 4 * k + o
                    def square(d, hh):
                        if not layer or not has(k, o, d):
                            return
                        act.wait_ge(norm_made, 4 * (s + d) + hh + 1)
                        g = 4 * (s + d) + hh
                        dst = K["n2"][:].rearrange("p g h -> p (g h)")
                        dst = dst[:, g:g + 1] if isinstance(g, int) else dst[:, bass.ds(g, 1)]
                        if not isinstance(g, int) or g >= 2:
                            act.wait_ge(norm_out, g - 1)
                        nc.scalar.activation(junk[:, hh % 2, :], ps_n[:, 0:C], ACT.Square, accum_out=dst).then_inc(norm_out, 1)

                    square(-2, 3)
                    if has(k, o, -2):
                        act.wait_ge(acc_made, s - 1)
                        nc.scalar.copy(acc[:, o % 2, :], ps_v[:, 0:S]).then_inc(acc_out, 1)
                    for t in range(NT):
                        if t in (3, 6, 9):
                            square(-1, t // 3 - 1)
                        if t == NT - 1 and has(k, o, 1):
                            act.wait_ge(m_turned, s + 2)
                            nc.scalar.copy(qb[KROWS:KROWS + 2, (o + 1) % RING, :], ps_t[KROWS:KROWS + 2, TURN(o, NT), :]).then_inc(m_rows, 1)
                        if has(k, o, 0):
                            if t == 0 and (not isinstance(s, int) or s >= 2):
                                act.wait_ge(acc_made, s - 1)
                                if layer:
                                    act.wait_ge(low_done, HALVES * (s - 1))
                                    act.wait_ge(norm_made, 4 * (s - 1))
                            act.wait_ge(st_made, NT * s + t + 1)
                            nc.scalar.activation(pe32[:, o % 2, t, :], ps_t[:, TURN(o, TILE_POS(t)), :], ACT.Exp, scale=SCALE).then_inc(exp_done, 1)
                            if layer and (t % 2 == 1 or t == NT - 1):
                                t0 = t - t % 2
                                act.wait_ge(exp_done, NT * s + t + 1)
                                nc.scalar.copy(ph[:, o % 2, t0:t + 1, :], pe32[:, o % 2, t0:t + 1, :]).then_inc(half_done, 1)
                        if t == 2 and has(k, o, -2):
                            act.wait_ge(turned, s - 1)
                            dst = K["res"][:, s - 2] if isinstance(s, int) else K["res"][:, bass.ds(s - 2, 1)].rearrange("p g h n -> p (g h) n")
                            src = ps_t[:, TURN(o, 3), 0:32 * NH].rearrange("p (h n) -> p h n", h=NH)[:, :, 0:2 * VW]
                            nc.scalar.copy(dst, src).then_inc(turned_out, 1)

                steps(act, step)

            @block.gpsimd
            def _(pool):
                nc.gpsimd.memset(shift[:], SHIFT[layer]).then_inc(ready, 1)
                pool.wait_ge(ready, 2)

                def step(k, o):
                    if not has(k, o, 1):
                        return
                    s, n = 4 * k + o + 1, (o + 1) % 2
                    pool.wait_ge(m1, s + 1)
                    nc.gpsimd.tensor_tensor(mn[:, n], mm[:, n], shift[:], ALU.add).then_inc(m2, 1)
                    if not isinstance(s, int) or s >= 2:
                        pool.wait_ge(m_turned, s - 1)
                    nc.gpsimd.tensor_tensor(mp[:, n, :, 0], mm[:, n], shift[:], ALU.add).then_inc(m3, 1)
                    pool.wait_ge(m2, s + 1)
                    pool.wait_ge(m3, s + 1)
                    nc.gpsimd.tensor_tensor(mp[:, n, :, 1], mn[:, n], mp[:, n, :, 0], ALU.subtract).then_inc(m_parts, 1)

                steps(pool, step)

            @block.vector
            def _(dve):
                if layer:
                    nc.vector.memset(kb[KROWS:KROWS + 2, :, TXT[0]:NV], 1.0)
                nc.vector.memset(ps_v[:], 0.0).then_inc(ready, 1)

                def step(k, o):
                    s = 4 * k + o

                    def chunk(d, c):
                        if not has(k, o, d):
                            return
                        pair = s + d
                        if c == 0 and (not isinstance(s, int) or pair >= 2):
                            dve.wait_ge(m1, pair - 1)
                        dve.wait_ge(chunk_made, 8 * pair + c + 1)
                        w = CUT[c % 2]
                        src = (ps_x, ps_y)[c % 2][:].rearrange("p a b -> p (a b)")[:, 0:w]
                        nc.vector.tensor_reduce(mx[:, (o + d) % 2, c:c + 1], src, AX.X, ALU.max).then_inc(chunk_max, 1)
                        if c == 7:
                            dve.wait_ge(chunk_max, 8 * (pair + 1))
                            if not isinstance(s, int) or pair >= 1:
                                dve.wait_ge(m3, pair)
                            nc.vector.tensor_reduce(mm[:, (o + d) % 2], mx[:, (o + d) % 2].rearrange("p (h e) -> p h e", e=2),
                                                    AX.X, ALU.max, negate=True).then_inc(m1, 1)

                    def low(n):
                        if not layer or not has(k, o, 0):
                            return
                        t0, t1 = 2 * n, min(2 * n + 2, NT)
                        dve.wait_ge(half_done, HALVES * s + n + 1)
                        nc.vector.tensor_tensor(pl[:, o % 2, t0:t1, :], pe32[:, o % 2, t0:t1, :], ph[:, o % 2, t0:t1, :],
                                                ALU.subtract).then_inc(low_done, 1)

                    for t in range(NT):
                        if t in CHUNK_AT[layer]:
                            chunk(*CHUNK_AT[layer][t])
                        if t % 2 == 0 and t:
                            low(t // 2 - 1)
                    low(HALVES - 1)

                steps(dve, step)


def close(nc, K, layer, banks, w, consts, bbox, spatial, out):
    with ExitStack() as st:
        def sbuf(name, shape, dt):
            return st.enter_context(nc.sbuf_tensor(f"{name}_{layer}", shape, dt))

        def sem(name):
            return st.enter_context(nc.semaphore(f"{name}_{layer}"))

        n = IP[layer]
        W = H * n
        CH = ((0, P), (P, D))
        RC = ((0, min(P, W)),) + (((P, W),) if W > P else ())
        tok = slice(IP[0] - n, IP[0])
        wki, wvi = sbuf("wki", [P, 2, D], F32), sbuf("wvi", [P, 2, D], F32)
        wo = (sbuf("wo0", [P, D], F32), sbuf("wo1", [D - P, D], F32))
        bias = sbuf("bias", [P, D], F32)
        mask_k = (sbuf("mask_k0", [P, W], F32), sbuf("mask_k1", [D - P, W], F32))
        mask_v = tuple(sbuf(f"mask_v{i}", [b - a, D], F32) for i, (a, b) in enumerate(RC))
        ip_rep = sbuf("ip_rep", [P, 2, B, W], F32)
        kip = (sbuf("kip0", [P, B, n], F32), sbuf("kip1", [D - P, B, n], F32))
        bk = (sbuf("bk0", [P, B, H, n], F32), sbuf("bk1", [D - P, B, H, n], F32))
        bv = tuple(sbuf(f"bv{i}", [b - a, B, D], F32) for i, (a, b) in enumerate(RC))
        extra = sbuf("extra", [P, U, H if layer else 1, n], F32)
        sc = sbuf("sc", [P, U, W], F32)
        smax, ssum = sbuf("smax", [P, U * H], F32), sbuf("ssum", [P, U * H], F32)
        pT = tuple(sbuf(f"pT{i}", [b - a, U, P], F32) for i, (a, b) in enumerate(RC))
        rz = sbuf("rz", [P, G, NH, 2], F32)
        text = sbuf("text", [P, U, D], F32)
        both = sbuf("both", [P, U, D], F32)
        oT = (sbuf("oT0", [P, U, P], F32), sbuf("oT1", [D - P, U, P], F32))
        base = sbuf("base", [P, U, D], F32)
        loaded = sem("loaded")
        NLOAD = 7 + len(RC) + (NH + 1 if layer else 2)
        rep_done, kip_made, kip_out, bk_done = sem("rep_done"), sem("kip_made"), sem("kip_out"), sem("bk_done")
        bv_made, bv_done = sem("bv_made"), sem("bv_done")
        sc_made = sem("sc_made")
        centred, exp_done, prob_done = sem("centred"), sem("exp_done"), sem("prob_done")
        pT_made, pT_out0, pT_out1 = sem("pT_made"), sem("pT_out0"), sem("pT_out1")
        o_made, o_out = sem("o_made"), sem("o_out")
        oT_made, oT_out0, oT_out1 = sem("oT_made"), sem("oT_out0"), sem("oT_out1")
        y_made, y_out, base_done = sem("y_made"), sem("y_out"), sem("base_done")
        dve_step = sem("dve_step")
        if layer:
            stored, root_done, sq_done, sq_made = sem("stored"), sem("root_done"), sem("sq_done"), sem("sq_made")
            norm = sbuf("norm", [P, G, NH, 2], F32)
            root = sbuf("root", [P, G, 4], F32)
            sq = sbuf("sq", [P, 2, B, n], F32)
            ones = sbuf("ones", [P, P], F32)
            ipn = sbuf("ipn", [P, B, n], F32)
            spat = sbuf("spat", [P, NH], F32)
        else:
            boxes = sbuf("boxes", [P, B, 4, 4], F32)
            grid = sbuf("grid", [P, 1 + NH], F32)
            cond = sbuf("cond", [P, 4, B, 4], F32)
            inside = sbuf("inside", [P, B, 4], F32)
            covered = sbuf("covered", [P, B], F32)

        with nc.Block() as block:
            @block.sync
            def _(sp):
                def load(dst, src):
                    sp.dma_start(dst, src).then_inc(loaded, 16)

                load(wki[:], w["wk_ip"][layer].rearrange("(c p) n -> p c n", p=P))
                load(wvi[:], w["wv_ip"][layer].rearrange("(c p) n -> p c n", p=P))
                load(wo[0][:], w["wo"][layer][0:P])
                load(wo[1][:], w["wo"][layer][P:D])
                load(bias[:], w["bo"][layer].partition_broadcast(P))
                load(mask_k[0][:], consts[f"mask_k{layer}"][0:P])
                load(mask_k[1][:], consts[f"mask_k{layer}"][P:D])
                for i, (a, b) in enumerate(RC):
                    load(mask_v[i][:], consts[f"mask_v{layer}"][a:b])
                if layer:
                    for h in range(NH):
                        load(spat[:, h:h + 1], spatial[h * P:(h + 1) * P].rearrange("(p o) -> p o", o=1))
                    load(ones[:], consts["ones"])
                else:
                    load(boxes[:].rearrange("p b m c -> p (b m c)"), bbox.rearrange("b m c -> (b m c)").partition_broadcast(P))
                    load(grid[:], consts["grid"])
                if out is not None:
                    for u in range(U):
                        sp.wait_ge(y_out, u + 1)
                        b, h = u // NH, u % NH
                        sp.dma_start(out[b, h * P:(h + 1) * P, :], K["xq"][:, u, :]).then_inc(stored, 16)
                    sp.wait_ge(stored, 16 * U)

            @block.tensor
            def _(pe):
                pe.wait_ge(loaded, 16 * NLOAD)
                for i, (a, b) in enumerate(CH):
                    for c in range(2):
                        last = pe.matmul(banks[i][0:b - a, 0:B * n], wki[:, c, a:b], K["ipT"][:, c, :, tok],
                                         start=(c == 0), stop=(c == 1))
                last.then_inc(kip_made, 1)
                pe.wait_ge(rep_done, 1)
                for b in range(B):
                    for i, (r0, r1) in enumerate(RC):
                        for c in range(2):
                            last = pe.matmul(banks[2 + b][0:r1 - r0, i * D:(i + 1) * D], ip_rep[:, c, b, r0:r1], wvi[:, c, :],
                                             start=(c == 0), stop=(c == 1))
                    last.then_inc(bv_made, 1)
                if layer:
                    pe.wait_ge(sq_done, 1)
                    for c in range(2):
                        last = pe.matmul(banks[6][:, 0:B * n], ones[:], sq[:, c], start=(c == 0), stop=(c == 1))
                    last.then_inc(sq_made, 1)
                    pe.wait_ge(root_done, 2)
                pe.wait_ge(bk_done, 2)
                pe.wait_ge(bv_done, B)
                for u in range(U):
                    b = u // NH
                    for i in range(2):
                        q = K[f"qT{i}"]
                        last = pe.matmul(banks[u][:, 0:W], q[:, u * P:(u + 1) * P], bk[i][:, b].rearrange("p h n -> p (h n)"),
                                         start=(i == 0), stop=(i == 1))
                    last.then_inc(sc_made, 1)
                pe.wait_ge(prob_done, 1)
                for u in range(U):
                    for i, (r0, r1) in enumerate(RC):
                        last = pe.transpose(banks[u][0:r1 - r0, i * P:(i + 1) * P], sc[:, u, r0:r1], K["ident"][:])
                    last.then_inc(pT_made, 1)
                for u in range(U):
                    pe.wait_ge(pT_out0, u + 1)
                    if len(RC) > 1:
                        pe.wait_ge(pT_out1, u + 1)
                    for i in range(len(RC)):
                        last = pe.matmul(banks[u][:, 0:D], pT[i][:, u, :], bv[i][:, u // NH, :], start=(i == 0), stop=(i == len(RC) - 1))
                    last.then_inc(o_made, 1)
                for u in range(U):
                    pe.wait_ge(o_out, u + 1)
                    for i, (a, b) in enumerate(CH):
                        last = pe.transpose(banks[u][0:b - a, i * P:(i + 1) * P], both[:, u, a:b], K["ident"][:])
                    last.then_inc(oT_made, 1)
                for u in range(U):
                    pe.wait_ge(oT_out0, u + 1)
                    pe.wait_ge(oT_out1, u + 1)
                    for i in range(2):
                        last = pe.matmul(banks[u][:, 0:D], oT[i][:, u, :], wo[i][:], start=(i == 0), stop=(i == 1))
                    last.then_inc(y_made, 1)

            @block.scalar
            def _(act):
                act.wait_ge(kip_made, 1)
                for i, (a, b) in enumerate(CH):
                    nc.scalar.copy(kip[i][:].rearrange("p b n -> p (b n)"), banks[i][0:b - a, 0:B * n]).then_inc(kip_out, 1)
                if layer:
                    nc.scalar.activation(root[:], K["n2"][:], ACT.Sqrt).then_inc(root_done, 1)
                    act.wait_ge(sq_made, 1)
                    nc.scalar.activation(ipn[:].rearrange("p b n -> p (b n)"), banks[6][:, 0:B * n], ACT.Sqrt).then_inc(root_done, 1)
                act.wait_ge(centred, 1)
                nc.scalar.activation(sc[:], sc[:], ACT.Exp).then_inc(exp_done, 1)
                for u in range(U):
                    act.wait_ge(pT_made, u + 1)
                    nc.scalar.copy(pT[0][:, u, :], banks[u][0:RC[0][1], 0:P]).then_inc(pT_out0, 1)
                    if len(RC) > 1:
                        nc.scalar.copy(pT[1][:, u, :], banks[u][0:RC[1][1] - P, P:2 * P]).then_inc(pT_out1, 1)
                for u in range(U):
                    act.wait_ge(oT_made, u + 1)
                    nc.scalar.copy(oT[0][:, u, :], banks[u][:, 0:P]).then_inc(oT_out0, 1)
                    nc.scalar.copy(oT[1][:, u, :], banks[u][0:D - P, P:2 * P]).then_inc(oT_out1, 1)

            @block.gpsimd
            def _(pool):
                pool.wait_ge(loaded, 16 * NLOAD)
                nc.gpsimd.tensor_tensor(base[:], K["xq"][:], bias[:].unsqueeze(1).to_broadcast([P, U, D]), ALU.add).then_inc(base_done, 1)

            @block.vector
            def _(dve):
                done = [0]

                def link(ins):
                    done[0] += 1
                    ins.then_inc(dve_step, 1)
                    dve.wait_ge(dve_step, done[0])

                vec = nc.vector
                for c in range(2):
                    last = vec.tensor_copy(ip_rep[:, c].rearrange("p b (h n) -> p b h n", n=n),
                                           K["ipT"][:, c, :, tok].unsqueeze(2).to_broadcast([P, B, H, n]))
                last.then_inc(rep_done, 1)
                if layer:
                    vec.tensor_tensor(sq[:], K["ipT"][:, :, :, tok], K["ipT"][:, :, :, tok], ALU.mult).then_inc(sq_done, 1)
                dve.wait_ge(loaded, 16 * NLOAD)
                dve.wait_ge(kip_out, 2)
                for i in range(2):
                    rows = CH[i][1] - CH[i][0]
                    vec.tensor_tensor(bk[i][:], kip[i][:].unsqueeze(2).to_broadcast([rows, B, H, n]),
                                      mask_k[i][:].rearrange("p (h n) -> p h n", n=n).unsqueeze(1).to_broadcast([rows, B, H, n]),
                                      ALU.mult).then_inc(bk_done, 1)
                for b in range(B):
                    dve.wait_ge(bv_made, b + 1)
                    for i, (r0, r1) in enumerate(RC):
                        last = vec.tensor_tensor(bv[i][:, b, :], banks[2 + b][0:r1 - r0, i * D:(i + 1) * D], mask_v[i][:], ALU.mult)
                    last.then_inc(bv_done, 1)

                res = K["res"]
                sums = res[:].rearrange("p g h (i v) -> p (g h) i v", i=2)[:, :, :, DH]
                if layer:
                    dve.wait_ge(root_done, 2)
                    link(vec.tensor_scalar(ipn[:], ipn[:], EPS, None, ALU.max))
                    link(vec.reciprocal(ipn[:], ipn[:]))
                    link(vec.tensor_scalar(ipn[:], ipn[:], SEM_SCALE, None, ALU.mult))
                    for b in range(B):
                        for h in range(NH):
                            g = slice(b, G, B)
                            last = vec.tensor_scalar(norm[:, g, h, :], root[:, g, h:4:NH], K["einv"][:, b:b + 1], None, ALU.mult)
                    link(last)
                    link(vec.scalar_tensor_tensor(out=norm[:].rearrange("p g h i -> p (g h) i"), in0=sums, scalar=EPS,
                                                  in1=norm[:].rearrange("p g h i -> p (g h) i"), op0=ALU.mult, op1=ALU.max))
                    link(vec.reciprocal(norm[:], norm[:]))
                    for u in range(U):
                        b, h = u // NH, u % NH
                        g = slice(b, G, B)
                        dots = res[:, g, h, :].rearrange("p g (i v) -> p g i v", i=2)[:, :, :, DH + 1:VW]
                        last = vec.tensor_tensor(extra[:, u].rearrange("p (g i) n -> p g i n", i=2), dots,
                                                 norm[:, g, h, :].unsqueeze(3).to_broadcast([P, PAIRS, 2, n]), ALU.mult)
                    link(last)
                    for b in range(B):
                        e = extra[:, NH * b:NH * (b + 1)].rearrange("p u h n -> p (u h) n")
                        last = vec.tensor_tensor(e, e, ipn[:, b].unsqueeze(1).to_broadcast([P, NH * H, n]), ALU.mult)
                    link(last)
                else:
                    for h in range(NH):
                        for c, (coord, at, op) in enumerate(((0, 0, ALU.is_le), (1, 1 + h, ALU.is_le), (2, 0, ALU.is_ge), (3, 1 + h, ALU.is_ge))):
                            last = vec.tensor_scalar(cond[:, c], boxes[:, :, :, coord], grid[:, at:at + 1], None, op)
                        link(last)
                        link(vec.tensor_tensor(cond[:, 0:2], cond[:, 0:2], cond[:, 2:4], ALU.mult))
                        link(vec.tensor_tensor(inside[:], cond[:, 0], cond[:, 1], ALU.mult))
                        vec.tensor_scalar(extra[:, h:U:NH, 0, 4:8], inside[:], -NEG, NEG, ALU.mult, ALU.add)
                        link(vec.tensor_reduce(covered[:], inside[:], AX.X, ALU.max))
                        link(vec.tensor_scalar(extra[:, h:U:NH, 0, 0:4], covered[:].unsqueeze(2).to_broadcast([P, B, 4]), NEG, None, ALU.mult))
                for u in range(U):
                    dve.wait_ge(sc_made, u + 1)
                    add = extra[:, u] if layer else extra[:, u].to_broadcast([P, H, n])
                    last = vec.scalar_tensor_tensor(out=sc[:, u].rearrange("p (h n) -> p h n", n=n),
                                                    in0=banks[u][:, 0:W].rearrange("p (h n) -> p h n", n=n), scalar=SCALE,
                                                    in1=add, op0=ALU.mult, op1=ALU.add)
                link(last)
                flat = sc[:].rearrange("p u (h n) -> p (u h) n", n=n)
                link(vec.tensor_reduce(smax[:], flat, AX.X, ALU.max))
                vec.tensor_tensor(flat, flat, smax[:].unsqueeze(2).to_broadcast([P, U * H, n]), ALU.subtract).then_inc(centred, 1)
                link(vec.reciprocal(rz[:].rearrange("p g h i -> p (g h) i"), sums))
                for u in range(U):
                    b, h = u // NH, u % NH
                    g = slice(b, G, B)
                    last = vec.tensor_tensor(text[:, u].rearrange("p (g i d) -> p g i d", i=2, d=DH),
                                             res[:, g, h, :].rearrange("p g (i v) -> p g i v", i=2)[:, :, :, 0:DH],
                                             rz[:, g, h, :].unsqueeze(3).to_broadcast([P, PAIRS, 2, DH]), ALU.mult)
                link(last)
                dve.wait_ge(exp_done, 1)
                link(vec.tensor_reduce(ssum[:], flat, AX.X, ALU.add))
                link(vec.reciprocal(ssum[:], ssum[:]))
                if layer:
                    s4 = ssum[:].rearrange("p (b h k) -> p b h k", b=B, h=NH)
                    link(vec.tensor_tensor(s4, s4, spat[:].unsqueeze(1).unsqueeze(3).to_broadcast([P, B, NH, H]), ALU.mult))
                vec.tensor_tensor(flat, flat, ssum[:].unsqueeze(2).to_broadcast([P, U * H, n]), ALU.mult).then_inc(prob_done, 1)
                for u in range(U):
                    dve.wait_ge(o_made, u + 1)
                    vec.tensor_tensor(both[:, u, :], banks[u][:, 0:D], text[:, u, :], ALU.add).then_inc(o_out, 1)
                dve.wait_ge(base_done, 1)
                for u in range(U):
                    dve.wait_ge(y_made, u + 1)
                    vec.tensor_tensor(K["xq"][:, u, :], banks[u][:, 0:D], base[:, u, :], ALU.add).then_inc(y_out, 1)


def kernel(**inputs):
    from concourse import bacc
    from concourse.bass_utils import run_bass_kernel_spmd

    nc = bacc.Bacc("TRN2", target_bir_lowering=False, num_devices=1)
    f = np.float32
    arrays, aps = {}, {}

    def give(name, a):
        a = np.ascontiguousarray(a)
        arrays[f"in_{name}"] = a
        aps[name] = nc.dram_tensor(f"in_{name}", a.shape, mybir.dt.from_np(a.dtype), kind="ExternalInput").ap()

    for name, a in inputs.items():
        give(name, a)
    fold = np.zeros((P, 2 * VW), f)
    for i in range(2):
        for odd in range(2):
            for v in range(VW):
                fold[32 * (2 * i + odd) + v, i * VW + v] = 1
    side = 16
    at = np.arange(S)
    gx, gy = (at % side).astype(f) / f(side - 1), (at // side).astype(f) / f(side - 1)
    grid = np.stack([gx[0:P], gy[0:P], gy[P:S]], axis=1)
    give("c_ident", np.eye(P, dtype=f))
    give("c_ones", np.ones((P, P), f))
    give("c_fold", fold)
    give("c_grid", grid)
    for l in range(2):
        row, col = np.arange(D)[:, None] // DH, np.arange(H * IP[l])[None] // IP[l]
        give(f"c_mask_k{l}", (row == col).astype(f))
        give(f"c_mask_v{l}", (row == col).astype(f).T)
    out = nc.dram_tensor("out_0", (B, S, D), F32, kind="ExternalOutput").ap()
    consts = {k[2:]: v for k, v in aps.items() if k.startswith("c_")}
    a = lambda names: [aps[names[0]], aps[names[1]]]
    w = dict(
        wq=a(("L0_xattn_w_q", "L1_xattn_W_q")), wk=a(("L0_xattn_w_k", "L1_xattn_W_k")),
        wv=a(("L0_xattn_w_v", "L1_xattn_W_v")), wk_ip=a(("L0_xattn_w_k_ip", "L1_xattn_W_k_ip")),
        wv_ip=a(("L0_xattn_w_v_ip", "L1_xattn_W_v_ip")), wo=a(("L0_xattn_w_out", "L1_xattn_W_out")),
        bo=a(("L0_xattn_b_out", "L1_xattn_b_out")),
    )
    build(nc, aps["x"], aps["ctx_2048"], aps["fside_Bx4x4_0"], aps["fside_S_0"], w, consts, out)
    r = run_bass_kernel_spmd(nc, [arrays], core_ids=[0])
    return r.results[0]["out_0"]
```

```python
from contextlib import ExitStack

import numpy as np
import concourse.bass as bass
from concourse import mybir

F32 = mybir.dt.float32
BF16 = mybir.dt.bfloat16
F16 = mybir.dt.float16
U32 = mybir.dt.uint32
ALU = mybir.AluOpType
ACT = mybir.ActivationFunctionType
AX = mybir.AxisListType

P = 128
B, S, D, C = 4, 256, 160, 256
H, DH = 20, 8
TOK = 1601
IP = (8, 4)
TXT = (TOK - IP[0], TOK - IP[1])
NT = (TOK + P - 1) // P
NPAD = NT * P
NK = 1600
PAIRS = H // 2
G = B * PAIRS
NH = S // P
U = B * NH
VW = (9, 13)
AT = 14
XW = AT + C + AT
RING = 4
KROWS = 96
Q_PART = (0, 0, 0, 1, 1, 2)
K_RUNS = ((0, 3), (3, 2), (5, 1))
SCALE = float(DH) ** -0.5
EPS = 1e-12
NEG = -10000.0
SEM_SCALE = 0.5
SHIFT = (0.0, 14 * float(np.log(2.0)) / SCALE)
KSEG = ((0, 0, 128, 0, 0), (1, 0, 32, 0, 16), (1, 32, 96, 1, 0), (2, 0, 64, 1, 12))


def build(nc, x, ctx_in, bbox, spatial, w, consts, out):
    top = ExitStack()
    with top:
        def sbuf(name, shape, dt, stack=top):
            return stack.enter_context(nc.sbuf_tensor(name, shape, dt))

        KS = [nc.dram_tensor(f"k_parts_{l}", [H, B, 3, DH, NK], BF16).ap() for l in range(2)]
        QS = [nc.dram_tensor(f"q_parts_{l}", [H, 6, DH, B, S], BF16).ap() for l in range(2)]
        VS = [nc.dram_tensor("v_cols_0", [PAIRS, B, P, NT * 2 * VW[0]], F32).ap(),
              nc.dram_tensor("v_cols_1", [PAIRS, B, P, 2 * NT * 2 * VW[1]], F16).ap()]

        ps_x = top.enter_context(nc.psum_tensor("ps_x", [P, 2, 512], F32))
        ps_y = top.enter_context(nc.psum_tensor("ps_y", [P, 2, 512], F32))
        ps_t = top.enter_context(nc.psum_tensor("ps_t", [P, 2, 512], F32))
        ps_v = top.enter_context(nc.psum_tensor("ps_v", [P, 512], F32))
        ps_n = top.enter_context(nc.psum_tensor("ps_n", [P, 512], F32))
        banks = [ps_x[:, 0], ps_x[:, 1], ps_y[:, 0], ps_y[:, 1], ps_t[:, 0], ps_t[:, 1], ps_v[:, :], ps_n[:, :]]

        K = dict(
            ident=sbuf("ident", [P, P], F32), identb=sbuf("identb", [P, P], BF16), fold=sbuf("fold", [P, 2 * VW[0]], F32),
            xq=sbuf("xq", [P, U, D], F32),
            qT0=sbuf("qT0", [P, U * P], F32), qT1=sbuf("qT1", [D - P, U * P], F32),
            ipT=sbuf("ipT", [P, 2, B, IP[0]], F32),
            eh=sbuf("eh", [P, B, NT, XW], F16), el=sbuf("el", [P, B, NT, XW], F16),
            inv=sbuf("inv", [P, 3, B], F32),
            res=sbuf("res", [P, G * NH * 2 * VW[1]], F32),
            n2=sbuf("n2", [P, G, 4], F32),
            kb=sbuf("kb", [P, RING, NPAD], BF16),
            qb=sbuf("qb", [P, RING, 2 * S], BF16),
        )
        prepare(nc, K, banks, ctx_in, x, w, consts, KS, VS)
        queries(nc, K, 0, banks, w["wq"][0], QS[0])
        attend(nc, K, 0, KS[0], QS[0], VS[0], ps_x, ps_y, ps_t, ps_v, ps_n)
        close(nc, K, 0, banks, w, consts, bbox, spatial, None)
        queries(nc, K, 1, banks, w["wq"][1], QS[1])
        attend(nc, K, 1, KS[1], QS[1], VS[1], ps_x, ps_y, ps_t, ps_v, ps_n)
        close(nc, K, 1, banks, w, consts, bbox, spatial, out)


CHUNK_AT = ({0: (1, 2), 2: (1, 3), 4: (1, 4), 5: (1, 5), 6: (1, 6), 8: (1, 7), 10: (2, 0), 12: (2, 1)},
            {0: (1, 1), 2: (1, 2), 3: (1, 3), 5: (1, 4), 6: (1, 5), 8: (1, 6), 9: (1, 7), 11: (2, 0)})


def result_of(K, layer):
    return K["res"][:, 0:G * NH * 2 * VW[layer]].rearrange("p (g h i v) -> p g h i v", g=G, h=NH, i=2)


def prepare(nc, K, banks, ctx_in, x, w, consts, KS, VS):
    with ExitStack() as st:
        def sbuf(name, shape, dt):
            return st.enter_context(nc.sbuf_tensor(name, shape, dt))

        def sem(name):
            return st.enter_context(nc.semaphore(name))

        LAST = TOK - P * (NT - 1)
        TR, KI, KC = (NT + 1) // 2, 12, 400
        e32 = sbuf("e32", [P, NT, C], F32)
        ctxT = sbuf("ctxT", [P, 2, NPAD], F32)
        kp = sbuf("kp", [P, 3, 3, NK], BF16)
        rem = sbuf("rem", [P, 2, KC], F32)
        vaug = sbuf("vaug", [P, PAIRS, NT, 2, VW[0]], F32)
        vcut = sbuf("vcut", [P, PAIRS, 2, NT, 2, VW[1]], F16)
        wk = sbuf("wk", [P, 2, 2 * D], F32)
        wv = sbuf("wv", [P, 2, 2 * D + IP[1]], F32)
        amax = sbuf("amax", [P, 4], F32)
        ebits = sbuf("ebits", [P, 2], U32)
        expo = sbuf("expo", [P, 3], F32)
        total = sbuf("total", [P, 3], F32)
        field = sbuf("field", [P, 2, 3], U32)
        scales = sbuf("scales", [P, 3], U32)
        const_in, weights_in, init = sem("const_in"), sem("weights_in"), sem("init")
        pool_init = sem("pool_init")
        ctx_loaded = sem("ctx_loaded")
        filled = [sem(f"filled_{n}") for n in range(8)]
        freed = [sem(f"freed_{n}") for n in range(8)]
        ip_done, k0_done, k1_done, k2_done = sem("ip_done"), sem("k0_done"), sem("k1_done"), sem("k2_done")
        v_sent, k_sent = sem("v_sent"), sem("k_sent")
        amax_done, amax_all, bits = sem("amax_done"), sem("amax_all"), sem("bits")
        vh_done = sem("vh_done")
        eh_done, el_done = sem("eh_done"), sem("el_done")

        def fills(b, n):
            return 4 * b + n // 8 + 1

        with nc.Block() as block:
            @block.sync
            def _(sp):
                sp.dma_start(K["ident"][:], consts["ident"]).then_inc(const_in, 16)
                sp.dma_start(K["fold"][:], consts["fold"]).then_inc(const_in, 16)
                sp.wait_ge(init, 1)

                def load(b):
                    src = ctx_in[b] if isinstance(b, int) else ctx_in[bass.ds(b, 1)].rearrange("a t c -> (a t) c")
                    sp.dma_start(e32[:, 0:NT - 1, :], src[0:P * (NT - 1)].rearrange("(t p) c -> p t c", p=P)).then_inc(ctx_loaded, 16)
                    sp.dma_start(e32[0:LAST, NT - 1, :], src[P * (NT - 1):TOK]).then_inc(ctx_loaded, 16)

                def send(b):
                    for m, r0, rows, l, h0 in KSEG:
                        sp.wait_ge(k2_done, KI * b + 4 * (m + 1))
                        sp.wait_ge(init, 1)
                        for part in range(3):
                            dst = KS[l][h0:h0 + rows // DH, bass.ds(b, 1), part]
                            sp.dma_start(dst, kp[r0:r0 + rows, m, part, :]).then_inc(k_sent, 16)
                    sp.wait_ge(freed[7], fills(b, 31))
                    sp.wait_ge(init, 1)
                    for l, v in ((0, vaug[:].rearrange("p g t i n -> p g (t i n)")), (1, vcut[:].rearrange("p g c t i n -> p g (c t i n)"))):
                        sp.dma_start(VS[l][:, bass.ds(b, 1)].rearrange("g b p n -> p b g n"), v).then_inc(v_sent, 16)

                load(0)
                for l in range(2):
                    sp.dma_start(wk[:, :, l * D:(l + 1) * D], w["wk"][l].rearrange("(c p) n -> p c n", p=P)).then_inc(weights_in, 16)
                    sp.dma_start(wv[:, :, l * D:(l + 1) * D], w["wv"][l].rearrange("(c p) n -> p c n", p=P)).then_inc(weights_in, 16)
                sp.dma_start(K["xq"][:], x.rearrange("b (h p) c -> p (b h) c", p=P)).then_inc(const_in, 16)

                def turn(b):
                    sp.wait_ge(el_done, 2 * b)
                    sp.wait_ge(freed[TR - 1], fills(b - 1, TR - 1))
                    sp.wait_ge(init, 1)
                    load(b)
                    send(b - 1)

                turn(1)
                with sp.Fori(2, B, 1) as b:
                    turn(b)
                send(B - 1)
                sp.wait_ge(const_in, 48)
                sp.wait_ge(k_sent, 16 * 3 * len(KSEG) * B)
                sp.wait_ge(v_sent, 16 * 2 * B)

            @block.tensor
            def _(pe):
                pe.wait_ge(const_in, 48)
                pe.wait_ge(weights_in, 64)

                def batch(b, first):
                    def bank(n):
                        if n >= 8 or not first:
                            pe.wait_ge(freed[n % 8], fills(b, n) - 1)
                        return banks[n % 8]

                    pe.wait_ge(ctx_loaded, 32 * (b + 1))
                    for n in range(TR):
                        ps = bank(n)
                        for t in range(2 * n, min(2 * n + 2, NT)):
                            for c in range(2):
                                at = ((t % 2) * 2 + c) * P
                                last = pe.transpose(ps[:, at:at + P], e32[:, t, c * P:(c + 1) * P], K["ident"][:])
                        last.then_inc(filled[n % 8], 1)
                    for n in range(TR):
                        pe.wait_ge(freed[n], fills(b, n))
                    for n in range(KI):
                        m, kc = n // 4, n % 4
                        rows = min(P, 2 * D - m * P)
                        ps = bank(TR + n)
                        for c in range(2):
                            last = pe.matmul(ps[0:rows, 0:KC], wk[:, c, m * P:m * P + rows],
                                             ctxT[:, c, kc * KC:(kc + 1) * KC], start=(c == 0), stop=(c == 1))
                        last.then_inc(filled[(TR + n) % 8], 1)
                    pe.wait_ge(ip_done, 2 * (b + 1))
                    for t in range(NT):
                        n = TR + KI + t
                        ps = bank(n)
                        for c in range(2):
                            last = pe.matmul(ps[:, 0:2 * D + IP[1]], ctxT[:, c, t * P:(t + 1) * P], wv[:, c, :],
                                             start=(c == 0), stop=(c == 1))
                        last.then_inc(filled[n % 8], 1)

                batch(0, True)
                with pe.Fori(1, B, 1) as b:
                    batch(b, False)

            def copy_transposed(eng, copy, b, n):
                nt = 2 if n < TR - 1 else 1
                eng.wait_ge(filled[n], fills(b, n))
                src = banks[n][:, 0:nt * 2 * P].rearrange("p (t c q) -> p c t q", t=nt, c=2)
                dst = ctxT[:, :, 2 * n * P:(2 * n + nt) * P].rearrange("p c (t q) -> p c t q", t=nt)
                copy(dst, src).then_inc(freed[n], 1)

            def context_part(part, rows, b, t0, t1):
                if isinstance(b, int):
                    return part[0:rows, b, t0:t1, AT:AT + C]
                return part[0:rows, bass.ds(b, 1), t0:t1, AT:AT + C].rearrange("p b t c -> p (b t) c")

            def v_pieces(n, t, rows):
                dots = banks[n % 8][0:rows, 2 * D:2 * D + IP[1]].unsqueeze(1).unsqueeze(1).to_broadcast([rows, PAIRS, 2, IP[1]])
                return ((1, [vcut[0:rows, :, c, t, :, 0:DH] for c in range(2)],
                         banks[n % 8][0:rows, D:2 * D].rearrange("p (g i d) -> p g i d", g=PAIRS, i=2)),
                        (2, [vcut[0:rows, :, c, t, :, DH + 1:VW[1]] for c in range(2)], dots))

            @block.scalar
            def _(act):
                def batch(b, first):
                    for n in (1, 3, 5):
                        copy_transposed(act, nc.scalar.copy, b, n)
                    if not first:
                        act.wait_ge(k_sent, 16 * 3 * len(KSEG) * b)
                    for n in range(KI):
                        m, kc = n // 4, n % 4
                        rows = min(P, 2 * D - m * P)
                        act.wait_ge(filled[(TR + n) % 8], fills(b, TR + n))
                        nc.scalar.copy(kp[0:rows, m, 0, kc * KC:(kc + 1) * KC], banks[(TR + n) % 8][0:rows, 0:KC]).then_inc(k0_done, 1)
                        if n == 3:
                            act.wait_ge(bits, 6 * (b + 1))
                            scale = scales[:, 0:1].bitcast(F32)
                            act.wait_ge(init, 3)
                            for t0, t1, rows in ((0, NT - 1, P), (NT - 1, NT, TXT[1] - P * (NT - 1))):
                                nc.scalar.activation(context_part(K["eh"], rows, b, t0, t1), e32[0:rows, t0:t1, :], ACT.Copy,
                                                     scale=scale[0:rows]).then_inc(eh_done, 1)
                    act.wait_ge(pool_init, 4)
                    if not first:
                        act.wait_ge(v_sent, 16 * 2 * b)
                    for t in range(NT):
                        n = TR + KI + t
                        act.wait_ge(filled[n % 8], fills(b, n))
                        rows = min(P, TXT[0] - t * P)
                        nc.scalar.copy(vaug[0:rows, :, t, :, 0:DH], banks[n % 8][0:rows, 0:D].rearrange("p (g i d) -> p g i d", g=PAIRS, i=2))
                        rows = min(P, TXT[1] - t * P)
                        for which, dst, src in v_pieces(n, t, rows):
                            last = nc.scalar.activation(dst[0], src, ACT.Copy, scale=scales[0:rows, which:which + 1].bitcast(F32))
                        last.then_inc(vh_done, 1)

                batch(0, True)
                with act.Fori(1, B, 1) as b:
                    batch(b, False)

            @block.gpsimd
            def _(pool):
                nc.gpsimd.memset(vaug[:], 0.0)
                nc.gpsimd.memset(vcut[:], 0.0).then_inc(pool_init, 1)
                pool.wait_ge(pool_init, 1)
                for l, ones in ((0, vaug[:, :, :, :, DH]), (1, vcut[:, :, 0, :, :, DH])):
                    rows = TXT[l] - P * (NT - 1)
                    nc.gpsimd.memset(ones[:, :, 0:NT - 1], 1.0)
                    last = nc.gpsimd.memset(ones[0:rows, :, NT - 1], 1.0)
                last.then_inc(pool_init, 3)
                pool.wait_ge(amax_done, 1)
                nc.gpsimd.partition_all_reduce(amax[:, 3:4], amax[:, 2:3], P, bass.bass_isa.ReduceOp.max).then_inc(amax_all, 1)

                def batch(b):
                    pool.wait_ge(amax_done, b + 2)
                    nc.gpsimd.partition_all_reduce(amax[:, 1:2], amax[:, 0:1], P, bass.bass_isa.ReduceOp.max).then_inc(amax_all, 1)

                batch(0)
                pool.wait_ge(amax_all, 2)
                nc.gpsimd.memset(K["qb"][:], 0.0)
                nc.gpsimd.memset(K["kb"][:, :, TXT[0]:NPAD], 0.0).then_inc(pool_init, 1)
                pool.wait_ge(pool_init, 5)
                nc.gpsimd.memset(K["kb"][KROWS:KROWS + 2, :, 0:TXT[0]], 1.0).then_inc(pool_init, 1)
                pool.wait_ge(pool_init, 6)
                for b in range(1, B):
                    batch(b)

            @block.vector
            def _(dve):
                nc.vector.memset(e32[64:P, NT - 1, :], 0.0).then_inc(init, 1)
                nc.vector.memset(K["eh"][:, :, NT - 1, :], 0.0).then_inc(init, 1)
                nc.vector.memset(K["el"][:, :, NT - 1, :], 0.0).then_inc(init, 1)
                nc.vector.memset(expo[:, 0:1], 118.0)
                dve.wait_ge(weights_in, 64)
                nc.vector.tensor_reduce(amax[:, 2:3], wv[:, :, D:2 * D], AX.XY, ALU.max, apply_absolute_value=True).then_inc(amax_done, 1)
                dve.wait_ge(init, 3)
                dve.wait_ge(const_in, 48)
                nc.vector.tensor_copy(K["identb"][:], K["ident"][:]).then_inc(init, 1)
                dve.wait_ge(init, 4)

                def batch(b, first):
                    for n in (0, 2, 4, 6):
                        copy_transposed(dve, nc.vector.tensor_copy, b, n)
                    dve.wait_ge(freed[6], fills(b, 6))
                    ipd = K["ipT"][:, :, b, :] if isinstance(b, int) else K["ipT"][:, :, bass.ds(b, 1), :].rearrange("p c b n -> p c (b n)")
                    nc.vector.tensor_copy(ipd, ctxT[:, :, TOK - IP[0]:TOK]).then_inc(ip_done, 1)
                    if not first:
                        dve.wait_ge(filled[7], fills(b, 31) - 4)
                    nc.vector.tensor_copy(wv[:, :, 2 * D:2 * D + IP[1]], ctxT[:, :, TOK - IP[1]:TOK]).then_inc(ip_done, 1)
                    nc.vector.tensor_reduce(amax[:, 0:1], e32[:], AX.XY, ALU.max, apply_absolute_value=True).then_inc(amax_done, 1)
                    for n in range(KI):
                        m, kc = n // 4, n % 4
                        rows = min(P, 2 * D - m * P)
                        k0 = kp[0:rows, m, 0, kc * KC:(kc + 1) * KC]
                        k1 = kp[0:rows, m, 1, kc * KC:(kc + 1) * KC]
                        k2 = kp[0:rows, m, 2, kc * KC:(kc + 1) * KC]
                        r = rem[0:rows, n % 2, :]
                        dve.wait_ge(k0_done, KI * b + n + 1)
                        nc.vector.tensor_tensor(r, banks[(TR + n) % 8][0:rows, 0:KC], k0, ALU.subtract).then_inc(freed[(TR + n) % 8], 1)
                        dve.wait_ge(freed[(TR + n) % 8], fills(b, TR + n))
                        nc.vector.tensor_copy(k1, r).then_inc(k1_done, 1)
                        dve.wait_ge(k1_done, KI * b + n + 1)
                        nc.vector.tensor_tensor(k2, r, k1, ALU.subtract).then_inc(k2_done, 1)
                        if n == 1:
                            dve.wait_ge(amax_all, b + 2)
                            if not first:
                                dve.wait_ge(el_done, 2 * b)
                                dve.wait_ge(freed[7], fills(b - 1, 31))
                            if first:
                                nc.vector.tensor_scalar(ebits[:, 0:1], amax[:, 3:4].bitcast(U32), 23, None, ALU.logical_shift_right)
                            nc.vector.tensor_scalar(ebits[:, 1:2], amax[:, 1:2].bitcast(U32), 23, None, ALU.logical_shift_right).then_inc(bits, 1)
                            dve.wait_ge(bits, 6 * b + 1)
                            nc.vector.tensor_scalar(expo[:, 1:3], ebits[:], 15, None, ALU.max).then_inc(bits, 1)
                            dve.wait_ge(bits, 6 * b + 2)
                            nc.vector.tensor_tensor(total[:], expo[:], expo[:, 2:3].to_broadcast([P, 3]), ALU.add).then_inc(bits, 1)
                            dve.wait_ge(bits, 6 * b + 3)
                            nc.vector.tensor_scalar(total[:], total[:], 133, 385, ALU.max, ALU.min).then_inc(bits, 1)
                            dve.wait_ge(bits, 6 * b + 4)
                            nc.vector.tensor_scalar(field[:, 0], total[:], -1, 386, ALU.mult, ALU.add)
                            nc.vector.tensor_scalar(field[:, 1], total[:], -132, None, ALU.add).then_inc(bits, 1)
                            dve.wait_ge(bits, 6 * b + 5)
                            inv = K["inv"][:, :, b:b + 1] if isinstance(b, int) else K["inv"][:, :, bass.ds(b, 1)]
                            nc.vector.tensor_scalar(inv.bitcast(U32), field[:, 1].unsqueeze(2), 23, None, ALU.logical_shift_left)
                            nc.vector.tensor_scalar(scales[:], field[:, 0], 23, None, ALU.logical_shift_left).then_inc(bits, 1)
                            dve.wait_ge(bits, 6 * b + 6)
                        if n in (5, 6):
                            t0, t1, rows = ((0, NT - 1, P), (NT - 1, NT, TXT[1] - P * (NT - 1)))[n - 5]
                            dve.wait_ge(eh_done, 2 * b + n - 4)
                            nc.vector.scalar_tensor_tensor(out=context_part(K["el"], rows, b, t0, t1), in0=e32[0:rows, t0:t1, :],
                                                           scalar=scales[0:rows, 0:1].bitcast(F32),
                                                           in1=context_part(K["eh"], rows, b, t0, t1), op0=ALU.mult, op1=ALU.subtract).then_inc(el_done, 1)
                    for t in range(NT):
                        n = TR + KI + t
                        rows = min(P, TXT[1] - t * P)
                        dve.wait_ge(vh_done, NT * b + t + 1)
                        for which, dst, src in v_pieces(n, t, rows):
                            for i in range(2):
                                last = nc.vector.scalar_tensor_tensor(out=dst[1][:, :, i], in0=src[:, :, i],
                                                                      scalar=scales[0:rows, which:which + 1].bitcast(F32),
                                                                      in1=dst[0][:, :, i], op0=ALU.mult, op1=ALU.subtract)
                        last.then_inc(freed[n % 8], 1)

                batch(0, True)
                with dve.Fori(1, B, 1) as b:
                    batch(b, False)


def queries(nc, K, layer, banks, wq, QS):
    with ExitStack() as st:
        def sbuf(name, shape, dt):
            return st.enter_context(nc.sbuf_tensor(f"{name}_{layer}", shape, dt))

        def sem(name):
            return st.enter_context(nc.semaphore(f"{name}_{layer}"))

        R1 = D - P
        xT0, xT1 = sbuf("xT0", [P, U * P], F32), sbuf("xT1", [R1, U * P], F32)
        w0, w1 = sbuf("wq0", [P, D], F32), sbuf("wq1", [R1, D], F32)
        parts = (sbuf("qp0", [P, 3, U * P], BF16), sbuf("qp1", [R1, 3, U * P], BF16))
        r = (sbuf("qr0", [P, U * P], F32), sbuf("qr1", [R1, U * P], F32))
        w_in, turned, xT_done, made, q_done = sem("w_in"), sem("turned"), sem("xT_done"), sem("made"), sem("q_done")
        cut = (sem("cut_0"), sem("cut_1"))
        sent = sem("sent")
        with nc.Block() as block:
            @block.sync
            def _(sp):
                sp.dma_start(w0[:], wq[0:P]).then_inc(w_in, 16)
                sp.dma_start(w1[:], wq[P:D]).then_inc(w_in, 16)
                for m in range(2):
                    sp.wait_ge(cut[m], 4)
                for m in range(2):
                    h0, nh = ((0, P // DH), (P // DH, R1 // DH))[m]
                    for j, part in enumerate(Q_PART):
                        dst = QS[h0:h0 + nh, j].rearrange("h d b q -> h d (b q)")
                        sp.dma_start(dst, parts[m][:, part, :]).then_inc(sent, 16)
                sp.wait_ge(sent, 16 * 12)

            @block.tensor
            def _(pe):
                for u in range(U):
                    pe.transpose(banks[u // 4][:, (u % 4) * P:(u % 4 + 1) * P], K["xq"][:, u, 0:P], K["ident"][:])
                    last = pe.transpose(banks[2 + u // 4][0:R1, (u % 4) * P:(u % 4 + 1) * P], K["xq"][:, u, P:D], K["ident"][:])
                last.then_inc(turned, 1)
                pe.wait_ge(w_in, 32)
                pe.wait_ge(xT_done, 4)
                for n in range(2):
                    for m, (c0, c1) in enumerate(((0, P), (P, D))):
                        ps = banks[4 + 2 * m + n][0:c1 - c0, :]
                        pe.matmul(ps, w0[:, c0:c1], xT0[:, n * 512:(n + 1) * 512], start=True, stop=False)
                        pe.matmul(ps, w1[:, c0:c1], xT1[:, n * 512:(n + 1) * 512], start=False, stop=True).then_inc(made, 1)

            @block.scalar
            def _(act):
                act.wait_ge(turned, 1)
                for n in range(2):
                    nc.scalar.copy(xT0[:, n * 512:(n + 1) * 512], banks[n]).then_inc(xT_done, 1)
                act.wait_ge(made, 4)
                for n in range(2):
                    nc.scalar.copy(K["qT0"][:, n * 512:(n + 1) * 512], banks[4 + n]).then_inc(q_done, 1)
                for n in range(2):
                    nc.scalar.copy(K["qT1"][:, n * 512:(n + 1) * 512], banks[6 + n][0:R1, :]).then_inc(q_done, 1)

            def cut_parts(eng, m, q):
                steps = cut[m]
                eng.tensor_copy(parts[m][:, 0], q).then_inc(steps, 1)
                eng.wait_ge(steps, 1)
                eng.tensor_tensor(r[m][:], q, parts[m][:, 0], ALU.subtract).then_inc(steps, 1)
                eng.wait_ge(steps, 2)
                eng.tensor_copy(parts[m][:, 1], r[m][:]).then_inc(steps, 1)
                eng.wait_ge(steps, 3)
                eng.tensor_tensor(parts[m][:, 2], r[m][:], parts[m][:, 1], ALU.subtract).then_inc(steps, 1)

            @block.vector
            def _(dve):
                dve.wait_ge(turned, 1)
                for n in range(2):
                    nc.vector.tensor_copy(xT1[:, n * 512:(n + 1) * 512], banks[2 + n][0:R1, :]).then_inc(xT_done, 1)
                dve.wait_ge(q_done, 2)
                cut_parts(nc.vector, 0, K["qT0"][:])
                dve.wait_ge(q_done, 4)
                cut_parts(nc.vector, 1, K["qT1"][:])


def attend(nc, K, layer, KS, QS, VS, ps_x, ps_y, ps_t, ps_v, ps_n):
    with ExitStack() as st:
        def sbuf(name, shape, dt):
            return st.enter_context(nc.sbuf_tensor(f"{name}_{layer}", shape, dt))

        def sem(name):
            return st.enter_context(nc.semaphore(f"{name}_{layer}"))

        NV = TXT[layer]
        CUT = ((NV + 1) // 2, NV // 2)
        kb, qb = K["kb"], K["qb"]
        cols = VW[layer]
        vb = sbuf("vb", [P, 2, 1 + layer, NT, 2, cols], F16 if layer else F32)
        pe32 = sbuf("pe32", [P, 2, NT, 2 * S], F32)
        if layer:
            ph = sbuf("ph", [P, 2, NT, 2 * S], F16)
            pl = sbuf("pl", [P, 2, NT, 2 * S], F16)
            junk = sbuf("junk", [P, 2, S], F32)
        else:
            acc = sbuf("acc", [P, 2, S], F32)
        mx = sbuf("mx", [P, 2, 8], F32)
        mm = sbuf("mm", [P, 2, 4], F32)
        mn = sbuf("mn", [P, 2, 4], F32)
        shift = sbuf("shift", [P, 4], F32)
        mp = sbuf("mp", [P, 2, 4, 2], BF16)
        ready = sem("ready")
        kq_loaded = [sem(f"kq_loaded_{n}") for n in range(RING)]
        v_loaded = [sem(f"v_loaded_{n}") for n in range(2)]
        chunk_made, chunk_max = sem("chunk_made"), sem("chunk_max")
        m1, m2, m3, m_parts = sem("m1"), sem("m2"), sem("m3"), sem("m_parts")
        m_turned, m_rows = sem("m_turned"), sem("m_rows")
        st_made, exp_done = sem("st_made"), sem("exp_done")
        if layer:
            half_done, low_done, norm_made, norm_out = sem("half_done"), sem("low_done"), sem("norm_made"), sem("norm_out")
            v_placed = sem("v_placed")
        else:
            acc_made, acc_out, turned, turned_out = sem("acc_made"), sem("acc_out"), sem("turned"), sem("turned_out")
        HALVES = (NT + 1) // 2

        USES = NT + (1 if layer else 2)

        def TILE_POS(t):
            return USES - 1 if t == NT - 1 else t + 1 if t > 2 and not layer else t

        def TURN(o, pos):
            return (o * USES + pos) % 2

        def at_least(eng, semaphore, value):
            if not isinstance(value, int) or value > 0:
                eng.wait_ge(semaphore, value)

        def uses(k, o, n):
            return (4 // n) * k + o // n + 1

        def steps(eng, step):
            for s in range(-2, 2):
                step(0, s)
            with eng.Fori(0, (G - 4) // 4, 1) as k:
                for o in range(2, 6):
                    step(k, o)
            for s in range(G - 2, G + 2):
                step(0, s)

        def has(k, o, d):
            return not isinstance(k, int) or 0 <= o + d < G

        with nc.Block() as block:
            @block.sync
            def _(sp):
                sp.wait_ge(ready, 2)

                def load(k, o):
                    s, n = 4 * k + o, o % RING
                    if not isinstance(s, int) or s >= RING:
                        sp.wait_ge(st_made, NT * (s - RING + 1))
                        sp.wait_ge(ready, 2)
                    for i in range(2):
                        for j, parts in K_RUNS:
                            src = KS[bass.ds(2 * (k + o // B) + i, 1), o % B, 0:parts, :, 0:NV].rearrange("h j d k -> (h j d) k")
                            r0 = 48 * i + DH * j
                            sp.dma_start(kb[r0:r0 + DH * parts, n, 0:NV], src).then_inc(kq_loaded[n], 16)
                        src = QS[bass.ds(2 * (k + o // B) + i, 1), :, :, o % B, :].rearrange("h j d q -> (h j d) q")
                        sp.dma_start(qb[48 * i:48 * i + 48, n, i * S:(i + 1) * S], src).then_inc(kq_loaded[n], 16)

                def load_v(k, o):
                    s = 4 * k + o
                    if not isinstance(s, int) or s >= 2:
                        sp.wait_ge(v_placed if layer else acc_made, s - 1)
                        sp.wait_ge(ready, 2)
                    src = VS[bass.ds(k + o // B, 1), o % B].rearrange("g p n -> (g p) n")
                    sp.dma_start(vb[:, o % 2].rearrange("p c t i n -> p (c t i n)"), src).then_inc(v_loaded[o % 2], 16)

                for s in range(RING):
                    load(0, s)
                    if s:
                        load_v(0, s - 1)
                with sp.Fori(1, G // 4, 1) as k:
                    for o in range(4):
                        load(k, o)
                        load_v(k, o - 1)
                load_v(0, G - 1)

            @block.tensor
            def _(pe):
                pe.wait_ge(ready, 2)

                def scores(k, o, c):
                    if not has(k, o, 1):
                        return
                    s, n = 4 * k + o + 1, (o + 1) % RING
                    hh, e = c // 2, c % 2
                    if c == 0:
                        pe.wait_ge(kq_loaded[n], 128 * uses(k, o + 1, RING))
                    at_least(pe, chunk_max, 8 * s + c - 1)
                    ps = (ps_x, ps_y)[c % 2]
                    k0, k1 = (0, CUT[0]) if e == 0 else (CUT[0], NV)
                    for a in range(k0, k1, 512):
                        z = min(a + 512, k1)
                        last = pe.matmul(ps[:, (a - k0) // 512, 0:z - a], qb[0:KROWS, n, hh * P:(hh + 1) * P],
                                         kb[0:KROWS, n, a:z], start=True, stop=True)
                    last.then_inc(chunk_made, 1)

                def turn_max(k, o):
                    if not has(k, o, 1):
                        return
                    s = 4 * k + o
                    pe.wait_ge(m_parts, s + 2)
                    if has(k, o, 0):
                        pe.wait_ge(exp_done, NT * s + NT - 2)
                    for hh in range(4):
                        last = pe.matmul(ps_t[KROWS:KROWS + 2, TURN(o, USES - 2), hh * P:(hh + 1) * P], mp[:, (o + 1) % 2, hh, :], K["identb"][:],
                                         start=True, stop=True)
                    last.then_inc(m_turned, 1)

                def turn_result(k, o):
                    if layer or not has(k, o, -2):
                        return
                    s = 4 * k + o
                    pe.wait_ge(acc_out, s - 1)
                    at_least(pe, exp_done, NT * s + 2 if has(k, o, 0) else NT * G)
                    for h in range(NH):
                        last = pe.matmul(ps_t[:, TURN(o, 3), 32 * h:32 * h + 2 * cols], acc[:, o % 2, h * P:(h + 1) * P], K["fold"][:],
                                         start=True, stop=True)
                    last.then_inc(turned, 1)

                def exponents(k, o, t):
                    if not has(k, o, 0):
                        return
                    s, n = 4 * k + o, o % RING
                    if t == 0:
                        pe.wait_ge(m_rows, s + 1)
                    if t == 4 and not layer and has(k, o, -2):
                        pe.wait_ge(turned_out, s - 1)
                    elif t:
                        at_least(pe, exp_done, NT * s + t - (0 if t == NT - 1 or t == 3 and not layer else 1))
                    pe.matmul(ps_t[:, TURN(o, TILE_POS(t)), :], kb[0:KROWS + 2, n, t * P:(t + 1) * P], qb[0:KROWS + 2, n, :],
                              start=True, stop=True).then_inc(st_made, 1)

                def products(k, o, tiles):
                    if layer or not has(k, o, -1):
                        return
                    s, n = 4 * k + o, (o - 1) % 2
                    if tiles[0] == 0:
                        at_least(pe, acc_out, s - 1)
                        pe.wait_ge(v_loaded[n], 16 * uses(k, o - 1, 2))
                    pe.wait_ge(exp_done, NT * (s - 1) + tiles[-1] + 1)
                    for i in range(2):
                        for t in tiles:
                            r0 = 32 * (2 * i + t % 2)
                            last = pe.matmul(ps_v[r0:r0 + cols, 0:S], vb[:, n, 0, t, i, :], pe32[:, n, t, i * S:(i + 1) * S],
                                             start=(t < 2), stop=(t >= NT - 2))
                    if tiles[-1] == NT - 1:
                        last.then_inc(acc_made, 1)

                def unit(k, o, q):
                    s, n = 4 * k + o, (o - 1) % 2
                    hh, t = q // NT, q % NT
                    if t == 0:
                        at_least(pe, norm_out, 4 * (s - 1) + hh - 1)
                    if hh == 0:
                        if t == 0:
                            pe.wait_ge(v_placed, s)
                        pe.wait_ge(low_done, HALVES * (s - 1) + t // 2 + 1)
                    b, c0 = (o - 1) % B, (1, AT)[hh // NH]
                    hi, lo = ph[:, n, t, hh * P:(hh + 1) * P], pl[:, n, t, hh * P:(hh + 1) * P]
                    eh, el = K["eh"][:, b, t, c0:c0 + cols + C], K["el"][:, b, t, c0:c0 + cols + C]
                    ps = (ps_v, ps_n)[hh % 2][:, 0:cols + C]
                    pe.matmul(ps, hi, eh, start=(t == 0), stop=False)
                    pe.matmul(ps, hi, el, start=False, stop=False)
                    last = pe.matmul(ps, lo, eh, start=False, stop=(t == NT - 1))
                    if t == NT - 1:
                        last.then_inc(norm_made, 1)

                def step(k, o):
                    for t in range(NT):
                        if t == NT - 1:
                            turn_max(k, o)
                        exponents(k, o, t)
                        if t == 2:
                            turn_result(k, o)
                        if t in CHUNK_AT[layer]:
                            d, c = CHUNK_AT[layer][t]
                            scores(k, o + d - 1, c)
                        if t % 2 == 1:
                            products(k, o, (t - 1, t))
                        elif t == NT - 1:
                            products(k, o, (t,))
                        if layer and has(k, o, -1):
                            for q in range(4 * t, 4 * t + 4):
                                unit(k, o, q)

                steps(pe, step)

            @block.scalar
            def _(act):
                def step(k, o):
                    s = 4 * k + o
                    def unit_out(d, hh):
                        if not layer or not has(k, o, d):
                            return
                        act.wait_ge(norm_made, 4 * (s + d) + hh + 1)
                        g = 4 * (s + d) + hh
                        i, h = hh // NH, hh % NH
                        ps = (ps_v, ps_n)[hh % 2]
                        v0, c0 = ((0, cols), (C, 0))[i]
                        dst = K["n2"][:].rearrange("p g h -> p (g h)")
                        dst = dst[:, g:g + 1] if isinstance(g, int) else dst[:, bass.ds(g, 1)]
                        if not isinstance(g, int) or g >= 2:
                            act.wait_ge(norm_out, g - 1)
                        nc.scalar.activation(junk[:, hh % 2, :], ps[:, c0:c0 + C], ACT.Square, accum_out=dst)
                        dst = result_of(K, 1)[:, s + d, h, i, :] if isinstance(s, int) else \
                            result_of(K, 1)[:, bass.ds(s + d, 1), h, i, :].rearrange("p g v -> p (g v)")
                        nc.scalar.copy(dst, ps[:, v0:v0 + cols]).then_inc(norm_out, 1)

                    unit_out(-2, 3)
                    if has(k, o, -2) and not layer:
                        act.wait_ge(acc_made, s - 1)
                        nc.scalar.copy(acc[:, o % 2, :], ps_v[:, 0:S]).then_inc(acc_out, 1)
                    for t in range(NT):
                        if t in (4, 7, 10):
                            unit_out(-1, t // 3 - 1)
                        if t == NT - 1 and has(k, o, 1):
                            act.wait_ge(m_turned, s + 2)
                            nc.scalar.copy(qb[KROWS:KROWS + 2, (o + 1) % RING, :], ps_t[KROWS:KROWS + 2, TURN(o, USES - 2), :]).then_inc(m_rows, 1)
                        if has(k, o, 0):
                            if t == 0 and (not isinstance(s, int) or s >= 2):
                                if not layer:
                                    act.wait_ge(acc_made, s - 1)
                                else:
                                    act.wait_ge(low_done, HALVES * (s - 1))
                                    act.wait_ge(norm_made, 4 * (s - 1))
                            act.wait_ge(st_made, NT * s + t + 1)
                            nc.scalar.activation(pe32[:, o % 2, t, :], ps_t[:, TURN(o, TILE_POS(t)), :], ACT.Exp, scale=SCALE).then_inc(exp_done, 1)
                            if layer and (t % 2 == 1 or t == NT - 1):
                                t0 = t - t % 2
                                act.wait_ge(exp_done, NT * s + t + 1)
                                nc.scalar.copy(ph[:, o % 2, t0:t + 1, :], pe32[:, o % 2, t0:t + 1, :]).then_inc(half_done, 1)
                        if t == 2 and not layer and has(k, o, -2):
                            act.wait_ge(turned, s - 1)
                            dst = result_of(K, 0).rearrange("p g h i v -> p g h (i v)")
                            dst = dst[:, s - 2] if isinstance(s, int) else dst[:, bass.ds(s - 2, 1)].rearrange("p g h n -> p (g h) n")
                            src = ps_t[:, TURN(o, 3), 0:32 * NH].rearrange("p (h n) -> p h n", h=NH)[:, :, 0:2 * cols]
                            nc.scalar.copy(dst, src).then_inc(turned_out, 1)

                steps(act, step)

            @block.gpsimd
            def _(pool):
                nc.gpsimd.memset(shift[:], SHIFT[layer]).then_inc(ready, 1)
                pool.wait_ge(ready, 2)

                def step(k, o):
                    if not has(k, o, 1):
                        return
                    s, n = 4 * k + o + 1, (o + 1) % 2
                    pool.wait_ge(m1, s + 1)
                    nc.gpsimd.tensor_tensor(mn[:, n], mm[:, n], shift[:], ALU.add).then_inc(m2, 1)
                    if not isinstance(s, int) or s >= 2:
                        pool.wait_ge(m_turned, s - 1)
                    nc.gpsimd.tensor_tensor(mp[:, n, :, 0], mm[:, n], shift[:], ALU.add).then_inc(m3, 1)
                    pool.wait_ge(m2, s + 1)
                    pool.wait_ge(m3, s + 1)
                    nc.gpsimd.tensor_tensor(mp[:, n, :, 1], mn[:, n], mp[:, n, :, 0], ALU.subtract).then_inc(m_parts, 1)

                steps(pool, step)

            @block.vector
            def _(dve):
                if layer:
                    nc.vector.memset(kb[KROWS:KROWS + 2, :, TXT[0]:NV], 1.0)
                nc.vector.memset(ps_v[:], 0.0).then_inc(ready, 1)

                def step(k, o):
                    s = 4 * k + o

                    def chunk(d, c):
                        if not has(k, o, d):
                            return
                        pair = s + d
                        if c == 0 and (not isinstance(s, int) or pair >= 2):
                            dve.wait_ge(m1, pair - 1)
                        dve.wait_ge(chunk_made, 8 * pair + c + 1)
                        w = CUT[c % 2]
                        src = (ps_x, ps_y)[c % 2][:].rearrange("p a b -> p (a b)")[:, 0:w]
                        nc.vector.tensor_reduce(mx[:, (o + d) % 2, c:c + 1], src, AX.X, ALU.max).then_inc(chunk_max, 1)
                        if c == 7:
                            dve.wait_ge(chunk_max, 8 * (pair + 1))
                            if not isinstance(s, int) or pair >= 1:
                                dve.wait_ge(m3, pair)
                            nc.vector.tensor_reduce(mm[:, (o + d) % 2], mx[:, (o + d) % 2].rearrange("p (h e) -> p h e", e=2),
                                                    AX.X, ALU.max, negate=True).then_inc(m1, 1)

                    def low(n):
                        if not layer or not has(k, o, 0):
                            return
                        t0, t1 = 2 * n, min(2 * n + 2, NT)
                        dve.wait_ge(half_done, HALVES * s + n + 1)
                        nc.vector.tensor_tensor(pl[:, o % 2, t0:t1, :], pe32[:, o % 2, t0:t1, :], ph[:, o % 2, t0:t1, :],
                                                ALU.subtract).then_inc(low_done, 1)

                    for t in range(NT):
                        if t == 4 and layer and has(k, o, 0):
                            dve.wait_ge(v_loaded[o % 2], 16 * uses(k, o, 2))
                            at_least(dve, norm_made, 4 * (s - 1))
                            for c, part in enumerate((K["eh"], K["el"])):
                                for i, c0 in enumerate((1, AT + C)):
                                    last = nc.vector.tensor_copy(part[:, o % B, :, c0:c0 + cols], vb[:, o % 2, c, :, i, :])
                            last.then_inc(v_placed, 1)
                        if t in CHUNK_AT[layer]:
                            chunk(*CHUNK_AT[layer][t])
                        if t % 2 == 0 and t:
                            low(t // 2 - 1)
                    low(HALVES - 1)

                steps(dve, step)


def close(nc, K, layer, banks, w, consts, bbox, spatial, out):
    with ExitStack() as st:
        def sbuf(name, shape, dt):
            return st.enter_context(nc.sbuf_tensor(f"{name}_{layer}", shape, dt))

        def sem(name):
            return st.enter_context(nc.semaphore(f"{name}_{layer}"))

        n = IP[layer]
        W = H * n
        CH = ((0, P), (P, D))
        RC = ((0, min(P, W)),) + (((P, W),) if W > P else ())
        tok = slice(IP[0] - n, IP[0])
        wki, wvi = sbuf("wki", [P, 2, D], F32), sbuf("wvi", [P, 2, D], F32)
        wo = (sbuf("wo0", [P, D], F32), sbuf("wo1", [D - P, D], F32))
        bias = sbuf("bias", [P, D], F32)
        mask_k = (sbuf("mask_k0", [P, W], F32), sbuf("mask_k1", [D - P, W], F32))
        mask_v = tuple(sbuf(f"mask_v{i}", [b - a, D], F32) for i, (a, b) in enumerate(RC))
        ip_rep = sbuf("ip_rep", [P, 2, B, W], F32)
        kip = (sbuf("kip0", [P, B, n], F32), sbuf("kip1", [D - P, B, n], F32))
        bk = (sbuf("bk0", [P, B, H, n], F32), sbuf("bk1", [D - P, B, H, n], F32))
        bv = tuple(sbuf(f"bv{i}", [b - a, B, D], F32) for i, (a, b) in enumerate(RC))
        extra = sbuf("extra", [P, U, H if layer else 1, n], F32)
        sc = sbuf("sc", [P, U, W], F32)
        smax, ssum = sbuf("smax", [P, U * H], F32), sbuf("ssum", [P, U * H], F32)
        pT = tuple(sbuf(f"pT{i}", [b - a, U, P], F32) for i, (a, b) in enumerate(RC))
        rz = sbuf("rz", [P, G, NH, 2], F32)
        text = sbuf("text", [P, U, D], F32)
        both = sbuf("both", [P, U, D], F32)
        oT = (sbuf("oT0", [P, U, P], F32), sbuf("oT1", [D - P, U, P], F32))
        base = sbuf("base", [P, U, D], F32)
        loaded = sem("loaded")
        NLOAD = 7 + len(RC) + (NH + 1 if layer else 2)
        rep_done, kip_made, kip_out, bk_done = sem("rep_done"), sem("kip_made"), sem("kip_out"), sem("bk_done")
        bv_made, bv_done = sem("bv_made"), sem("bv_done")
        sc_made = sem("sc_made")
        centred, exp_done, prob_done = sem("centred"), sem("exp_done"), sem("prob_done")
        pT_made, pT_out0, pT_out1 = sem("pT_made"), sem("pT_out0"), sem("pT_out1")
        o_made, o_out = sem("o_made"), sem("o_out")
        oT_made, oT_out0, oT_out1 = sem("oT_made"), sem("oT_out0"), sem("oT_out1")
        y_made, y_out, base_done = sem("y_made"), sem("y_out"), sem("base_done")
        dve_step = sem("dve_step")
        if layer:
            stored, root_done, sq_done, sq_made = sem("stored"), sem("root_done"), sem("sq_done"), sem("sq_made")
            norm = sbuf("norm", [P, G, NH, 2], F32)
            root = sbuf("root", [P, G, 4], F32)
            sq = sbuf("sq", [P, 2, B, n], F32)
            ones = sbuf("ones", [P, P], F32)
            ipn = sbuf("ipn", [P, B, n], F32)
            spat = sbuf("spat", [P, NH], F32)
        else:
            boxes = sbuf("boxes", [P, B, 4, 4], F32)
            grid = sbuf("grid", [P, 1 + NH], F32)
            cond = sbuf("cond", [P, 4, B, 4], F32)
            inside = sbuf("inside", [P, B, 4], F32)
            covered = sbuf("covered", [P, B], F32)

        with nc.Block() as block:
            @block.sync
            def _(sp):
                def load(dst, src):
                    sp.dma_start(dst, src).then_inc(loaded, 16)

                load(wki[:], w["wk_ip"][layer].rearrange("(c p) n -> p c n", p=P))
                load(wvi[:], w["wv_ip"][layer].rearrange("(c p) n -> p c n", p=P))
                load(wo[0][:], w["wo"][layer][0:P])
                load(wo[1][:], w["wo"][layer][P:D])
                load(bias[:], w["bo"][layer].partition_broadcast(P))
                load(mask_k[0][:], consts[f"mask_k{layer}"][0:P])
                load(mask_k[1][:], consts[f"mask_k{layer}"][P:D])
                for i, (a, b) in enumerate(RC):
                    load(mask_v[i][:], consts[f"mask_v{layer}"][a:b])
                if layer:
                    for h in range(NH):
                        load(spat[:, h:h + 1], spatial[h * P:(h + 1) * P].rearrange("(p o) -> p o", o=1))
                    load(ones[:], consts["ones"])
                else:
                    load(boxes[:].rearrange("p b m c -> p (b m c)"), bbox.rearrange("b m c -> (b m c)").partition_broadcast(P))
                    load(grid[:], consts["grid"])
                if out is not None:
                    for u in range(U):
                        sp.wait_ge(y_out, u + 1)
                        b, h = u // NH, u % NH
                        sp.dma_start(out[b, h * P:(h + 1) * P, :], K["xq"][:, u, :]).then_inc(stored, 16)
                    sp.wait_ge(stored, 16 * U)

            @block.tensor
            def _(pe):
                pe.wait_ge(loaded, 16 * NLOAD)
                for i, (a, b) in enumerate(CH):
                    for c in range(2):
                        last = pe.matmul(banks[i][0:b - a, 0:B * n], wki[:, c, a:b], K["ipT"][:, c, :, tok],
                                         start=(c == 0), stop=(c == 1))
                last.then_inc(kip_made, 1)
                pe.wait_ge(rep_done, 1)
                for b in range(B):
                    for i, (r0, r1) in enumerate(RC):
                        for c in range(2):
                            last = pe.matmul(banks[2 + b][0:r1 - r0, i * D:(i + 1) * D], ip_rep[:, c, b, r0:r1], wvi[:, c, :],
                                             start=(c == 0), stop=(c == 1))
                    last.then_inc(bv_made, 1)
                if layer:
                    pe.wait_ge(sq_done, 1)
                    for c in range(2):
                        last = pe.matmul(banks[6][:, 0:B * n], ones[:], sq[:, c], start=(c == 0), stop=(c == 1))
                    last.then_inc(sq_made, 1)
                    pe.wait_ge(root_done, 2)
                pe.wait_ge(bk_done, 2)
                pe.wait_ge(bv_done, B)
                for u in range(U):
                    b = u // NH
                    for i in range(2):
                        q = K[f"qT{i}"]
                        last = pe.matmul(banks[u][:, 0:W], q[:, u * P:(u + 1) * P], bk[i][:, b].rearrange("p h n -> p (h n)"),
                                         start=(i == 0), stop=(i == 1))
                    last.then_inc(sc_made, 1)
                pe.wait_ge(prob_done, 1)
                for u in range(U):
                    for i, (r0, r1) in enumerate(RC):
                        last = pe.transpose(banks[u][0:r1 - r0, i * P:(i + 1) * P], sc[:, u, r0:r1], K["ident"][:])
                    last.then_inc(pT_made, 1)
                for u in range(U):
                    pe.wait_ge(pT_out0, u + 1)
                    if len(RC) > 1:
                        pe.wait_ge(pT_out1, u + 1)
                    for i in range(len(RC)):
                        last = pe.matmul(banks[u][:, 0:D], pT[i][:, u, :], bv[i][:, u // NH, :], start=(i == 0), stop=(i == len(RC) - 1))
                    last.then_inc(o_made, 1)
                for u in range(U):
                    pe.wait_ge(o_out, u + 1)
                    for i, (a, b) in enumerate(CH):
                        last = pe.transpose(banks[u][0:b - a, i * P:(i + 1) * P], both[:, u, a:b], K["ident"][:])
                    last.then_inc(oT_made, 1)
                for u in range(U):
                    pe.wait_ge(oT_out0, u + 1)
                    pe.wait_ge(oT_out1, u + 1)
                    for i in range(2):
                        last = pe.matmul(banks[u][:, 0:D], oT[i][:, u, :], wo[i][:], start=(i == 0), stop=(i == 1))
                    last.then_inc(y_made, 1)

            @block.scalar
            def _(act):
                act.wait_ge(kip_made, 1)
                for i, (a, b) in enumerate(CH):
                    nc.scalar.copy(kip[i][:].rearrange("p b n -> p (b n)"), banks[i][0:b - a, 0:B * n]).then_inc(kip_out, 1)
                if layer:
                    nc.scalar.activation(root[:], K["n2"][:], ACT.Sqrt).then_inc(root_done, 1)
                    act.wait_ge(sq_made, 1)
                    nc.scalar.activation(ipn[:].rearrange("p b n -> p (b n)"), banks[6][:, 0:B * n], ACT.Sqrt).then_inc(root_done, 1)
                act.wait_ge(centred, 1)
                nc.scalar.activation(sc[:], sc[:], ACT.Exp).then_inc(exp_done, 1)
                for u in range(U):
                    act.wait_ge(pT_made, u + 1)
                    nc.scalar.copy(pT[0][:, u, :], banks[u][0:RC[0][1], 0:P]).then_inc(pT_out0, 1)
                    if len(RC) > 1:
                        nc.scalar.copy(pT[1][:, u, :], banks[u][0:RC[1][1] - P, P:2 * P]).then_inc(pT_out1, 1)
                for u in range(U):
                    act.wait_ge(oT_made, u + 1)
                    nc.scalar.copy(oT[0][:, u, :], banks[u][:, 0:P]).then_inc(oT_out0, 1)
                    nc.scalar.copy(oT[1][:, u, :], banks[u][0:D - P, P:2 * P]).then_inc(oT_out1, 1)

            @block.gpsimd
            def _(pool):
                pool.wait_ge(loaded, 16 * NLOAD)
                nc.gpsimd.tensor_tensor(base[:], K["xq"][:], bias[:].unsqueeze(1).to_broadcast([P, U, D]), ALU.add).then_inc(base_done, 1)

            @block.vector
            def _(dve):
                done = [0]

                def link(ins):
                    done[0] += 1
                    ins.then_inc(dve_step, 1)
                    dve.wait_ge(dve_step, done[0])

                vec = nc.vector
                for c in range(2):
                    last = vec.tensor_copy(ip_rep[:, c].rearrange("p b (h n) -> p b h n", n=n),
                                           K["ipT"][:, c, :, tok].unsqueeze(2).to_broadcast([P, B, H, n]))
                last.then_inc(rep_done, 1)
                if layer:
                    vec.tensor_tensor(sq[:], K["ipT"][:, :, :, tok], K["ipT"][:, :, :, tok], ALU.mult).then_inc(sq_done, 1)
                dve.wait_ge(loaded, 16 * NLOAD)
                dve.wait_ge(kip_out, 2)
                for i in range(2):
                    rows = CH[i][1] - CH[i][0]
                    vec.tensor_tensor(bk[i][:], kip[i][:].unsqueeze(2).to_broadcast([rows, B, H, n]),
                                      mask_k[i][:].rearrange("p (h n) -> p h n", n=n).unsqueeze(1).to_broadcast([rows, B, H, n]),
                                      ALU.mult).then_inc(bk_done, 1)
                for b in range(B):
                    dve.wait_ge(bv_made, b + 1)
                    for i, (r0, r1) in enumerate(RC):
                        last = vec.tensor_tensor(bv[i][:, b, :], banks[2 + b][0:r1 - r0, i * D:(i + 1) * D], mask_v[i][:], ALU.mult)
                    last.then_inc(bv_done, 1)

                res = result_of(K, layer)
                sums = res.rearrange("p g h i v -> p (g h) i v")[:, :, :, DH]
                if layer:
                    dve.wait_ge(root_done, 2)
                    link(vec.tensor_scalar(ipn[:], ipn[:], EPS, None, ALU.max))
                    link(vec.reciprocal(ipn[:], ipn[:]))
                    for b in range(B):
                        last = vec.tensor_scalar(ipn[:, b], ipn[:, b], K["inv"][:, 2, b:b + 1], SEM_SCALE, ALU.mult, ALU.mult)
                    link(last)
                    for b in range(B):
                        for h in range(NH):
                            g = slice(b, G, B)
                            last = vec.tensor_scalar(norm[:, g, h, :], root[:, g, h:4:NH], K["inv"][:, 0, b:b + 1], None, ALU.mult)
                    link(last)
                    link(vec.scalar_tensor_tensor(out=norm[:].rearrange("p g h i -> p (g h) i"), in0=sums, scalar=EPS,
                                                  in1=norm[:].rearrange("p g h i -> p (g h) i"), op0=ALU.mult, op1=ALU.max))
                    link(vec.reciprocal(norm[:], norm[:]))
                    for u in range(U):
                        b, h = u // NH, u % NH
                        g = slice(b, G, B)
                        dots = res[:, g, h, :, DH + 1:VW[1]]
                        last = vec.tensor_tensor(extra[:, u].rearrange("p (g i) n -> p g i n", i=2), dots,
                                                 norm[:, g, h, :].unsqueeze(3).to_broadcast([P, PAIRS, 2, n]), ALU.mult)
                    link(last)
                    for b in range(B):
                        e = extra[:, NH * b:NH * (b + 1)].rearrange("p u h n -> p (u h) n")
                        last = vec.tensor_tensor(e, e, ipn[:, b].unsqueeze(1).to_broadcast([P, NH * H, n]), ALU.mult)
                    link(last)
                else:
                    for h in range(NH):
                        for c, (coord, at, op) in enumerate(((0, 0, ALU.is_le), (1, 1 + h, ALU.is_le), (2, 0, ALU.is_ge), (3, 1 + h, ALU.is_ge))):
                            last = vec.tensor_scalar(cond[:, c], boxes[:, :, :, coord], grid[:, at:at + 1], None, op)
                        link(last)
                        link(vec.tensor_tensor(cond[:, 0:2], cond[:, 0:2], cond[:, 2:4], ALU.mult))
                        link(vec.tensor_tensor(inside[:], cond[:, 0], cond[:, 1], ALU.mult))
                        vec.tensor_scalar(extra[:, h:U:NH, 0, 4:8], inside[:], -NEG, NEG, ALU.mult, ALU.add)
                        link(vec.tensor_reduce(covered[:], inside[:], AX.X, ALU.max))
                        link(vec.tensor_scalar(extra[:, h:U:NH, 0, 0:4], covered[:].unsqueeze(2).to_broadcast([P, B, 4]), NEG, None, ALU.mult))
                for u in range(U):
                    dve.wait_ge(sc_made, u + 1)
                    add = extra[:, u] if layer else extra[:, u].to_broadcast([P, H, n])
                    last = vec.scalar_tensor_tensor(out=sc[:, u].rearrange("p (h n) -> p h n", n=n),
                                                    in0=banks[u][:, 0:W].rearrange("p (h n) -> p h n", n=n), scalar=SCALE,
                                                    in1=add, op0=ALU.mult, op1=ALU.add)
                link(last)
                flat = sc[:].rearrange("p u (h n) -> p (u h) n", n=n)
                link(vec.tensor_reduce(smax[:], flat, AX.X, ALU.max))
                vec.tensor_tensor(flat, flat, smax[:].unsqueeze(2).to_broadcast([P, U * H, n]), ALU.subtract).then_inc(centred, 1)
                link(vec.reciprocal(rz[:].rearrange("p g h i -> p (g h) i"), sums))
                if layer:
                    for b in range(B):
                        last = vec.tensor_scalar(rz[:, b:G:B], rz[:, b:G:B], K["inv"][:, 1, b:b + 1], None, ALU.mult)
                    link(last)
                for u in range(U):
                    b, h = u // NH, u % NH
                    g = slice(b, G, B)
                    last = vec.tensor_tensor(text[:, u].rearrange("p (g i d) -> p g i d", i=2, d=DH),
                                             res[:, g, h, :, 0:DH],
                                             rz[:, g, h, :].unsqueeze(3).to_broadcast([P, PAIRS, 2, DH]), ALU.mult)
                link(last)
                dve.wait_ge(exp_done, 1)
                link(vec.tensor_reduce(ssum[:], flat, AX.X, ALU.add))
                link(vec.reciprocal(ssum[:], ssum[:]))
                if layer:
                    s4 = ssum[:].rearrange("p (b h k) -> p b h k", b=B, h=NH)
                    link(vec.tensor_tensor(s4, s4, spat[:].unsqueeze(1).unsqueeze(3).to_broadcast([P, B, NH, H]), ALU.mult))
                vec.tensor_tensor(flat, flat, ssum[:].unsqueeze(2).to_broadcast([P, U * H, n]), ALU.mult).then_inc(prob_done, 1)
                for u in range(U):
                    dve.wait_ge(o_made, u + 1)
                    vec.tensor_tensor(both[:, u, :], banks[u][:, 0:D], text[:, u, :], ALU.add).then_inc(o_out, 1)
                dve.wait_ge(base_done, 1)
                for u in range(U):
                    dve.wait_ge(y_made, u + 1)
                    vec.tensor_tensor(K["xq"][:, u, :], banks[u][:, 0:D], base[:, u, :], ALU.add).then_inc(y_out, 1)


def kernel(**inputs):
    from concourse import bacc
    from concourse.bass_utils import run_bass_kernel_spmd

    nc = bacc.Bacc("TRN2", target_bir_lowering=False, num_devices=1)
    f = np.float32
    arrays, aps = {}, {}

    def give(name, a):
        a = np.ascontiguousarray(a)
        arrays[f"in_{name}"] = a
        aps[name] = nc.dram_tensor(f"in_{name}", a.shape, mybir.dt.from_np(a.dtype), kind="ExternalInput").ap()

    for name, a in inputs.items():
        give(name, a)
    fold = np.zeros((P, 2 * VW[0]), f)
    for i in range(2):
        for odd in range(2):
            for v in range(VW[0]):
                fold[32 * (2 * i + odd) + v, i * VW[0] + v] = 1
    side = 16
    at = np.arange(S)
    gx, gy = (at % side).astype(f) / f(side - 1), (at // side).astype(f) / f(side - 1)
    grid = np.stack([gx[0:P], gy[0:P], gy[P:S]], axis=1)
    give("c_ident", np.eye(P, dtype=f))
    give("c_ones", np.ones((P, P), f))
    give("c_fold", fold)
    give("c_grid", grid)
    for l in range(2):
        row, col = np.arange(D)[:, None] // DH, np.arange(H * IP[l])[None] // IP[l]
        give(f"c_mask_k{l}", (row == col).astype(f))
        give(f"c_mask_v{l}", (row == col).astype(f).T)
    out = nc.dram_tensor("out_0", (B, S, D), F32, kind="ExternalOutput").ap()
    consts = {k[2:]: v for k, v in aps.items() if k.startswith("c_")}
    a = lambda names: [aps[names[0]], aps[names[1]]]
    w = dict(
        wq=a(("L0_xattn_w_q", "L1_xattn_W_q")), wk=a(("L0_xattn_w_k", "L1_xattn_W_k")),
        wv=a(("L0_xattn_w_v", "L1_xattn_W_v")), wk_ip=a(("L0_xattn_w_k_ip", "L1_xattn_W_k_ip")),
        wv_ip=a(("L0_xattn_w_v_ip", "L1_xattn_W_v_ip")), wo=a(("L0_xattn_w_out", "L1_xattn_W_out")),
        bo=a(("L0_xattn_b_out", "L1_xattn_b_out")),
    )
    build(nc, aps["x"], aps["ctx_2048"], aps["fside_Bx4x4_0"], aps["fside_S_0"], w, consts, out)
    r = run_bass_kernel_spmd(nc, [arrays], core_ids=[0])
    return r.results[0]["out_0"]
```

```python
from contextlib import ExitStack

import numpy as np
import concourse.bass as bass
from concourse import mybir

F32 = mybir.dt.float32
BF16 = mybir.dt.bfloat16
F16 = mybir.dt.float16
U32 = mybir.dt.uint32
ALU = mybir.AluOpType
ACT = mybir.ActivationFunctionType
AX = mybir.AxisListType

P = 128
B, S, D, C = 4, 256, 160, 256
H, DH = 20, 8
TOK = 1601
IP = (8, 4)
TXT = (TOK - IP[0], TOK - IP[1])
NT = (TOK + P - 1) // P
NPAD = NT * P
NK = 1600
PAIRS = H // 2
G = B * PAIRS
NH = S // P
U = B * NH
VW = (9, 13)
AT = 14
XW = AT + C + AT
RING = 4
KROWS = 96
Q_PART = (0, 0, 0, 1, 1, 2)
K_RUNS = ((0, 3), (3, 2), (5, 1))
SCALE = float(DH) ** -0.5
EPS = 1e-12
NEG = -10000.0
SEM_SCALE = 0.5
SHIFT = (0.0, 14 * float(np.log(2.0)) / SCALE)
KSEG = ((0, 0, 128, 0, 0), (1, 0, 32, 0, 16), (1, 32, 96, 1, 0))
KREST = 2 * D - 2 * P


def build(nc, x, ctx_in, bbox, spatial, w, consts, out):
    top = ExitStack()
    with top:
        def sbuf(name, shape, dt, stack=top):
            return stack.enter_context(nc.sbuf_tensor(name, shape, dt))

        KS = [nc.dram_tensor(f"k_parts_{l}", [H, B, 3, DH, NK], BF16).ap() for l in range(2)]
        QS = [nc.dram_tensor(f"q_parts_{l}", [H, 6, DH, B, S], BF16).ap() for l in range(2)]
        VS = [nc.dram_tensor("v_cols_0", [PAIRS, B, P, NT, 2 * VW[0]], F32).ap(),
              nc.dram_tensor("v_cols_1", [PAIRS, B, P, 2 * NT * 2 * VW[1]], F16).ap()]

        ps_x = top.enter_context(nc.psum_tensor("ps_x", [P, 2, 512], F32))
        ps_y = top.enter_context(nc.psum_tensor("ps_y", [P, 2, 512], F32))
        ps_t = top.enter_context(nc.psum_tensor("ps_t", [P, 2, 512], F32))
        ps_v = top.enter_context(nc.psum_tensor("ps_v", [P, 512], F32))
        ps_n = top.enter_context(nc.psum_tensor("ps_n", [P, 512], F32))
        banks = [ps_x[:, 0], ps_x[:, 1], ps_y[:, 0], ps_y[:, 1], ps_t[:, 0], ps_t[:, 1], ps_v[:, :], ps_n[:, :]]

        K = dict(
            ident=sbuf("ident", [P, P], F32), identb=sbuf("identb", [P, P], BF16), fold=sbuf("fold", [P, 2 * VW[0]], F32),
            xq=sbuf("xq", [P, U, D], F32),
            ipT=sbuf("ipT", [P, 2, B, IP[0]], F32),
            eh=sbuf("eh", [P, B, NT, XW], F16), el=sbuf("el", [P, B, NT, XW], F16),
            inv=sbuf("inv", [P, 3, B], F32),
            res=sbuf("res", [P, G * NH * 2 * VW[1]], F32),
            n2=sbuf("n2", [P, G, 4], F32),
            kb=sbuf("kb", [P, RING, NPAD], BF16),
            qb=sbuf("qb", [P, RING, 2 * S], BF16),
        )
        for layer in range(2):
            with ExitStack() as st:
                n = IP[layer]
                L = dict(
                    parts=(sbuf(f"qp0_{layer}", [P, 3, U * P], BF16, st), sbuf(f"qp1_{layer}", [D - P, 3, U * P], BF16, st)),
                    kq_loaded=[st.enter_context(nc.semaphore(f"kq_loaded_{m}_{layer}")) for m in range(RING)],
                    sent=[st.enter_context(nc.semaphore(f"sent_{m}_{layer}")) for m in range(2)],
                    wo=(sbuf(f"wo0_{layer}", [P, D], F32, st), sbuf(f"wo1_{layer}", [D - P, D], F32, st)),
                    bv=tuple(sbuf(f"bv{i}_{layer}", [b - a, B, D], F32, st) for i, (a, b) in enumerate(token_rows(layer))),
                    sc=sbuf(f"sc_{layer}", [P, U, H * n], F32, st),
                    base=sbuf(f"base_{layer}", [P, U, D], F32, st),
                )
                if layer:
                    L.update(token_sq=sbuf("token_sq", [P, B, n], F32, st),
                             spat=sbuf("spat", [P, NH], F32, st))
                if not layer:
                    L.update(mask=sbuf("mask", [P, U, 1, n], F32, st), vaug=sbuf("vaug", [P, PAIRS, NT, 2, VW[0]], F32, st),
                             vcut=sbuf("vcut", [P, PAIRS, 2, NT, 2, VW[1]], F16, st),
                             v1_sent=st.enter_context(nc.semaphore("v1_sent")), v_sent=st.enter_context(nc.semaphore("v_sent")))
                    with ExitStack() as first:
                        e32 = sbuf("e32", [P, NT, C], F32, first)
                        ctx_loaded = first.enter_context(nc.semaphore("ctx_loaded"))
                        queries(nc, K, L, 0, banks, w, consts, KS[0], QS[0], (x, ctx_in, e32, ctx_loaded, bbox))
                        prepare(nc, K, L, banks, ctx_in, w, e32, ctx_loaded, KS, QS, VS)
                else:
                    queries(nc, K, L, 1, banks, w, consts, KS[1], QS[1], None, spatial)
                attend(nc, K, L, layer, KS[layer], QS[layer], VS, ps_x, ps_y, ps_t, ps_v, ps_n)
                close(nc, K, L, layer, banks, out if layer else None)


def token_rows(layer):
    W = H * IP[layer]
    return ((0, min(P, W)),) + (((P, W),) if W > P else ())


CHUNK_AT = ({0: (1, 3), 2: (1, 4), 3: (1, 5), 5: (1, 6), 7: (1, 7), 8: (2, 0), 10: (2, 1), 11: (2, 2)},
            {0: (1, 1), 2: (1, 2), 3: (1, 3), 5: (1, 4), 6: (1, 5), 8: (1, 6), 9: (1, 7), 11: (2, 0)})

PRODUCTS_AT = {1: (0, 1), 2: (2, 3), 4: (4, 5), 7: (6, 7), 9: (8, 9), 10: (10, 11), 12: (12,)}


def send_cut_v(sp, VS, L, b):
    sp.dma_start(VS[1][:, bass.ds(b, 1)].rearrange("g b p n -> p b g n"), L["vcut"][:].rearrange("p g c t i n -> p g (c t i n)")).then_inc(L["v1_sent"], 16)


def load_pair(sp, K, L, layer, KS, QS, k, o, first=False):
    n = o % RING
    loaded = L["kq_loaded"][n]
    for i in range(2):
        for j, parts in K_RUNS:
            src = KS[bass.ds(2 * (k + o // B) + i, 1), o % B, 0:parts, :, 0:TXT[layer]].rearrange("h j d k -> (h j d) k")
            r0 = 48 * i + DH * j
            sp.dma_start(K["kb"][r0:r0 + DH * parts, n, 0:TXT[layer]], src).then_inc(loaded, 16)
    if first:
        sp.wait_ge(L["sent"][0], 16 * 6)
    for i in range(2):
        src = QS[bass.ds(2 * (k + o // B) + i, 1), :, :, o % B, :].rearrange("h j d q -> (h j d) q")
        sp.dma_start(K["qb"][48 * i:48 * i + 48, n, i * S:(i + 1) * S], src).then_inc(loaded, 16)


def result_of(K, layer):
    return K["res"][:, 0:G * NH * 2 * VW[layer]].rearrange("p (g h i v) -> p g h i v", g=G, h=NH, i=2)


def prepare(nc, K, L, banks, ctx_in, w, e32, ctx_loaded, KS, QS, VS):
    with ExitStack() as st:
        def sbuf(name, shape, dt):
            return st.enter_context(nc.sbuf_tensor(name, shape, dt))

        def sem(name):
            return st.enter_context(nc.semaphore(name))

        LAST = TOK - P * (NT - 1)
        TR, KI, KC = (NT + 1) // 2, 10, 400
        SENDS = 3 * (len(KSEG) + 2)
        ctxT = sbuf("ctxT", [P, 2, NPAD], F32)
        kp = sbuf("kp", [P, 3, 3, NK], BF16)
        vaug, vcut, v_sent = L["vaug"], L["vcut"], L["v_sent"]
        RR = 4
        rem = K["res"][:, 0:RR * KC].rearrange("p (r k) -> p r k", r=RR)
        wk = sbuf("wk", [P, 2, 2 * D], F32)
        wv = sbuf("wv", [P, 2, 2 * D + IP[1]], F32)
        amax = sbuf("amax", [P, 4], F32)
        ebits = sbuf("ebits", [P, 2], U32)
        expo = sbuf("expo", [P, 3], F32)
        total = sbuf("total", [P, 3], F32)
        field = sbuf("field", [P, 2, 3], U32)
        scales = sbuf("scales", [P, 3], U32)
        weights_in, init = sem("weights_in"), sem("init")
        pool_init = sem("pool_init")
        filled = [sem(f"filled_{n}") for n in range(8)]
        freed = [sem(f"freed_{n}") for n in range(8)]
        ip_done, k0_done, k1_done, k2_done = sem("ip_done"), sem("k0_done"), sem("k1_done"), sem("k2_done")
        k_sent = sem("k_sent")
        amax_done, amax_all, bits = sem("amax_done"), sem("amax_all"), sem("bits")
        vh_done = sem("vh_done")
        centred, exp_done, sm_step = sem("centred_0"), sem("exp_done_p"), sem("sm_step")
        smax = K["res"][:, RR * KC:RR * KC + U * H]
        ssum = K["n2"][:].rearrange("p g h -> p (g h)")[:, 0:U * H]
        eh_done, el_done = sem("eh_done"), sem("el_done")

        LASTF = TR + KI + NT - 1

        def fills(b, n):
            return (4 if n % 8 <= LASTF % 8 else 3) * b + n // 8 + 1

        with nc.Block() as block:
            @block.sync
            def _(sp):
                def load(b):
                    src = ctx_in[b] if isinstance(b, int) else ctx_in[bass.ds(b, 1)].rearrange("a t c -> (a t) c")
                    sp.dma_start(e32[:, 0:NT - 1, :], src[0:P * (NT - 1)].rearrange("(t p) c -> p t c", p=P)).then_inc(ctx_loaded, 16)
                    sp.dma_start(e32[0:LAST, NT - 1, :], src[P * (NT - 1):TOK]).then_inc(ctx_loaded, 16)

                def send(b):
                    if isinstance(b, int) and b == B - 1:
                        sp.wait_ge(k_sent, 16 * SENDS * (B - 1))
                        sp.wait_ge(pool_init, 6)
                        load_pair(sp, K, L, 0, KS[0], QS[0], 0, 0, first=True)
                    for m, r0, rows, l, h0 in KSEG:
                        sp.wait_ge(k2_done, KI * b + 4 * (m + 1))
                        sp.wait_ge(init, 1)
                        for part in range(3):
                            dst = KS[l][h0:h0 + rows // DH, bass.ds(b, 1), part]
                            sp.dma_start(dst, kp[r0:r0 + rows, m, part, :]).then_inc(k_sent, 16)
                    sp.wait_ge(k2_done, KI * (b + 1))
                    sp.wait_ge(init, 1)
                    for j in range(2):
                        for part in range(3):
                            dst = KS[1][H - KREST // DH:H, bass.ds(b, 1), part].rearrange("h b d (g j k) -> h b d g j k", j=2, k=KC)[:, :, :, :, j]
                            src = kp[KREST * j:KREST * (j + 1), 2, part, 0:2 * KC].rearrange("p (g k) -> p g k", k=KC)
                            sp.dma_start(dst, src).then_inc(k_sent, 16)
                    for t0, t1 in ((0, NT // 2), (NT // 2, NT)):
                        n = TR + KI + t1 - 1
                        sp.wait_ge(freed[n % 8], fills(b, n))
                        sp.wait_ge(init, 1)
                        sp.dma_start(VS[0][:, bass.ds(b, 1), :, t0:t1].rearrange("g b p t n -> p b g (t n)"),
                                     vaug[:, :, t0:t1].rearrange("p g t i n -> p g (t i n)")).then_inc(v_sent, 16)
                    if not isinstance(b, int) or b < B - 1:
                        send_cut_v(sp, VS, L, b)

                for l in range(2):
                    sp.dma_start(wk[:, :, l * D:(l + 1) * D], w["wk"][l].rearrange("(c p) n -> p c n", p=P)).then_inc(weights_in, 16)
                    sp.dma_start(wv[:, :, l * D:(l + 1) * D], w["wv"][l].rearrange("(c p) n -> p c n", p=P)).then_inc(weights_in, 16)

                def turn(b):
                    sp.wait_ge(el_done, 2 * b)
                    sp.wait_ge(freed[TR - 1], fills(b - 1, TR - 1))
                    sp.wait_ge(init, 1)
                    load(b)
                    send(b - 1)

                turn(1)
                with sp.Fori(2, B, 1) as b:
                    turn(b)
                send(B - 1)
                sp.wait_ge(k_sent, 16 * SENDS * B)

            @block.tensor
            def _(pe):

                def batch(b, first):
                    def bank(n):
                        if n >= 8 or not first:
                            pe.wait_ge(freed[n % 8], fills(b, n) - 1)
                        return banks[n % 8]

                    pe.wait_ge(ctx_loaded, 32 * (b + 1))
                    for n in range(TR):
                        ps = bank(n)
                        for t in range(2 * n, min(2 * n + 2, NT)):
                            for c in range(2):
                                at = ((t % 2) * 2 + c) * P
                                last = pe.transpose(ps[:, at:at + P], e32[:, t, c * P:(c + 1) * P], K["ident"][:])
                        last.then_inc(filled[n % 8], 1)
                    pe.wait_ge(weights_in, 64)
                    for n in range(KI):
                        m, kc = n // 4, n % 4
                        if m == 0:
                            group = ((kc + 1) * KC - 1) // (2 * P)
                            for g in range(0 if kc == 0 else (kc * KC - 1) // (2 * P) + 1, group + 1):
                                pe.wait_ge(freed[g], fills(b, g))
                        ps = bank(TR + n)
                        for c in range(2):
                            if m < 2:
                                last = pe.matmul(ps[:, 0:KC], wk[:, c, m * P:(m + 1) * P],
                                                 ctxT[:, c, kc * KC:(kc + 1) * KC], start=(c == 0), stop=(c == 1))
                            else:
                                for j in range(2):
                                    last = pe.matmul(ps[KREST * j:KREST * (j + 1), 0:KC], wk[:, c, m * P:m * P + KREST],
                                                     ctxT[:, c, (2 * kc + j) * KC:(2 * kc + j + 1) * KC], start=(c == 0), stop=(c == 1))
                        last.then_inc(filled[(TR + n) % 8], 1)
                    pe.wait_ge(ip_done, b + 1)
                    for t in range(NT):
                        n = TR + KI + t
                        ps = bank(n)
                        for c in range(2):
                            last = pe.matmul(ps[:, 0:2 * D + IP[1]], ctxT[:, c, t * P:(t + 1) * P], wv[:, c, :],
                                             start=(c == 0), stop=(c == 1))
                        last.then_inc(filled[n % 8], 1)

                batch(0, True)
                with pe.Fori(1, B, 1) as b:
                    batch(b, False)

            def copy_transposed(eng, copy, b, n):
                nt = 2 if n < TR - 1 else 1
                eng.wait_ge(filled[n], fills(b, n))
                src = banks[n][:, 0:nt * 2 * P].rearrange("p (t c q) -> p c t q", t=nt, c=2)
                dst = ctxT[:, :, 2 * n * P:(2 * n + nt) * P].rearrange("p c (t q) -> p c t q", t=nt)
                copy(dst, src).then_inc(freed[n], 1)

            def context_part(part, rows, b, t0, t1):
                if isinstance(b, int):
                    return part[0:rows, b, t0:t1, AT:AT + C]
                return part[0:rows, bass.ds(b, 1), t0:t1, AT:AT + C].rearrange("p b t c -> p (b t) c")

            def v_pieces(n, t, rows):
                dots = banks[n % 8][0:rows, 2 * D:2 * D + IP[1]].unsqueeze(1).unsqueeze(1).to_broadcast([rows, PAIRS, 2, IP[1]])
                return ((1, [vcut[0:rows, :, c, t, :, 0:DH] for c in range(2)],
                         banks[n % 8][0:rows, D:2 * D].rearrange("p (g i d) -> p g i d", g=PAIRS, i=2)),
                        (2, [vcut[0:rows, :, c, t, :, DH + 1:VW[1]] for c in range(2)], dots))

            @block.scalar
            def _(act):
                def batch(b, first):
                    for n in range(TR) if first else (1, 3, 4, 5):
                        copy_transposed(act, nc.scalar.copy, b, n)
                    if first:
                        act.wait_ge(centred, 1)
                        nc.scalar.activation(L["sc"][:], L["sc"][:], ACT.Exp).then_inc(exp_done, 1)
                    if not first:
                        act.wait_ge(k_sent, 16 * SENDS * b)
                    for n in range(KI):
                        m, kc = n // 4, n % 4
                        act.wait_ge(filled[(TR + n) % 8], fills(b, TR + n))
                        nc.scalar.copy(kp[:, m, 0, kc * KC:(kc + 1) * KC], banks[(TR + n) % 8][:, 0:KC]).then_inc(k0_done, 1)
                        if n == 3:
                            act.wait_ge(bits, 6 * (b + 1))
                            scale = scales[:, 0:1].bitcast(F32)
                            act.wait_ge(init, 3)
                            for t0, t1, rows in ((0, NT - 1, P), (NT - 1, NT, TXT[1] - P * (NT - 1))):
                                nc.scalar.activation(context_part(K["eh"], rows, b, t0, t1), e32[0:rows, t0:t1, :], ACT.Copy,
                                                     scale=scale[0:rows]).then_inc(eh_done, 1)
                    act.wait_ge(pool_init, 4)
                    if not first:
                        act.wait_ge(v_sent, 16 * 2 * b)
                        act.wait_ge(L["v1_sent"], 16 * b)
                    for t in range(NT):
                        n = TR + KI + t
                        act.wait_ge(filled[n % 8], fills(b, n))
                        rows = min(P, TXT[0] - t * P)
                        nc.scalar.copy(vaug[0:rows, :, t, :, 0:DH], banks[n % 8][0:rows, 0:D].rearrange("p (g i d) -> p g i d", g=PAIRS, i=2))
                        rows = min(P, TXT[1] - t * P)
                        for which, dst, src in v_pieces(n, t, rows):
                            last = nc.scalar.activation(dst[0], src, ACT.Copy, scale=scales[0:rows, which:which + 1].bitcast(F32))
                        last.then_inc(vh_done, 1)

                batch(0, True)
                with act.Fori(1, B, 1) as b:
                    batch(b, False)

            @block.gpsimd
            def _(pool):
                nc.gpsimd.memset(vaug[:], 0.0)
                nc.gpsimd.memset(vcut[:], 0.0).then_inc(pool_init, 1)
                pool.wait_ge(pool_init, 1)
                for l, ones in ((0, vaug[:, :, :, :, DH]), (1, vcut[:, :, 0, :, :, DH])):
                    rows = TXT[l] - P * (NT - 1)
                    nc.gpsimd.memset(ones[:, :, 0:NT - 1], 1.0)
                    last = nc.gpsimd.memset(ones[0:rows, :, NT - 1], 1.0)
                last.then_inc(pool_init, 3)
                pool.wait_ge(amax_done, 1)
                nc.gpsimd.partition_all_reduce(amax[:, 3:4], amax[:, 2:3], P, bass.bass_isa.ReduceOp.max).then_inc(amax_all, 1)

                def batch(b):
                    pool.wait_ge(amax_done, b + 2)
                    nc.gpsimd.partition_all_reduce(amax[:, 1:2], amax[:, 0:1], P, bass.bass_isa.ReduceOp.max).then_inc(amax_all, 1)

                def last_parts(b):
                    for n in range(KI):
                        m, kc = n // 4, n % 4
                        k1 = kp[:, m, 1, kc * KC:(kc + 1) * KC]
                        k2 = kp[:, m, 2, kc * KC:(kc + 1) * KC]
                        pool.wait_ge(k1_done, KI * b + n + 1)
                        nc.gpsimd.tensor_tensor(k2, rem[:, n % RR, :], k1, ALU.subtract).then_inc(k2_done, 1)

                batch(0)
                last_parts(0)
                pool.wait_ge(amax_all, 2)
                nc.gpsimd.memset(K["qb"][:], 0.0)
                nc.gpsimd.memset(K["kb"][:, :, TXT[0]:NPAD], 0.0).then_inc(pool_init, 1)
                pool.wait_ge(pool_init, 5)
                nc.gpsimd.memset(K["kb"][KROWS:KROWS + 2, :, 0:TXT[0]], 1.0).then_inc(pool_init, 1)
                pool.wait_ge(pool_init, 6)
                for b in range(1, B):
                    batch(b)
                    last_parts(b)

            @block.vector
            def _(dve):
                nc.vector.memset(K["eh"][:, :, NT - 1, :], 0.0).then_inc(init, 2)
                nc.vector.memset(K["el"][:, :, NT - 1, :], 0.0).then_inc(init, 1)
                nc.vector.memset(expo[:, 0:1], 118.0)
                dve.wait_ge(weights_in, 64)
                nc.vector.tensor_reduce(amax[:, 2:3], wv[:, :, D:2 * D], AX.XY, ALU.max, apply_absolute_value=True).then_inc(amax_done, 1)
                dve.wait_ge(init, 3)
                nc.vector.tensor_copy(K["identb"][:], K["ident"][:]).then_inc(init, 1)
                dve.wait_ge(init, 4)
                done = [0]

                def link(ins):
                    done[0] += 1
                    ins.then_inc(sm_step, 1)
                    dve.wait_ge(sm_step, done[0])

                centre(nc.vector, link, L, 0, L["mask"], smax).then_inc(centred, 1)

                def batch(b, first):
                    for n in () if first else (0, 2, 6):
                        copy_transposed(dve, nc.vector.tensor_copy, b, n)
                    if not first:
                        dve.wait_ge(filled[LASTF % 8], fills(b, LASTF) - 4)
                    tok = slice(IP[0] - IP[1], IP[0])
                    ip = K["ipT"][:, :, b, tok] if isinstance(b, int) else K["ipT"][:, :, bass.ds(b, 1), tok].rearrange("p c b n -> p c (b n)")
                    nc.vector.tensor_copy(wv[:, :, 2 * D:2 * D + IP[1]], ip).then_inc(ip_done, 1)
                    nc.vector.tensor_reduce(amax[:, 0:1], e32[:], AX.XY, ALU.max, apply_absolute_value=True).then_inc(amax_done, 1)
                    for n in range(KI):
                        m, kc = n // 4, n % 4
                        k0 = kp[:, m, 0, kc * KC:(kc + 1) * KC]
                        k1 = kp[:, m, 1, kc * KC:(kc + 1) * KC]
                        r = rem[:, n % RR, :]
                        if not first or n >= RR:
                            dve.wait_ge(k2_done, KI * b + n - RR + 1)
                        dve.wait_ge(k0_done, KI * b + n + 1)
                        nc.vector.tensor_tensor(r, banks[(TR + n) % 8][:, 0:KC], k0, ALU.subtract).then_inc(freed[(TR + n) % 8], 1)
                        dve.wait_ge(freed[(TR + n) % 8], fills(b, TR + n))
                        nc.vector.tensor_copy(k1, r).then_inc(k1_done, 1)
                        if n == 1:
                            dve.wait_ge(amax_all, b + 2)
                            if not first:
                                dve.wait_ge(el_done, 2 * b)
                                dve.wait_ge(freed[LASTF % 8], fills(b - 1, LASTF))
                            if first:
                                nc.vector.tensor_scalar(ebits[:, 0:1], amax[:, 3:4].bitcast(U32), 23, None, ALU.logical_shift_right)
                            nc.vector.tensor_scalar(ebits[:, 1:2], amax[:, 1:2].bitcast(U32), 23, None, ALU.logical_shift_right).then_inc(bits, 1)
                            dve.wait_ge(bits, 6 * b + 1)
                            nc.vector.tensor_scalar(expo[:, 1:3], ebits[:], 15, None, ALU.max).then_inc(bits, 1)
                            dve.wait_ge(bits, 6 * b + 2)
                            nc.vector.tensor_tensor(total[:], expo[:], expo[:, 2:3].to_broadcast([P, 3]), ALU.add).then_inc(bits, 1)
                            dve.wait_ge(bits, 6 * b + 3)
                            nc.vector.tensor_scalar(total[:], total[:], 133, 385, ALU.max, ALU.min).then_inc(bits, 1)
                            dve.wait_ge(bits, 6 * b + 4)
                            nc.vector.tensor_scalar(field[:, 0], total[:], -1, 386, ALU.mult, ALU.add)
                            nc.vector.tensor_scalar(field[:, 1], total[:], -132, None, ALU.add).then_inc(bits, 1)
                            dve.wait_ge(bits, 6 * b + 5)
                            inv = K["inv"][:, :, b:b + 1] if isinstance(b, int) else K["inv"][:, :, bass.ds(b, 1)]
                            nc.vector.tensor_scalar(inv.bitcast(U32), field[:, 1].unsqueeze(2), 23, None, ALU.logical_shift_left)
                            nc.vector.tensor_scalar(scales[:], field[:, 0], 23, None, ALU.logical_shift_left).then_inc(bits, 1)
                            dve.wait_ge(bits, 6 * b + 6)
                        if n in (5, 6):
                            t0, t1, rows = ((0, NT - 1, P), (NT - 1, NT, TXT[1] - P * (NT - 1)))[n - 5]
                            dve.wait_ge(eh_done, 2 * b + n - 4)
                            nc.vector.scalar_tensor_tensor(out=context_part(K["el"], rows, b, t0, t1), in0=e32[0:rows, t0:t1, :],
                                                           scalar=scales[0:rows, 0:1].bitcast(F32),
                                                           in1=context_part(K["eh"], rows, b, t0, t1), op0=ALU.mult, op1=ALU.subtract).then_inc(el_done, 1)
                    if first:
                        dve.wait_ge(exp_done, 1)
                        link(normalise(nc.vector, link, L, 0, None, ssum))
                    for t in range(NT):
                        n = TR + KI + t
                        rows = min(P, TXT[1] - t * P)
                        dve.wait_ge(vh_done, NT * b + t + 1)
                        for which, dst, src in v_pieces(n, t, rows):
                            for i in range(2):
                                last = nc.vector.scalar_tensor_tensor(out=dst[1][:, :, i], in0=src[:, :, i],
                                                                      scalar=scales[0:rows, which:which + 1].bitcast(F32),
                                                                      in1=dst[0][:, :, i], op0=ALU.mult, op1=ALU.subtract)
                        last.then_inc(freed[n % 8], 1)

                batch(0, True)
                with dve.Fori(1, B, 1) as b:
                    batch(b, False)


def queries(nc, K, L, layer, banks, w, consts, KS, QS, first, spatial=None):
    with ExitStack() as st:
        def sbuf(name, shape, dt):
            return st.enter_context(nc.sbuf_tensor(f"{name}_{layer}", shape, dt))

        def sem(name):
            return st.enter_context(nc.semaphore(f"{name}_{layer}"))

        R1 = D - P
        n = IP[layer]
        W = H * n
        CH = ((0, P), (P, D))
        RC = token_rows(layer)
        tok = slice(IP[0] - n, IP[0])
        wq = w["wq"][layer]
        xT0, xT1 = sbuf("xT0", [P, U * P], F32), sbuf("xT1", [P, U * P], F32)
        qT = (sbuf("qT0", [P, U * P], F32), sbuf("qT1", [P, U * P], F32))
        w0, w1 = sbuf("wq0", [P, D], F32), sbuf("wq1", [P, D], F32)
        parts = L["parts"]
        r = (sbuf("qr0", [P, U * P], F32), sbuf("qr1", [R1, U * P], F32))
        wki, wvi = sbuf("wki", [P, 2, D], F32), sbuf("wvi", [P, 2, D], F32)
        bias = sbuf("bias", [P, D], F32)
        mask_k = (sbuf("mask_k0", [P, W], F32), sbuf("mask_k1", [R1, W], F32))
        mask_v = tuple(sbuf(f"mask_v{i}", [b - a, D], F32) for i, (a, b) in enumerate(RC))
        ip_rep = sbuf("ip_rep", [P, 2, B, W], F32)
        kip = (sbuf("kip0", [P, B, n], F32), sbuf("kip1", [R1, B, n], F32))
        bk = (sbuf("bk0", [P, B, H, n], F32), sbuf("bk1", [P, B, H, n], F32))
        w_in, loaded, padded = sem("w_in"), sem("loaded"), sem("padded")
        turned, xT_done, made, q_done = sem("turned"), sem("xT_done"), sem("made"), sem("q_done")
        cut = (sem("cut_0"), sem("cut_1"))
        rep_done, kip_made, kip_out, bk_done = sem("rep_done"), sem("kip_made"), sem("kip_out"), sem("bk_done")
        bv_made, bv_done, sc_made = sem("bv_made"), sem("bv_done"), sem("sc_made")
        if first:
            x, ctx_in, e32, ctx_loaded, bbox = first
            tokens = sbuf("tokens", [B * IP[0], C], F32)
            boxes = sbuf("boxes", [P, B, 4, 4], F32)
            grid = sbuf("grid", [P, 1 + NH], F32)
            cond = sbuf("cond", [P, 4, B, 4], F32)
            inside = sbuf("inside", [P, B, 4], F32)
            covered = sbuf("covered", [P, B], F32)
            boxes_in, dve_step, zeroed = sem("boxes_in"), sem("mask_step"), sem("zeroed")
            first_in, ip_turned, ip_out = sem("first_in"), sem("ip_turned"), sem("ip_out")
        NLOAD = 7 + len(RC) + (NH + 1 if layer else 0)
        if layer:
            sq, ones = sbuf("sq", [P, 2, B, n], F32), sbuf("ones", [P, P], F32)
            sq_done, sq_made = sem("sq_done"), sem("sq_made")
        with nc.Block() as block:
            @block.sync
            def _(sp):
                def load(dst, src, signal=loaded):
                    sp.dma_start(dst, src).then_inc(signal, 16)

                if first:
                    load(K["ident"][:], consts["ident"], first_in)
                    for h in range(2):
                        load(K["xq"][:, h * NH * 2:(h + 1) * NH * 2], x[2 * h:2 * h + 2].rearrange("b (h p) c -> p (b h) c", p=P), first_in)
                    load(w0[:], wq[0:P], w_in)
                    load(w1[0:R1], wq[P:D], w_in)
                    for b in range(B):
                        load(tokens[b * IP[0]:(b + 1) * IP[0], :], ctx_in[b, TOK - IP[0]:TOK, :], first_in)
                if not first:
                    load(w0[:], wq[0:P], w_in)
                    load(w1[0:R1], wq[P:D], w_in)
                load(wki[:], w["wk_ip"][layer].rearrange("(c p) n -> p c n", p=P))
                load(wvi[:], w["wv_ip"][layer].rearrange("(c p) n -> p c n", p=P))
                if first:
                    load(e32[:, 0:NT - 1, :], ctx_in[0, 0:P * (NT - 1)].rearrange("(t p) c -> p t c", p=P), ctx_loaded)
                    sp.wait_ge(zeroed, 1)
                    load(e32[0:TOK - P * (NT - 1), NT - 1, :], ctx_in[0, P * (NT - 1):TOK, :], ctx_loaded)
                load(mask_k[0][:], consts[f"mask_k{layer}"][0:P])
                load(mask_k[1][:], consts[f"mask_k{layer}"][P:D])
                for i, (a, b) in enumerate(RC):
                    load(mask_v[i][:], consts[f"mask_v{layer}"][a:b])
                load(L["wo"][0][:], w["wo"][layer][0:P])
                load(L["wo"][1][:], w["wo"][layer][P:D])
                load(bias[:], w["bo"][layer].partition_broadcast(P))
                if first:
                    load(boxes[:].rearrange("p b m c -> p (b m c)"), bbox.rearrange("b m c -> (b m c)").partition_broadcast(P), boxes_in)
                    load(grid[:], consts["grid"], boxes_in)
                    load(K["fold"][:], consts["fold"], boxes_in)
                if layer:
                    for h in range(NH):
                        load(L["spat"][:, h:h + 1], spatial[h * P:(h + 1) * P].rearrange("(p o) -> p o", o=1))
                    load(ones[:], consts["ones"])
                for m in range(2):
                    sp.wait_ge(cut[m], 4)
                    h0, nh = ((0, P // DH), (P // DH, R1 // DH))[m]
                    for j, part in enumerate(Q_PART):
                        dst = QS[h0:h0 + nh, j].rearrange("h d b q -> h d (b q)")
                        load(dst, parts[m][:, part, :], L["sent"][m])
                    if layer and m == 0:
                        load_pair(sp, K, L, layer, KS, QS, 0, 0, first=True)

            @block.tensor
            def _(pe):
                if first:
                    pe.wait_ge(first_in, 16 * (3 + B))
                    for c in range(2):
                        last = pe.transpose(banks[7][:, c * B * IP[0]:(c + 1) * B * IP[0]], tokens[:, c * P:(c + 1) * P],
                                            K["ident"][0:B * IP[0], 0:B * IP[0]])
                    last.then_inc(ip_turned, 1)
                for u in range(U):
                    pe.transpose(banks[u // 4][:, (u % 4) * P:(u % 4 + 1) * P], K["xq"][:, u, 0:P], K["ident"][:])
                    last = pe.transpose(banks[2 + u // 4][0:R1, (u % 4) * P:(u % 4 + 1) * P], K["xq"][:, u, P:D], K["ident"][:])
                last.then_inc(turned, 1)
                pe.wait_ge(w_in, 32)
                pe.wait_ge(padded, 2 * (P // R1 - 1))
                pe.wait_ge(xT_done, 4)
                if first:
                    pe.wait_ge(ip_out, 1)
                for m, (c0, c1) in enumerate(CH):
                    for h in range(2):
                        ps = banks[4 + 2 * m + h][0:c1 - c0, :]
                        pe.matmul(ps, w0[:, c0:c1], xT0[:, h * 512:(h + 1) * 512], start=True, stop=False)
                        pe.matmul(ps, w1[:, c0:c1], xT1[:, h * 512:(h + 1) * 512], start=False, stop=True).then_inc(made, 1)
                pe.wait_ge(loaded, 16 * NLOAD)
                if layer:
                    pe.wait_ge(sq_done, 1)
                    for c in range(2):
                        last = pe.matmul(banks[0][:, P:P + B * n], ones[:], sq[:, c], start=(c == 0), stop=(c == 1))
                    last.then_inc(sq_made, 1)
                for i, (a, b) in enumerate(CH):
                    for c in range(2):
                        last = pe.matmul(banks[i][0:b - a, 0:B * n], wki[:, c, a:b], K["ipT"][:, c, :, tok],
                                         start=(c == 0), stop=(c == 1))
                last.then_inc(kip_made, 1)
                pe.wait_ge(rep_done, 1)
                pe.wait_ge(q_done, 2)
                for b in range(B):
                    for i, (r0, r1) in enumerate(RC):
                        for c in range(2):
                            last = pe.matmul(banks[2 + b][0:r1 - r0, i * D:(i + 1) * D], ip_rep[:, c, b, r0:r1], wvi[:, c, :],
                                             start=(c == 0), stop=(c == 1))
                    last.then_inc(bv_made, 1)
                pe.wait_ge(q_done, 4)
                pe.wait_ge(bk_done, 2)
                pe.wait_ge(bv_done, B)
                pe.wait_ge(padded, 4 * (P // R1 - 1))
                for u in range(U):
                    for i in range(2):
                        last = pe.matmul(banks[u][:, 0:W], qT[i][:, u * P:(u + 1) * P], bk[i][:, u // NH].rearrange("p h n -> p (h n)"),
                                         start=(i == 0), stop=(i == 1))
                    last.then_inc(sc_made, 1)

            @block.scalar
            def _(act):
                if first:
                    act.wait_ge(ip_turned, 1)
                    nc.scalar.copy(K["ipT"][:].rearrange("p c b n -> p (c b n)"), banks[7][:, 0:2 * B * IP[0]]).then_inc(ip_out, 1)
                act.wait_ge(turned, 1)
                for h in range(2):
                    nc.scalar.copy(xT0[:, h * 512:(h + 1) * 512], banks[h]).then_inc(xT_done, 1)
                for m in range(2):
                    for h in range(2):
                        act.wait_ge(made, 2 * m + h + 1)
                        nc.scalar.copy(qT[m][0:(P, R1)[m], h * 512:(h + 1) * 512], banks[4 + 2 * m + h][0:(P, R1)[m], :]).then_inc(q_done, 1)
                act.wait_ge(kip_made, 1)
                if layer:
                    act.wait_ge(sq_made, 1)
                    nc.scalar.copy(L["token_sq"][:].rearrange("p b n -> p (b n)"), banks[0][:, P:P + B * n])
                for i, (a, b) in enumerate(CH):
                    nc.scalar.copy(kip[i][:].rearrange("p b n -> p (b n)"), banks[i][0:b - a, 0:B * n]).then_inc(kip_out, 1)
                for u in range(U):
                    act.wait_ge(sc_made, u + 1)
                    nc.scalar.activation(L["sc"][:, u], banks[u][:, 0:W], ACT.Copy, scale=SCALE)

            @block.gpsimd
            def _(pool):
                for r0 in range(R1, P, R1):
                    nc.gpsimd.memset(xT1[r0:r0 + R1, :], 0.0).then_inc(padded, 1)
                    nc.gpsimd.memset(w1[r0:r0 + R1, :], 0.0).then_inc(padded, 1)
                for r0 in range(R1, P, R1):
                    nc.gpsimd.memset(qT[1][r0:r0 + R1, :], 0.0).then_inc(padded, 1)
                    nc.gpsimd.memset(bk[1][r0:r0 + R1].rearrange("p b h n -> p (b h n)"), 0.0).then_inc(padded, 1)
                pool.wait_ge(padded, 4 * (P // R1 - 1))
                pool.wait_ge(loaded, 16 * NLOAD)
                if first:
                    pool.wait_ge(first_in, 16 * (3 + B))
                nc.gpsimd.tensor_tensor(L["base"][:], K["xq"][:], bias[:].unsqueeze(1).to_broadcast([P, U, D]), ALU.add)

            def cut_parts(eng, m, q):
                steps = cut[m]
                eng.tensor_copy(parts[m][:, 0], q).then_inc(steps, 1)
                eng.wait_ge(steps, 1)
                eng.tensor_tensor(r[m][:], q, parts[m][:, 0], ALU.subtract).then_inc(steps, 1)
                eng.wait_ge(steps, 2)
                eng.tensor_copy(parts[m][:, 1], r[m][:]).then_inc(steps, 1)
                eng.wait_ge(steps, 3)
                eng.tensor_tensor(parts[m][:, 2], r[m][:], parts[m][:, 1], ALU.subtract).then_inc(steps, 1)

            @block.vector
            def _(dve):
                vec = nc.vector
                if first:
                    vec.memset(e32[64:P, NT - 1, :], 0.0).then_inc(zeroed, 1)
                dve.wait_ge(turned, 1)
                for h in range(2):
                    vec.tensor_copy(xT1[0:R1, h * 512:(h + 1) * 512], banks[2 + h][0:R1, :]).then_inc(xT_done, 1)
                if first:
                    dve.wait_ge(ip_out, 1)
                for c in range(2):
                    last = vec.tensor_copy(ip_rep[:, c].rearrange("p b (h n) -> p b h n", n=n),
                                           K["ipT"][:, c, :, tok].unsqueeze(2).to_broadcast([P, B, H, n]))
                last.then_inc(rep_done, 1)
                if layer:
                    vec.tensor_tensor(sq[:], K["ipT"][:, :, :, tok], K["ipT"][:, :, :, tok], ALU.mult).then_inc(sq_done, 1)
                dve.wait_ge(q_done, 2)
                cut_parts(vec, 0, qT[0][:])
                dve.wait_ge(loaded, 16 * NLOAD)
                dve.wait_ge(kip_out, 2)
                for i in range(2):
                    rows = CH[i][1] - CH[i][0]
                    vec.tensor_tensor(bk[i][0:rows], kip[i][:].unsqueeze(2).to_broadcast([rows, B, H, n]),
                                      mask_k[i][:].rearrange("p (h n) -> p h n", n=n).unsqueeze(1).to_broadcast([rows, B, H, n]),
                                      ALU.mult).then_inc(bk_done, 1)
                for b in range(B):
                    dve.wait_ge(bv_made, b + 1)
                    for i, (r0, r1) in enumerate(RC):
                        last = vec.tensor_tensor(L["bv"][i][:, b, :], banks[2 + b][0:r1 - r0, i * D:(i + 1) * D], mask_v[i][:], ALU.mult)
                    last.then_inc(bv_done, 1)
                dve.wait_ge(q_done, 4)
                cut_parts(vec, 1, qT[1][0:R1])
                if first:
                    done = [0]

                    def link(ins):
                        done[0] += 1
                        ins.then_inc(dve_step, 1)
                        dve.wait_ge(dve_step, done[0])

                    dve.wait_ge(boxes_in, 48)
                    for h in range(NH):
                        for c, (coord, at, op) in enumerate(((0, 0, ALU.is_le), (1, 1 + h, ALU.is_le), (2, 0, ALU.is_ge), (3, 1 + h, ALU.is_ge))):
                            last = vec.tensor_scalar(cond[:, c], boxes[:, :, :, coord], grid[:, at:at + 1], None, op)
                        link(last)
                        link(vec.tensor_tensor(cond[:, 0:2], cond[:, 0:2], cond[:, 2:4], ALU.mult))
                        link(vec.tensor_tensor(inside[:], cond[:, 0], cond[:, 1], ALU.mult))
                        vec.tensor_scalar(L["mask"][:, h:U:NH, 0, 4:8], inside[:], -NEG, NEG, ALU.mult, ALU.add)
                        link(vec.tensor_reduce(covered[:], inside[:], AX.X, ALU.max))
                        link(vec.tensor_scalar(L["mask"][:, h:U:NH, 0, 0:4], covered[:].unsqueeze(2).to_broadcast([P, B, 4]), NEG, None, ALU.mult))


def attend(nc, K, L, layer, KS, QS, VSs, ps_x, ps_y, ps_t, ps_v, ps_n):
    with ExitStack() as st:
        def sbuf(name, shape, dt):
            return st.enter_context(nc.sbuf_tensor(f"{name}_{layer}", shape, dt))

        def sem(name):
            return st.enter_context(nc.semaphore(f"{name}_{layer}"))

        VS = VSs[layer]
        NV = TXT[layer]
        CUT = ((NV + 1) // 2, NV // 2)
        kb, qb = K["kb"], K["qb"]
        cols = VW[layer]
        vb = sbuf("vb", [P, 2, 1 + layer, NT, 2, cols], F16 if layer else F32)
        pe32 = sbuf("pe32", [P, 2 - layer, NT, 2 * S], F32)
        if layer:
            ph = sbuf("ph", [P, 2, NT, 2 * S], F16)
            pl = sbuf("pl", [P, 2, NT, 2 * S], F16)
            junk = sbuf("junk", [P, 2, S], F32)
        else:
            acc = sbuf("acc", [P, 2, S], F32)
        mx = sbuf("mx", [P, 2, 8], F32)
        mm = sbuf("mm", [P, 2, 4], F32)
        mn = sbuf("mn", [P, 2, 4], F32)
        shift = sbuf("shift", [P, 4], F32)
        mp = sbuf("mp", [P, 2, 4, 2], BF16)
        ready = sem("ready")
        kq_loaded = L["kq_loaded"]
        v_loaded = [sem(f"v_loaded_{n}") for n in range(2)]
        chunk_made, chunk_max = sem("chunk_made"), sem("chunk_max")
        m1, m2, m3, m_parts = sem("m1"), sem("m2"), sem("m3"), sem("m_parts")
        m_turned, m_rows = sem("m_turned"), sem("m_rows")
        st_made, exp_done = sem("st_made"), sem("exp_done")
        if layer:
            half_done, low_done, norm_made, norm_out = sem("half_done"), sem("low_done"), sem("norm_made"), sem("norm_out")
            v_placed = sem("v_placed")
        else:
            acc_made, acc_out, turned, turned_out = sem("acc_made"), sem("acc_out"), sem("turned"), sem("turned_out")
        HALVES = (NT + 1) // 2

        USES = NT + layer
        MAX_AT = NT - 2 + layer

        def TURN(o, pos):
            return (o * USES + pos) % 2

        def tile_bank(o, t):
            return ps_t[:, TURN(o, USES - 1 if t == NT - 1 else t), :]

        def maxima_bank(o):
            return ps_t[KROWS:KROWS + 2, TURN(o, NT - 1), :] if layer else ps_n[KROWS:KROWS + 2, :]

        def at_least(eng, semaphore, value):
            if not isinstance(value, int) or value > 0:
                eng.wait_ge(semaphore, value)

        def uses(k, o, n):
            return (4 // n) * k + o // n + 1

        def steps(eng, step):
            for s in range(-2, 2):
                step(0, s)
            with eng.Fori(0, (G - 4) // 4, 1) as k:
                for o in range(2, 6):
                    step(k, o)
            for s in range(G - 2, G + 2):
                step(0, s)

        def has(k, o, d):
            return not isinstance(k, int) or 0 <= o + d < G

        with nc.Block() as block:
            @block.sync
            def _(sp):
                sp.wait_ge(ready, 2)

                def load(k, o):
                    s = 4 * k + o
                    sp.wait_ge(st_made, NT * (s - RING + 1))
                    sp.wait_ge(ready, 2)
                    load_pair(sp, K, L, layer, KS, QS, k, o)

                def load_v(k, o):
                    s = 4 * k + o
                    if not isinstance(s, int) or s >= 2:
                        sp.wait_ge(v_placed if layer else acc_made, s - 1)
                        sp.wait_ge(ready, 2)
                    src = VS[bass.ds(k + o // B, 1), o % B].rearrange("g p n -> (g p) n" if layer else "g p t n -> (g p) (t n)")
                    sp.dma_start(vb[:, o % 2].rearrange("p c t i n -> p (c t i n)"), src).then_inc(v_loaded[o % 2], 16)

                for s in range(1, RING):
                    load_pair(sp, K, L, layer, KS, QS, 0, s)
                load_v(0, 0)
                sp.wait_ge(L["sent"][1], 16 * 6)
                if not layer:
                    sp.wait_ge(L["v_sent"], 16 * 2 * B)
                    send_cut_v(sp, VSs, L, B - 1)
                with sp.Fori(1, G // 4, 1) as k:
                    for o in range(4):
                        load_v(k, o - 3)
                        load(k, o)
                for s in range(G - 3, G):
                    load_v(0, s)
                if not layer:
                    sp.wait_ge(L["v1_sent"], 16 * B)

            @block.tensor
            def _(pe):
                pe.wait_ge(ready, 2)

                def scores(k, o, c):
                    if not has(k, o, 1):
                        return
                    s, n = 4 * k + o + 1, (o + 1) % RING
                    hh, e = c // 2, c % 2
                    if c == 0:
                        pe.wait_ge(kq_loaded[n], 128 * uses(k, o + 1, RING))
                    at_least(pe, chunk_max, 8 * s + c - 1)
                    ps = (ps_x, ps_y)[c % 2]
                    k0, k1 = (0, CUT[0]) if e == 0 else (CUT[0], NV)
                    for a in range(k0, k1, 512):
                        z = min(a + 512, k1)
                        last = pe.matmul(ps[:, (a - k0) // 512, 0:z - a], qb[0:KROWS, n, hh * P:(hh + 1) * P],
                                         kb[0:KROWS, n, a:z], start=True, stop=True)
                    last.then_inc(chunk_made, 1)

                def turn_max(k, o):
                    if not has(k, o, 1):
                        return
                    s = 4 * k + o
                    pe.wait_ge(m_parts, s + 2)
                    if layer:
                        if has(k, o, 0):
                            pe.wait_ge(exp_done, NT * s + NT - 2)
                    elif has(k, o, -2):
                        pe.wait_ge(turned_out, s - 1)
                    else:
                        at_least(pe, m_rows, s + 1)
                    for hh in range(4):
                        last = pe.matmul(maxima_bank(o)[:, hh * P:(hh + 1) * P], mp[:, (o + 1) % 2, hh, :], K["identb"][:],
                                         start=True, stop=True)
                    last.then_inc(m_turned, 1)

                def turn_result(k, o):
                    if layer or not has(k, o, -2):
                        return
                    s = 4 * k + o
                    pe.wait_ge(acc_out, s - 1)
                    pe.wait_ge(m_rows, min(s + 1, G) if isinstance(s, int) else s + 1)
                    for h in range(NH):
                        last = pe.matmul(ps_n[:, 32 * h:32 * h + 2 * cols], acc[:, o % 2, h * P:(h + 1) * P], K["fold"][:],
                                         start=True, stop=True)
                    last.then_inc(turned, 1)

                def exponents(k, o, t):
                    if not has(k, o, 0):
                        return
                    s, n = 4 * k + o, o % RING
                    if t == 0:
                        pe.wait_ge(m_rows, s + 1)
                    if t or not layer:
                        at_least(pe, exp_done, NT * s + t - (0 if t == NT - 1 and layer else 1))
                    pe.matmul(tile_bank(o, t), kb[0:KROWS + 2, n, t * P:(t + 1) * P], qb[0:KROWS + 2, n, :],
                              start=True, stop=True).then_inc(st_made, 1)

                def products(k, o, tiles):
                    if layer or not has(k, o, -1):
                        return
                    s, n = 4 * k + o, (o - 1) % 2
                    if tiles[0] == 0:
                        at_least(pe, acc_out, s - 1)
                        pe.wait_ge(v_loaded[n], 16 * uses(k, o - 1, 2))
                    pe.wait_ge(exp_done, NT * (s - 1) + tiles[-1] + 1)
                    for i in range(2):
                        for t in tiles:
                            r0 = 32 * (2 * i + t % 2)
                            last = pe.matmul(ps_v[r0:r0 + cols, 0:S], vb[:, n, 0, t, i, :], pe32[:, n, t, i * S:(i + 1) * S],
                                             start=(t < 2), stop=(t >= NT - 2))
                    if tiles[-1] == NT - 1:
                        last.then_inc(acc_made, 1)

                def unit(k, o, q):
                    s, n = 4 * k + o, (o - 1) % 2
                    hh, t = q // NT, q % NT
                    if t == 0:
                        at_least(pe, norm_out, 4 * (s - 1) + hh - 1)
                    if hh == 0:
                        if t == 0:
                            pe.wait_ge(v_placed, s)
                        pe.wait_ge(low_done, HALVES * (s - 1) + t // 2 + 1)
                    b, c0 = (o - 1) % B, (1, AT)[hh // NH]
                    hi, lo = ph[:, n, t, hh * P:(hh + 1) * P], pl[:, n, t, hh * P:(hh + 1) * P]
                    eh, el = K["eh"][:, b, t, c0:c0 + cols + C], K["el"][:, b, t, c0:c0 + cols + C]
                    ps = (ps_v, ps_n)[hh % 2][:, 0:cols + C]
                    pe.matmul(ps, hi, eh, start=(t == 0), stop=False)
                    pe.matmul(ps, hi, el, start=False, stop=False)
                    last = pe.matmul(ps, lo, eh, start=False, stop=(t == NT - 1))
                    if t == NT - 1:
                        last.then_inc(norm_made, 1)

                def step(k, o):
                    for t in range(NT):
                        if t == MAX_AT:
                            turn_max(k, o)
                        exponents(k, o, t)
                        if t in CHUNK_AT[layer]:
                            d, c = CHUNK_AT[layer][t]
                            scores(k, o + d - 1, c)
                        if t == 6:
                            turn_result(k, o)
                        if t in PRODUCTS_AT:
                            products(k, o, PRODUCTS_AT[t])
                        if layer and has(k, o, -1):
                            for q in range(4 * t, 4 * t + 4):
                                unit(k, o, q)

                steps(pe, step)

            @block.scalar
            def _(act):
                def step(k, o):
                    s = 4 * k + o
                    def unit_out(d, hh):
                        if not layer or not has(k, o, d):
                            return
                        act.wait_ge(norm_made, 4 * (s + d) + hh + 1)
                        g = 4 * (s + d) + hh
                        i, h = hh // NH, hh % NH
                        ps = (ps_v, ps_n)[hh % 2]
                        v0, c0 = ((0, cols), (C, 0))[i]
                        dst = K["n2"][:].rearrange("p g h -> p (g h)")
                        dst = dst[:, g:g + 1] if isinstance(g, int) else dst[:, bass.ds(g, 1)]
                        if not isinstance(g, int) or g >= 2:
                            act.wait_ge(norm_out, g - 1)
                        nc.scalar.activation(junk[:, hh % 2, :], ps[:, c0:c0 + C], ACT.Square, accum_out=dst)
                        dst = result_of(K, 1)[:, s + d, h, i, :] if isinstance(s, int) else \
                            result_of(K, 1)[:, bass.ds(s + d, 1), h, i, :].rearrange("p g v -> p (g v)")
                        nc.scalar.copy(dst, ps[:, v0:v0 + cols]).then_inc(norm_out, 1)

                    unit_out(-2, 3)
                    if has(k, o, -2) and not layer:
                        act.wait_ge(acc_made, s - 1)
                        nc.scalar.copy(acc[:, o % 2, :], ps_v[:, 0:S]).then_inc(acc_out, 1)
                    for t in range(NT):
                        if t in (4, 7, 10):
                            unit_out(-1, t // 3 - 1)
                        if t == MAX_AT and has(k, o, 1):
                            act.wait_ge(m_turned, s + 2)
                            nc.scalar.copy(qb[KROWS:KROWS + 2, (o + 1) % RING, :], maxima_bank(o)).then_inc(m_rows, 1)
                        if has(k, o, 0):
                            if t == 0 and (not isinstance(s, int) or s >= 2):
                                if not layer:
                                    act.wait_ge(acc_made, s - 1)
                                else:
                                    act.wait_ge(norm_made, 4 * (s - 1))
                            act.wait_ge(st_made, NT * s + t + 1)
                            if layer and t % 2 == 0 and (not isinstance(s, int) or s >= 1):
                                act.wait_ge(low_done, HALVES * (s - 1) + t // 2 + 1)
                            nc.scalar.activation(pe32[:, 0 if layer else o % 2, t, :], tile_bank(o, t), ACT.Exp, scale=SCALE).then_inc(exp_done, 1)
                            if layer and (t % 2 == 1 or t == NT - 1):
                                t0 = t - t % 2
                                act.wait_ge(exp_done, NT * s + t + 1)
                                nc.scalar.copy(ph[:, o % 2, t0:t + 1, :], pe32[:, 0, t0:t + 1, :]).then_inc(half_done, 1)
                        if t == 6 and not layer and has(k, o, -2):
                            act.wait_ge(turned, s - 1)
                            dst = result_of(K, 0).rearrange("p g h i v -> p g h (i v)")
                            dst = dst[:, s - 2] if isinstance(s, int) else dst[:, bass.ds(s - 2, 1)].rearrange("p g h n -> p (g h) n")
                            src = ps_n[:, 0:32 * NH].rearrange("p (h n) -> p h n", h=NH)[:, :, 0:2 * cols]
                            nc.scalar.copy(dst, src).then_inc(turned_out, 1)

                steps(act, step)

            @block.gpsimd
            def _(pool):
                nc.gpsimd.memset(shift[:], SHIFT[layer]).then_inc(ready, 1)
                pool.wait_ge(ready, 2)

                def step(k, o):
                    if not has(k, o, 1):
                        return
                    s, n = 4 * k + o + 1, (o + 1) % 2
                    pool.wait_ge(m1, s + 1)
                    nc.gpsimd.tensor_tensor(mn[:, n], mm[:, n], shift[:], ALU.add).then_inc(m2, 1)
                    if not isinstance(s, int) or s >= 2:
                        pool.wait_ge(m_turned, s - 1)
                    nc.gpsimd.tensor_tensor(mp[:, n, :, 0], mm[:, n], shift[:], ALU.add).then_inc(m3, 1)
                    pool.wait_ge(m2, s + 1)
                    pool.wait_ge(m3, s + 1)
                    nc.gpsimd.tensor_tensor(mp[:, n, :, 1], mn[:, n], mp[:, n, :, 0], ALU.subtract).then_inc(m_parts, 1)

                steps(pool, step)

            @block.vector
            def _(dve):
                if layer:
                    nc.vector.memset(kb[KROWS:KROWS + 2, :, TXT[0]:NV], 1.0)
                nc.vector.memset(ps_v[:], 0.0).then_inc(ready, 1)

                def step(k, o):
                    s = 4 * k + o

                    def chunk(d, c):
                        if not has(k, o, d):
                            return
                        pair = s + d
                        if c == 0 and (not isinstance(s, int) or pair >= 2):
                            dve.wait_ge(m1, pair - 1)
                        dve.wait_ge(chunk_made, 8 * pair + c + 1)
                        w = CUT[c % 2]
                        src = (ps_x, ps_y)[c % 2][:].rearrange("p a b -> p (a b)")[:, 0:w]
                        nc.vector.tensor_reduce(mx[:, (o + d) % 2, c:c + 1], src, AX.X, ALU.max).then_inc(chunk_max, 1)
                        if c == 7:
                            dve.wait_ge(chunk_max, 8 * (pair + 1))
                            if not isinstance(s, int) or pair >= 1:
                                dve.wait_ge(m3, pair)
                            nc.vector.tensor_reduce(mm[:, (o + d) % 2], mx[:, (o + d) % 2].rearrange("p (h e) -> p h e", e=2),
                                                    AX.X, ALU.max, negate=True).then_inc(m1, 1)

                    def low(n):
                        if not layer or not has(k, o, 0):
                            return
                        t0, t1 = 2 * n, min(2 * n + 2, NT)
                        dve.wait_ge(half_done, HALVES * s + n + 1)
                        nc.vector.tensor_tensor(pl[:, o % 2, t0:t1, :], pe32[:, 0, t0:t1, :], ph[:, o % 2, t0:t1, :],
                                                ALU.subtract).then_inc(low_done, 1)

                    for t in range(NT):
                        if t == 4 and layer and has(k, o, 0):
                            dve.wait_ge(v_loaded[o % 2], 16 * uses(k, o, 2))
                            at_least(dve, norm_made, 4 * (s - 1))
                            for c, part in enumerate((K["eh"], K["el"])):
                                for i, c0 in enumerate((1, AT + C)):
                                    last = nc.vector.tensor_copy(part[:, o % B, :, c0:c0 + cols], vb[:, o % 2, c, :, i, :])
                            last.then_inc(v_placed, 1)
                        if t in CHUNK_AT[layer]:
                            chunk(*CHUNK_AT[layer][t])
                        if t % 2 == 0 and t:
                            low(t // 2 - 1)
                    low(HALVES - 1)

                steps(dve, step)


def centre(vec, link, L, layer, extra, smax):
    n = IP[layer]
    sc = L["sc"]
    if layer:
        link(vec.tensor_tensor(sc[:], sc[:], extra[:].rearrange("p u h n -> p u (h n)"), ALU.add))
    else:
        for u in range(U):
            last = vec.tensor_tensor(sc[:, u].rearrange("p (h n) -> p h n", n=n), sc[:, u].rearrange("p (h n) -> p h n", n=n),
                                     extra[:, u].to_broadcast([P, H, n]), ALU.add)
        link(last)
    flat = sc[:].rearrange("p u (h n) -> p (u h) n", n=n)
    link(vec.tensor_reduce(smax[:], flat, AX.X, ALU.max))
    return vec.tensor_tensor(flat, flat, smax[:].unsqueeze(2).to_broadcast([P, U * H, n]), ALU.subtract)


def normalise(vec, link, L, layer, spat, ssum):
    n = IP[layer]
    flat = L["sc"][:].rearrange("p u (h n) -> p (u h) n", n=n)
    link(vec.tensor_reduce(ssum[:], flat, AX.X, ALU.add))
    link(vec.reciprocal(ssum[:], ssum[:]))
    if layer:
        s4 = ssum[:].rearrange("p (b h k) -> p b h k", b=B, h=NH)
        link(vec.tensor_tensor(s4, s4, spat[:].unsqueeze(1).unsqueeze(3).to_broadcast([P, B, NH, H]), ALU.mult))
    return vec.tensor_tensor(flat, flat, ssum[:].unsqueeze(2).to_broadcast([P, U * H, n]), ALU.mult)


def close(nc, K, L, layer, banks, out):
    with ExitStack() as st:
        def sbuf(name, shape, dt):
            return st.enter_context(nc.sbuf_tensor(f"{name}_{layer}", shape, dt))

        def sem(name):
            return st.enter_context(nc.semaphore(f"{name}_{layer}"))

        n = IP[layer]
        CH = ((0, P), (P, D))
        RC = token_rows(layer)
        sc, bv = L["sc"], L["bv"]
        pT = tuple(sbuf(f"pT{i}", [b - a, U, P], F32) for i, (a, b) in enumerate(RC))
        rz = sbuf("rz", [P, G, NH, 2], F32)
        text = sbuf("text", [P, U, D], F32)
        both = sbuf("both", [P, U, D], F32)
        oT = (sbuf("oT0", [P, U, P], F32), sbuf("oT1", [D - P, U, P], F32))
        dve_step = sem("dve_step")
        pT_made, pT_out0, o_made, o_out = sem("pT_made"), sem("pT_out0"), sem("o_made"), sem("o_out")
        pT_out1 = sem("pT_out1") if len(RC) > 1 else None
        oT_made, oT_out0, oT_out1 = sem("oT_made"), sem("oT_out0"), sem("oT_out1")
        y_made, y_out = sem("y_made"), sem("y_out")
        if layer:
            stored, root_done = sem("stored"), sem("root_done")
            centred, exp_done, prob_done = sem("centred"), sem("exp_done"), sem("prob_done")
            extra = sbuf("extra", [P, U, H, n], F32)
            smax, ssum = sbuf("smax", [P, U * H], F32), sbuf("ssum", [P, U * H], F32)
            norm = sbuf("norm", [P, G, NH, 2], F32)
            root = sbuf("root", [P, G, 4], F32)
            ipn = sbuf("ipn", [P, B, n], F32)

        with nc.Block() as block:
            if layer:
                @block.sync
                def _(sp):
                    for u in range(U):
                        sp.wait_ge(y_out, u + 1)
                        b, h = u // NH, u % NH
                        sp.dma_start(out[b, h * P:(h + 1) * P, :], K["xq"][:, u, :]).then_inc(stored, 16)
                    sp.wait_ge(stored, 16 * U)

            @block.tensor
            def _(pe):
                if layer:
                    pe.wait_ge(prob_done, 1)
                for u in range(U):
                    for i, (r0, r1) in enumerate(RC):
                        last = pe.transpose(banks[u][0:r1 - r0, i * P:(i + 1) * P], sc[:, u, r0:r1], K["ident"][:])
                    last.then_inc(pT_made, 1)
                for u in range(U):
                    pe.wait_ge(pT_out0, u + 1)
                    if len(RC) > 1:
                        pe.wait_ge(pT_out1, u + 1)
                    for i in range(len(RC)):
                        last = pe.matmul(banks[u][:, 0:D], pT[i][:, u, :], bv[i][:, u // NH, :], start=(i == 0), stop=(i == len(RC) - 1))
                    last.then_inc(o_made, 1)
                for u in range(U):
                    pe.wait_ge(o_out, u + 1)
                    for i, (a, b) in enumerate(CH):
                        last = pe.transpose(banks[u][0:b - a, i * P:(i + 1) * P], both[:, u, a:b], K["ident"][:])
                    last.then_inc(oT_made, 1)
                for u in range(U):
                    pe.wait_ge(oT_out0, u + 1)
                    pe.wait_ge(oT_out1, u + 1)
                    for i in range(2):
                        last = pe.matmul(banks[u][:, 0:D], oT[i][:, u, :], L["wo"][i][:], start=(i == 0), stop=(i == 1))
                    last.then_inc(y_made, 1)

            @block.scalar
            def _(act):
                if layer:
                    nc.scalar.activation(root[:], K["n2"][:], ACT.Sqrt).then_inc(root_done, 1)
                    nc.scalar.activation(ipn[:], L["token_sq"][:], ACT.Sqrt).then_inc(root_done, 1)
                    act.wait_ge(centred, 1)
                    nc.scalar.activation(sc[:], sc[:], ACT.Exp).then_inc(exp_done, 1)
                for u in range(U):
                    act.wait_ge(pT_made, u + 1)
                    nc.scalar.copy(pT[0][:, u, :], banks[u][0:RC[0][1], 0:P]).then_inc(pT_out0, 1)
                    if len(RC) > 1:
                        nc.scalar.copy(pT[1][:, u, :], banks[u][0:RC[1][1] - P, P:2 * P]).then_inc(pT_out1, 1)
                for u in range(U):
                    act.wait_ge(oT_made, u + 1)
                    nc.scalar.copy(oT[0][:, u, :], banks[u][:, 0:P]).then_inc(oT_out0, 1)
                    nc.scalar.copy(oT[1][:, u, :], banks[u][0:D - P, P:2 * P]).then_inc(oT_out1, 1)

            @block.vector
            def _(dve):
                done = [0]

                def link(ins):
                    done[0] += 1
                    ins.then_inc(dve_step, 1)
                    dve.wait_ge(dve_step, done[0])

                vec = nc.vector
                res = result_of(K, layer)
                sums = res.rearrange("p g h i v -> p (g h) i v")[:, :, :, DH]
                if layer:
                    dve.wait_ge(root_done, 2)
                    link(vec.tensor_scalar(ipn[:], ipn[:], EPS, None, ALU.max))
                    link(vec.reciprocal(ipn[:], ipn[:]))
                    for b in range(B):
                        last = vec.tensor_scalar(ipn[:, b], ipn[:, b], K["inv"][:, 2, b:b + 1], SEM_SCALE, ALU.mult, ALU.mult)
                    link(last)
                    for b in range(B):
                        for h in range(NH):
                            g = slice(b, G, B)
                            last = vec.tensor_scalar(norm[:, g, h, :], root[:, g, h:4:NH], K["inv"][:, 0, b:b + 1], None, ALU.mult)
                    link(last)
                    link(vec.scalar_tensor_tensor(out=norm[:].rearrange("p g h i -> p (g h) i"), in0=sums, scalar=EPS,
                                                  in1=norm[:].rearrange("p g h i -> p (g h) i"), op0=ALU.mult, op1=ALU.max))
                    link(vec.reciprocal(norm[:], norm[:]))
                    for u in range(U):
                        b, h = u // NH, u % NH
                        g = slice(b, G, B)
                        dots = res[:, g, h, :, DH + 1:VW[1]]
                        last = vec.tensor_tensor(extra[:, u].rearrange("p (g i) n -> p g i n", i=2), dots,
                                                 norm[:, g, h, :].unsqueeze(3).to_broadcast([P, PAIRS, 2, n]), ALU.mult)
                    link(last)
                    for b in range(B):
                        e = extra[:, NH * b:NH * (b + 1)].rearrange("p u h n -> p (u h) n")
                        last = vec.tensor_tensor(e, e, ipn[:, b].unsqueeze(1).to_broadcast([P, NH * H, n]), ALU.mult)
                    link(last)
                    centre(vec, link, L, 1, extra, smax).then_inc(centred, 1)
                    dve.wait_ge(exp_done, 1)
                    normalise(vec, link, L, 1, L["spat"], ssum).then_inc(prob_done, 1)
                link(vec.reciprocal(rz[:].rearrange("p g h i -> p (g h) i"), sums))
                if layer:
                    for b in range(B):
                        last = vec.tensor_scalar(rz[:, b:G:B], rz[:, b:G:B], K["inv"][:, 1, b:b + 1], None, ALU.mult)
                    link(last)
                for u in range(U):
                    b, h = u // NH, u % NH
                    g = slice(b, G, B)
                    last = vec.tensor_tensor(text[:, u].rearrange("p (g i d) -> p g i d", i=2, d=DH), res[:, g, h, :, 0:DH],
                                             rz[:, g, h, :].unsqueeze(3).to_broadcast([P, PAIRS, 2, DH]), ALU.mult)
                link(last)
                for u in range(U):
                    dve.wait_ge(o_made, u + 1)
                    vec.tensor_tensor(both[:, u, :], banks[u][:, 0:D], text[:, u, :], ALU.add).then_inc(o_out, 1)
                for u in range(U):
                    dve.wait_ge(y_made, u + 1)
                    vec.tensor_tensor(K["xq"][:, u, :], banks[u][:, 0:D], L["base"][:, u, :], ALU.add).then_inc(y_out, 1)


def kernel(**inputs):
    from concourse import bacc
    from concourse.bass_utils import run_bass_kernel_spmd

    nc = bacc.Bacc("TRN2", target_bir_lowering=False, num_devices=1)
    f = np.float32
    arrays, aps = {}, {}

    def give(name, a):
        a = np.ascontiguousarray(a)
        arrays[f"in_{name}"] = a
        aps[name] = nc.dram_tensor(f"in_{name}", a.shape, mybir.dt.from_np(a.dtype), kind="ExternalInput").ap()

    for name, a in inputs.items():
        give(name, a)
    fold = np.zeros((P, 2 * VW[0]), f)
    for i in range(2):
        for odd in range(2):
            for v in range(VW[0]):
                fold[32 * (2 * i + odd) + v, i * VW[0] + v] = 1
    side = 16
    at = np.arange(S)
    gx, gy = (at % side).astype(f) / f(side - 1), (at // side).astype(f) / f(side - 1)
    grid = np.stack([gx[0:P], gy[0:P], gy[P:S]], axis=1)
    give("c_ident", np.eye(P, dtype=f))
    give("c_ones", np.ones((P, P), f))
    give("c_fold", fold)
    give("c_grid", grid)
    for l in range(2):
        row, col = np.arange(D)[:, None] // DH, np.arange(H * IP[l])[None] // IP[l]
        give(f"c_mask_k{l}", (row == col).astype(f))
        give(f"c_mask_v{l}", (row == col).astype(f).T)
    out = nc.dram_tensor("out_0", (B, S, D), F32, kind="ExternalOutput").ap()
    consts = {k[2:]: v for k, v in aps.items() if k.startswith("c_")}
    a = lambda names: [aps[names[0]], aps[names[1]]]
    w = dict(
        wq=a(("L0_xattn_w_q", "L1_xattn_W_q")), wk=a(("L0_xattn_w_k", "L1_xattn_W_k")),
        wv=a(("L0_xattn_w_v", "L1_xattn_W_v")), wk_ip=a(("L0_xattn_w_k_ip", "L1_xattn_W_k_ip")),
        wv_ip=a(("L0_xattn_w_v_ip", "L1_xattn_W_v_ip")), wo=a(("L0_xattn_w_out", "L1_xattn_W_out")),
        bo=a(("L0_xattn_b_out", "L1_xattn_b_out")),
    )
    build(nc, aps["x"], aps["ctx_2048"], aps["fside_Bx4x4_0"], aps["fside_S_0"], w, consts, out)
    r = run_bass_kernel_spmd(nc, [arrays], core_ids=[0])
    return r.results[0]["out_0"]
```
